# Optimizing a Trainium2 kernel written in Bass

```python
import numpy as np
import jax
import jax.numpy as jnp

def _softmax(x, axis=-1):
    return jax.nn.softmax(x, axis=axis)

def _gelu(x):
    return jax.nn.gelu(x, approximate=True)

def _silu(x):
    return jax.nn.silu(x)

def _sigmoid(x):
    return jax.nn.sigmoid(x)

def _layernorm(x, axis=-1, eps=1e-05):
    m = jnp.mean(x, axis=axis, keepdims=True)
    v = jnp.var(x, axis=axis, keepdims=True)
    return (x - m) / jnp.sqrt(v + eps)

def _scatter_add(tgt, idx, src, axis=0):
    return tgt.at[idx].add(src)

def _segment_sum(src, seg, n):
    return jax.ops.segment_sum(src, seg, n)
kernel_name = 'mk_gnn_ffn_d2_gnn_r8_7b97f5'

def setup_inputs(seed: int=0):
    np.random.seed(seed)
    _w = jnp.asarray

    def _rec_inputs():
        import jax
        import jax.numpy as jnp
        _gk = jax.random.key(seed)
        x = -6.415e-05 + 1 * jax.random.normal(jax.random.fold_in(_gk, 1), (1250, 512), jnp.float32)
        _s = jax.random.randint(jax.random.fold_in(_gk, 2), (20000,), 0, 1250, jnp.int32)
        _d = jax.random.randint(jax.random.fold_in(_gk, 3), (20000,), 0, 1250, jnp.int32)
        _loop = jnp.arange(1250, dtype=jnp.int32)
        src = jnp.concatenate([_s, _d, _loop])
        dst = jnp.concatenate([_d, _s, _loop])
        _o = jnp.argsort(dst, stable=True)
        src = src[_o]
        dst = dst[_o]
        edge_type_32 = jax.random.randint(jax.random.fold_in(_gk, 13), (41250,), 0, 32, jnp.int32)
        edge_weight1 = jax.random.uniform(jax.random.fold_in(_gk, 14), (41250, 1), jnp.float32, 0.0, 0.999996)
        return (x, src, dst, edge_type_32, edge_weight1)
    x, src, dst, edge_type_32, edge_weight1 = _rec_inputs()

    def _L0_gnn_setup():
        import jax, jax.numpy as jnp
        import numpy as np
        N_NODES = 2500
        N_EDGES = 40000
        IN_FEAT = 512
        OUT_FEAT = 512
        NUM_RELS = 32
        NUM_BASES = 8
        key = jax.random.key(seed)
        ks = jax.random.split(key, 8)
        x = jax.random.normal(ks[0], (N_NODES, IN_FEAT), dtype=jnp.float32)
        bases = jax.random.normal(ks[1], (NUM_BASES, IN_FEAT, OUT_FEAT), dtype=jnp.float32) * (1.0 / np.sqrt(IN_FEAT))
        w_comp = jax.random.normal(ks[2], (NUM_RELS, NUM_BASES), dtype=jnp.float32) * (1.0 / np.sqrt(NUM_BASES))
        h_bias = jnp.zeros((OUT_FEAT,), dtype=jnp.float32)
        norm = jax.random.uniform(ks[3], (N_EDGES, 1), dtype=jnp.float32)
        src = jax.random.randint(ks[4], (N_EDGES,), 0, N_NODES, dtype=jnp.int32)
        dst = jax.random.randint(ks[5], (N_EDGES,), 0, N_NODES, dtype=jnp.int32)
        etype = jnp.sort(jax.random.randint(ks[6], (N_EDGES,), 0, NUM_RELS, dtype=jnp.int32))
        return {'x': x, 'bases': bases, 'w_comp': w_comp, 'h_bias': h_bias, 'norm': norm, 'src': src, 'dst': dst, 'etype': etype}
    _L0_gnn_all = _L0_gnn_setup()
    _L0_gnn_in = {k: v for k, v in _L0_gnn_all.items() if k in ('bases', 'w_comp', 'h_bias')}
    del _L0_gnn_all

    def _L0_ffn_setup():
        import jax, jax.numpy as jnp
        import numpy as np
        MIN_EXPERT_CAPACITY = 4
        EPS = 1e-09
        CAPACITY_FACTOR = 2.0

        def cumsum_exclusive(t, axis):
            return jnp.cumsum(t, axis=axis) - t

        def safe_one_hot(idx, depth):
            return jax.nn.one_hot(idx, depth + 1)[..., :depth]

        def top2_gating(x, w_gating):
            b, n, d = x.shape
            e = w_gating.shape[-1]
            raw_gates = jax.nn.softmax(jnp.einsum('bnd,de->bne', x, w_gating), axis=-1)
            gate_1 = jnp.max(raw_gates, axis=-1)
            index_1 = jnp.argmax(raw_gates, axis=-1)
            mask_1 = jax.nn.one_hot(index_1, e, dtype=raw_gates.dtype)
            gates_without_top1 = raw_gates * (1.0 - mask_1)
            gate_2 = jnp.max(gates_without_top1, axis=-1)
            index_2 = jnp.argmax(gates_without_top1, axis=-1)
            mask_2 = jax.nn.one_hot(index_2, e, dtype=raw_gates.dtype)
            denom = gate_1 + gate_2 + EPS
            gate_1 = gate_1 / denom
            gate_2 = gate_2 / denom
            density_1 = jnp.mean(mask_1, axis=-2)
            density_1_proxy = jnp.mean(raw_gates, axis=-2)
            loss = jnp.mean(density_1_proxy * density_1) * float(e * e)
            capacity = max(min(n, int(n * 2 * CAPACITY_FACTOR / e)), MIN_EXPERT_CAPACITY)
            cap_f = float(capacity)
            pos1 = cumsum_exclusive(mask_1, axis=-2) * mask_1
            mask_1 = mask_1 * (pos1 < cap_f).astype(mask_1.dtype)
            mask_1_count = jnp.sum(mask_1, axis=-2, keepdims=True)
            mask_1_flat = jnp.sum(mask_1, axis=-1)
            pos1 = jnp.sum(pos1, axis=-1)
            gate_1 = gate_1 * mask_1_flat
            pos2 = (cumsum_exclusive(mask_2, axis=-2) + mask_1_count) * mask_2
            mask_2 = mask_2 * (pos2 < cap_f).astype(mask_2.dtype)
            mask_2_flat = jnp.sum(mask_2, axis=-1)
            pos2 = jnp.sum(pos2, axis=-1)
            gate_2 = gate_2 * mask_2_flat
            combine = gate_1[..., None, None] * mask_1_flat[..., None, None] * jax.nn.one_hot(index_1, e, dtype=x.dtype)[..., None] * safe_one_hot(pos1.astype(jnp.int32), capacity)[..., None, :] + gate_2[..., None, None] * mask_2_flat[..., None, None] * jax.nn.one_hot(index_2, e, dtype=x.dtype)[..., None] * safe_one_hot(pos2.astype(jnp.int32), capacity)[..., None, :]
            dispatch = (combine > 0).astype(combine.dtype)
            return (dispatch, combine, loss)
        key = jax.random.key(seed)
        k_x, k_g, k_w1, k_w2 = jax.random.split(key, 4)
        b, n, d, e, h = (2, 512, 512, 16, 256)
        x = jax.random.normal(k_x, (b, n, d), dtype=jnp.float32)
        w_gating = jax.random.normal(k_g, (d, e), dtype=jnp.float32) / np.sqrt(d)
        w1 = jax.random.normal(k_w1, (e, d, h), dtype=jnp.float32) / np.sqrt(d)
        w2 = jax.random.normal(k_w2, (e, h, d), dtype=jnp.float32) / np.sqrt(h)
        return {'x': x, 'w_gating': w_gating, 'w1': w1, 'w2': w2}
    _L0_ffn_all = _L0_ffn_setup()
    _L0_ffn_in = {k: v for k, v in _L0_ffn_all.items() if k in ('w_gating', 'w1', 'w2')}
    del _L0_ffn_all

    def _L1_gnn_setup():
        import jax, jax.numpy as jnp
        import numpy as np
        N = 6250
        IN_CH = 512
        OUT_CH = 512
        DEG = 32
        E = N * DEG
        key = jax.random.key(seed)
        kx, kwc, kwn, kb, ke = jax.random.split(key, 5)
        x = jax.random.normal(kx, (N, IN_CH), dtype=jnp.float32)
        bound = 1.0 / np.sqrt(IN_CH)
        wc = jax.random.uniform(kwc, (IN_CH, OUT_CH), minval=-bound, maxval=bound, dtype=jnp.float32)
        wn = jax.random.uniform(kwn, (IN_CH, OUT_CH), minval=-bound, maxval=bound, dtype=jnp.float32)
        bias = jax.random.uniform(kb, (OUT_CH,), minval=-bound, maxval=bound, dtype=jnp.float32)
        src = jnp.repeat(jnp.arange(N, dtype=jnp.int64), DEG)
        dst = jax.random.randint(ke, (E,), 0, N, dtype=jnp.int64)
        edge_index = jnp.stack([src, dst], axis=0)
        return {'x': x, 'wc': wc, 'wn': wn, 'bias': bias, 'edge_index': edge_index}
    _L1_gnn_all = _L1_gnn_setup()
    _L1_gnn_in = {k: v for k, v in _L1_gnn_all.items() if k in ('wc', 'wn', 'bias')}
    del _L1_gnn_all

    def _L1_ffn_setup():
        import jax, jax.numpy as jnp
        import numpy as np
        NUM_EXPERTS = 8
        TOP_K = 2
        key = jax.random.key(seed)
        k0, k1, k2, k3, k4 = jax.random.split(key, 5)
        sl, bs, hs, ffn = (256, 2, 512, 256)
        T = sl * bs
        x = jax.random.normal(k0, (sl, bs, hs), jnp.float32)
        expert_weights = jax.random.uniform(k1, (T, TOP_K), jnp.float32)
        expert_indices = jax.random.randint(k2, (T, TOP_K), 0, NUM_EXPERTS)
        w1 = jax.random.normal(k3, (NUM_EXPERTS, hs, ffn), jnp.float32) * hs ** (-0.5)
        w2 = jax.random.normal(k4, (NUM_EXPERTS, ffn, hs), jnp.float32) * ffn ** (-0.5)
        return dict(x=x, expert_weights=expert_weights, expert_indices=expert_indices, w1=w1, w2=w2)
    _L1_ffn_all = _L1_ffn_setup()
    _L1_ffn_in = {k: v for k, v in _L1_ffn_all.items() if k in ('expert_weights', 'expert_indices', 'w1', 'w2')}
    del _L1_ffn_all
    return {'x': x, 'src': src, 'dst': dst, 'edge_type_32': edge_type_32, 'edge_weight1': edge_weight1, 'L0_gnn_bases': _L0_gnn_in['bases'], 'L0_gnn_w_comp': _L0_gnn_in['w_comp'], 'L0_gnn_h_bias': _L0_gnn_in['h_bias'], 'L0_ffn_w_gating': _L0_ffn_in['w_gating'], 'L0_ffn_w1': _L0_ffn_in['w1'], 'L0_ffn_w2': _L0_ffn_in['w2'], 'L1_gnn_wc': _L1_gnn_in['wc'], 'L1_gnn_wn': _L1_gnn_in['wn'], 'L1_gnn_bias': _L1_gnn_in['bias'], 'L1_ffn_expert_weights': _L1_ffn_in['expert_weights'], 'L1_ffn_expert_indices': _L1_ffn_in['expert_indices'], 'L1_ffn_w1': _L1_ffn_in['w1'], 'L1_ffn_w2': _L1_ffn_in['w2']}

def reference(x, src, dst, edge_type_32, edge_weight1, L0_gnn_bases, L0_gnn_w_comp, L0_gnn_h_bias, L0_ffn_w_gating, L0_ffn_w1, L0_ffn_w2, L1_gnn_wc, L1_gnn_wn, L1_gnn_bias, L1_ffn_expert_weights, L1_ffn_expert_indices, L1_ffn_w1, L1_ffn_w2):
    import jax
    import jax.numpy as jnp

    def _L0_gnn_ref(x, bases, w_comp, h_bias, norm, src, dst, etype):
        import jax, jax.numpy as jnp
        import numpy as np
        N_NODES = 2500
        N_EDGES = 40000
        IN_FEAT = 512
        OUT_FEAT = 512
        NUM_RELS = 32
        NUM_BASES = 8
        n_nodes = x.shape[0]
        weight = jnp.einsum('rb,bio->rio', w_comp, bases)
        h_rel = jnp.einsum('ni,rio->rno', x, weight)
        msg = h_rel[etype, src] * norm
        out = jax.ops.segment_sum(msg, dst, num_segments=n_nodes)
        out = out + h_bias
        return out

    def _L0_ffn_ref(x, w_gating, w1, w2):
        import jax, jax.numpy as jnp
        import numpy as np
        MIN_EXPERT_CAPACITY = 4
        EPS = 1e-09
        CAPACITY_FACTOR = 2.0

        def cumsum_exclusive(t, axis):
            return jnp.cumsum(t, axis=axis) - t

        def safe_one_hot(idx, depth):
            return jax.nn.one_hot(idx, depth + 1)[..., :depth]

        def top2_gating(x, w_gating):
            b, n, d = x.shape
            e = w_gating.shape[-1]
            raw_gates = jax.nn.softmax(jnp.einsum('bnd,de->bne', x, w_gating), axis=-1)
            gate_1 = jnp.max(raw_gates, axis=-1)
            index_1 = jnp.argmax(raw_gates, axis=-1)
            mask_1 = jax.nn.one_hot(index_1, e, dtype=raw_gates.dtype)
            gates_without_top1 = raw_gates * (1.0 - mask_1)
            gate_2 = jnp.max(gates_without_top1, axis=-1)
            index_2 = jnp.argmax(gates_without_top1, axis=-1)
            mask_2 = jax.nn.one_hot(index_2, e, dtype=raw_gates.dtype)
            denom = gate_1 + gate_2 + EPS
            gate_1 = gate_1 / denom
            gate_2 = gate_2 / denom
            density_1 = jnp.mean(mask_1, axis=-2)
            density_1_proxy = jnp.mean(raw_gates, axis=-2)
            loss = jnp.mean(density_1_proxy * density_1) * float(e * e)
            capacity = max(min(n, int(n * 2 * CAPACITY_FACTOR / e)), MIN_EXPERT_CAPACITY)
            cap_f = float(capacity)
            pos1 = cumsum_exclusive(mask_1, axis=-2) * mask_1
            mask_1 = mask_1 * (pos1 < cap_f).astype(mask_1.dtype)
            mask_1_count = jnp.sum(mask_1, axis=-2, keepdims=True)
            mask_1_flat = jnp.sum(mask_1, axis=-1)
            pos1 = jnp.sum(pos1, axis=-1)
            gate_1 = gate_1 * mask_1_flat
            pos2 = (cumsum_exclusive(mask_2, axis=-2) + mask_1_count) * mask_2
            mask_2 = mask_2 * (pos2 < cap_f).astype(mask_2.dtype)
            mask_2_flat = jnp.sum(mask_2, axis=-1)
            pos2 = jnp.sum(pos2, axis=-1)
            gate_2 = gate_2 * mask_2_flat
            combine = gate_1[..., None, None] * mask_1_flat[..., None, None] * jax.nn.one_hot(index_1, e, dtype=x.dtype)[..., None] * safe_one_hot(pos1.astype(jnp.int32), capacity)[..., None, :] + gate_2[..., None, None] * mask_2_flat[..., None, None] * jax.nn.one_hot(index_2, e, dtype=x.dtype)[..., None] * safe_one_hot(pos2.astype(jnp.int32), capacity)[..., None, :]
            dispatch = (combine > 0).astype(combine.dtype)
            return (dispatch, combine, loss)
        dispatch, combine, loss = top2_gating(x, w_gating)
        expert_inputs = jnp.einsum('bnd,bnec->ebcd', x, dispatch)
        hidden = jax.nn.relu(jnp.einsum('ebcd,edh->ebch', expert_inputs, w1))
        expert_outputs = jnp.einsum('ebch,ehd->ebcd', hidden, w2)
        output = jnp.einsum('ebcd,bnec->bnd', expert_outputs, combine)
        return output

    def _L1_gnn_ref(x, wc, wn, bias, edge_index):
        import jax, jax.numpy as jnp
        import numpy as np
        N = 6250
        IN_CH = 512
        OUT_CH = 512
        DEG = 32
        E = N * DEG
        alpha = x @ wc
        beta = x @ wn
        src, dst = (edge_index[0], edge_index[1])
        sums = jax.ops.segment_sum(beta[dst], src, num_segments=x.shape[0])
        counts = jax.ops.segment_sum(jnp.ones_like(src, dtype=beta.dtype), src, num_segments=x.shape[0])
        gamma = sums / counts[:, None]
        return alpha + gamma + bias

    def _L1_ffn_ref(x, expert_weights, expert_indices, w1, w2):
        import jax, jax.numpy as jnp
        import numpy as np
        NUM_EXPERTS = 8
        TOP_K = 2
        'Dropless MoE: sort assignments by expert, gather tokens, grouped MLP,\n            scatter-combine with top-k router weights (megablocks gather/scatter semantics).'
        in_shape = x.shape
        hs = in_shape[-1]
        x_flat = x.reshape(-1, hs)
        T = x_flat.shape[0]
        flat_ids = expert_indices.reshape(-1)
        order = jnp.argsort(flat_ids)
        bin_ids = flat_ids[order]
        token_ids = order // TOP_K
        xg = x_flat[token_ids]
        y = jnp.zeros_like(xg)
        for e in range(NUM_EXPERTS):
            h = jax.nn.gelu(xg @ w1[e], approximate=False)
            y = jnp.where((bin_ids == e)[:, None], h @ w2[e], y)
        w = expert_weights.reshape(-1)[order][:, None]
        out = jnp.zeros((T, hs), x.dtype).at[token_ids].add(w * y)
        return out.reshape(in_shape)
    edge_index = jnp.stack([src, dst])
    x = x + _L0_gnn_ref(_layernorm(x, axis=-1), L0_gnn_bases, L0_gnn_w_comp, L0_gnn_h_bias, edge_weight1, src, dst, edge_type_32)
    x = x + _L0_ffn_ref(_layernorm(x, axis=-1)[None], L0_ffn_w_gating, L0_ffn_w1, L0_ffn_w2)[0]
    x = x + _L1_gnn_ref(_layernorm(x, axis=-1), L1_gnn_wc, L1_gnn_wn, L1_gnn_bias, edge_index)
    x = x + _L1_ffn_ref(_layernorm(x, axis=-1)[None], L1_ffn_expert_weights, L1_ffn_expert_indices, L1_ffn_w1, L1_ffn_w2)[0]
    return x

_drawn_inputs = setup_inputs


def setup_inputs(seed=0):
    import zlib

    import numpy as np

    out = dict(_drawn_inputs(seed))
    spreads = {'L0_gnn_h_bias': (0.0, 0.1)}
    factors = {'L1_gnn_bias': 8.0}
    for name, (base, spread) in spreads.items():
        noise = np.random.default_rng([zlib.crc32(name.encode()), seed]).standard_normal(out[name].shape)
        drawn = base * np.exp(spread * noise) if base else spread * noise
        out[name] = jnp.asarray(drawn.astype(out[name].dtype))
    for name, factor in factors.items():
        out[name] = (out[name] * factor).astype(out[name].dtype)
    return out
```

```python
import concourse.bass as bass
from concourse import mybir
from contextlib import ExitStack

P = 128
N = 1250
F = 512
NF = F // P
NT = -(-N // P)
NP = NT * P
LAST = N - (NT - 1) * P
E = 41250
BCH = 6
NB = -(-E // (P * BCH))
NCH = NB * BCH
TCOL = NCH + BCH
WIN = 8
W = N + 2 * WIN - N % WIN - (WIN - N % WIN) % WIN
W = -(-N // WIN) * WIN + WIN
ROWS = 108
RT = NCH // ROWS
NREL, NBASE = 32, 8
QCH = NCH // 4
EX0, CAP, H0 = 16, 312, 256
SLOTS = EX0 * CAP
SC = SLOTS // P
ST = CAP // 3
T1, EX1, TOPK, H1 = 512, 8, 2, 256
TT1 = T1 // P
EPS = 1e-5
NOSLOT = 8192.0
UH = NT

f32 = mybir.dt.float32
bf16 = mybir.dt.bfloat16
i32 = mybir.dt.int32
ALU = mybir.AluOpType
ACT = mybir.ActivationFunctionType
AX = mybir.AxisListType
ds = bass.ds


def rows(t):
    return P if t < NT - 1 else LAST


def build(nc, x, src_cols, dst_cols, wgt_cols, etype, dst_rows, bases, w_comp, h_bias, w_gating, f0_w1, f0_w2,
          wc, wn, g1_bias, x_weights, x_indices, f1_w1, f1_w2, out):
    xh1_d = nc.dram_tensor("xh1_d", (N, F), f32).ap()
    x1_d = nc.dram_tensor("x1_d", (N, F), f32).ap()
    xh2_d = nc.dram_tensor("xh2_d", (N, F), f32).ap()
    slot_d = nc.dram_tensor("slot_d", (SLOTS, 1), i32).ap()
    ye_d = nc.dram_tensor("ye_d", (SLOTS, F), f32).ap()

    with ExitStack() as ctx:
        def sb(name, shape, dt=f32):
            return ctx.enter_context(nc.sbuf_tensor(name, shape, dt))

        def sem(name):
            return ctx.enter_context(nc.semaphore(name))

        big = sb("big", [P, 32 * W])
        mid = sb("mid", [P, 3072 + TCOL * NBASE])
        agg = big[:, :].rearrange("p (f b w) -> p f b w", f=NF, b=NBASE)
        aggw = big[:, :].rearrange("p (fb w) -> p fb w", w=W)
        xin = big[:, 0:NT * F].rearrange("p (t f) -> p t f", f=F)
        xh = big[:, NT * F:2 * NT * F].rearrange("p (t f) -> p t f", f=F)
        o = 2 * NT * F
        etb = big[:, o:o + QCH * P].bitcast(i32)
        o += QCH * P
        onet = big[:, o:o + QCH * P // 2].bitcast(bf16)
        o += QCH * P // 2
        dstr_i = big[:, o:o + RT * P].bitcast(i32).rearrange("p (t e) -> p t e", e=P)
        dstr = big[:, o + RT * P:o + 2 * RT * P].rearrange("p (t e) -> p t e", e=P)
        dstm = big[:, o + 2 * RT * P:o + 3 * RT * P].rearrange("p (t e) -> p t e", e=P)
        SETUP = o + 3 * RT * P
        xg = mid[:, 0:BCH * F].rearrange("p (j f) -> p j f", f=F)
        coef = mid[:, BCH * F:BCH * F + TCOL * NBASE].rearrange("p (c b) -> p c b", b=NBASE)
        cb = sb("cb", [P, 2, BCH, NBASE, WIN])
        oh = sb("oh", [P, 2, BCH, WIN])
        rel = sb("rel", [P, TCOL])
        basef = sb("basef", [P, TCOL])
        base0 = sb("base0", [P, TCOL])
        basec = sb("basec", [1, TCOL])
        basei = sb("basei", [1, TCOL], i32)
        src_i = sb("src_i", [P, TCOL], i32)
        dst_i = sb("dst_i", [P, TCOL], i32)
        dstf = sb("dstf", [P, TCOL])
        wgt = sb("wgt", [P, TCOL])
        idx = sb("idx", [P, 2, BCH], i32)
        rounds_i = sb("rounds_i", [1, 4], i32)
        mins = sb("mins", [ROWS, 3, RT])
        minb = big[0:ROWS, SETUP:SETUP + (RT + 1) * P].rearrange("p (t e) -> p t e", e=P)
        SETUP += (RT + 1) * P
        gap = sb("gap", [P, 1])
        gap_i = sb("gap_i", [P, 1], i32)
        iota_i = sb("iota_i", [P, P], i32)
        part_i = sb("part_i", [P, 3], i32)
        iota = sb("iota", [P, P])
        part = sb("part", [P, 3])
        ident = sb("ident", [P, P])
        identr = sb("tri", [P, P], bf16)
        tri = identr
        ones = sb("ones", [P, P], bf16)
        wc4 = sb("wc4", [P, NBASE])
        wpart = sb("wpart", [P, 3, NBASE], bf16)
        qmask = sb("qmask", [P, 4])
        wbd = sb("wbd", [P, 3, 4, NBASE], bf16)
        hb = sb("hb", [P, F])
        eps = sb("eps", [P, 1])
        stats = sb("stats", [P, NT, 6])
        mv = sb("mv", [P, NT, 2])
        std = sb("std", [P, NT])
        rstd = sb("rstd", [P, NT])
        bring = mid[:, 0:2 * NF * F].rearrange("p (s k f) -> p s k f", s=2, k=NF)
        xt = mid[:, 4096:4096 + 512]
        xo = mid[:, 4096 + 512:4096 + 1024]
        xn = mid[:, 4096 + 1024:4096 + 1536]
        x1 = big[:, 0:NT * F].rearrange("p (t f) -> p t f", f=F)
        xh2 = big[:, 5120:10240].rearrange("p (t f) -> p t f", f=F)
        xT = big[:, 10240:15360].rearrange("p (k n) -> p k n", n=NP)
        xe = big[:, 15360:15360 + NF * SLOTS].rearrange("p (k s) -> p k s", s=SLOTS)
        xer = big[:, 35328:35328 + 6 * F].rearrange("p (j f) -> p j f", f=F)
        wring = mid[:, 0:4096].rearrange("p (s n) -> p s n", s=2)
        w1r = [wring[:, s, 0:1024].rearrange("p (k h) -> p k h", k=NF) for s in range(2)]
        w2r = [wring[:, s, 1024:2048].rearrange("p (k f) -> p k f", k=2) for s in range(2)]
        wg = mid[:, 4096:4096 + NF * EX0].rearrange("p (k e) -> p k e", e=EX0)
        hT = xh2.rearrange("p t f -> p (t f)")[:, 0:2 * 2 * CAP].rearrange("p (s k c) -> p s k c", s=2, k=2)
        ysb = xh2.rearrange("p t f -> p (t f)")[:, 1280:1280 + 2 * 3 * F].rearrange("p (s k c) -> p s k c", s=2, k=3)
        g_ = big[:, 38400:38400 + 12 * NT * EX0].rearrange("p (k t e) -> p k t e", k=12, t=NT)
        s_ = sb("small", [P, 16, NT])
        mb = sb("mb", [P, NT, EX0], bf16)
        pref = sb("pref", [P, NT, EX0])
        slot_i = sb("slot_i", [P, 4, NT], i32)
        tok_i = sb("tok_i", [P, NT], i32)
        slots_in = sb("slots_in", [P, SC], i32)
        zero_i = sb("zero_i", [P, SC], i32)
        nT = big[:, 5120:5120 + UH * W].rearrange("p (u w) -> p u w", w=W)
        adj = big[:, 17760:17760 + NT * NP].rearrange("p (t u) -> p t u", u=NP)
        xh3 = big[:, 30560:35680].rearrange("p (t f) -> p t f", f=F)
        y2 = big[:, 35680:35680 + 4 * F].rearrange("p (j f) -> p j f", f=F)
        xT3 = big[:, 5120:10240].rearrange("p (k n) -> p k n", n=NP)
        sT = big[:, 10240:15360].rearrange("p (k n) -> p k n", n=NP)
        wcs = mid[:, 0:2048].rearrange("p (k f) -> p k f", k=NF)
        wns = mid[:, 2048:4096].rearrange("p (k f) -> p k f", k=NF)
        ohw = sb("ohw", [P, 2, BCH, WIN])
        ohu = sb("ohu", [P, 2, BCH, UH])
        lside = mid[:, 4160:4160 + BCH * UH * WIN].bitcast(bf16).rearrange("p (h j u w) -> p h j u w", h=2, j=BCH, u=UH)
        rside = mid[:, 4640:4640 + BCH * P].bitcast(bf16).rearrange("p (h j u) -> p h j u", h=2, j=BCH)
        ulo_i = sb("ulo_i", [P, TCOL], i32)
        uhi_i = dst_i
        ulo = wgt
        uhi = sb("uhi", [P, TCOL])
        gbias = big[:, 37728:37728 + F]
        cnt = sb("cnt", [P, UH])
        rcnt = sb("rcnt", [P, UH])
        xh4 = big[:, 30560:30560 + TT1 * F].rearrange("p (t f) -> p t f", f=F)
        xT4 = big[:, 17760:17760 + NF * T1].rearrange("p (k n) -> p k n", n=T1)
        hT1 = big[:, 20000:20000 + 2 * 2 * T1].rearrange("p (s k n) -> p s k n", s=2, k=2)
        ei = sb("ei", [P, TT1, TOPK], i32)
        ef = sb("ef", [P, TT1, TOPK])
        ew = sb("ew", [P, TT1, TOPK])
        comb = sb("comb", [P, TT1, EX1])
        combt = sb("combt", [P, TT1, TOPK, EX1])

        ps = [ctx.enter_context(nc.psum_tensor(f"ps{i}", [P, 512], f32)) for i in range(8)]

        names = """ld_edges ld_rows ld_etype ld_x ld_small pad_ready const_ready xh1_ready xh1_stored dve act
        onet_ready coef_mm coef_done base_mm rounds_ready zeroed table_ready round_ready c_ready mm_done acc_done
        idx_ready dma_zero basis_mm base_ld0 base_ld1 x_ld xo_ready x1_stored sq sqd x1_ld tp tp_done lg
        cum cum_done slots_ready slot_zero slot_set slot_ld xe_tp xe_ev w0_ld0 w0_ld1 up relu down y_ev y_st0 y_st1 ycopy
        y2_used xh3_ready n_c n_mm n_acc n_round tr tr_done sx sx_ev wcn_ld gm g_ev out_st x4_ready tp4 tp4_done
        w1_ld0 w1_ld1 up1 gelu down1 fin ld_moe bias_ld cnt_ready tp3 tp3_done zero_ready n_ready adj_ready""".split()
        S = {n: sem(n) for n in names}
        g = [sem(f"gather{j}") for j in range(BCH)]
        gx = [sem(f"gather_slot{j}") for j in range(6)]
        gy = [sem(f"gather_out{j}") for j in range(4)]
        block = ctx.enter_context(nc.Block())

        def layer_norm(dve, link, src_of, dst_of, tiles, sqrt_no):
            for t in tiles:
                link(nc.vector.bn_stats(stats[0:rows(t), t, :], src_of(t)))
                link(nc.vector.bn_aggr(mv[0:rows(t), t, :], stats[0:rows(t), t, :]))
            nc.vector.engine_nop().then_inc(S["sq"], 1)
            dve.wait_ge(S["sqd"], sqrt_no)
            a, b = tiles[0], tiles[-1] + 1
            link(nc.vector.reciprocal(rstd[:, a:b], std[:, a:b]))
            for t in tiles:
                r = rows(t)
                link(nc.vector.tensor_scalar(dst_of(t), src_of(t), mv[0:r, t, 0:1], rstd[0:r, t:t + 1],
                                             ALU.subtract, ALU.mult))

        ROOTS = [(0, NT)] + [(t, t + 1) for t in range(NT)] + [(0, NT), (0, TT1)]

        @block.sync
        def _(sp):
            sp.dma_start(dstr_i[0:ROWS, :, :], dst_rows.rearrange("(t p) e -> p t e", p=ROWS)).then_inc(S["ld_rows"], 16)
            sp.dma_start(src_i[:], src_cols).then_inc(S["ld_edges"], 16)
            sp.dma_start(dst_i[:], dst_cols).then_inc(S["ld_edges"], 16)
            sp.dma_start(wgt[:], wgt_cols).then_inc(S["ld_edges"], 16)
            sp.dma_start(xin[:, 0:NT - 1, :], x[0:(NT - 1) * P, :].rearrange("(t p) f -> p t f", p=P)).then_inc(S["ld_x"], 16)
            sp.dma_start(xin[0:LAST, NT - 1, :], x[(NT - 1) * P:N, :]).then_inc(S["ld_x"], 16)
            for q in range(4):
                sp.dma_start(etb[32 * q:32 * q + 32, :], etype[q:q + 1, :].to_broadcast([32, QCH * P])).then_inc(S["ld_etype"], 16)
                sp.dma_start(wc4[32 * q:32 * q + 32, :], w_comp).then_inc(S["ld_small"], 16)
            sp.dma_start(hb[:], h_bias.to_broadcast([P, F])).then_inc(S["ld_small"], 16)
            sp.wait_ge(S["xh1_ready"], 1)
            sp.dma_start(xh1_d[0:(NT - 1) * P, :].rearrange("(t p) f -> p t f", p=P), xh[:, 0:NT - 1, :]).then_inc(S["xh1_stored"], 16)
            sp.dma_start(xh1_d[(NT - 1) * P:N, :], xh[0:LAST, NT - 1, :]).then_inc(S["xh1_stored"], 16)
            sp.wait_ge(S["zero_ready"], 1)
            sp.dma_start(slot_d.rearrange("(p c) o -> p (c o)", p=P), zero_i[:]).then_inc(S["slot_zero"], 16)
            for n in range(2 * NBASE):
                if n < 2:
                    sp.wait_ge(S["table_ready"], 3)
                else:
                    sp.wait_ge(S["basis_mm"], n - 1)
                sp.dma_start(bring[:, n % 2], bases[n % NBASE].rearrange("(k p) f -> p k f", p=P)).then_inc(S[f"base_ld{n % 2}"], 16)
                if n == 1:
                    sp.dma_start(xt[:, :], x[0:P, :]).then_inc(S["x_ld"], 16)
            sp.wait_ge(S["x1_stored"], 32 * NT)
            sp.wait_ge(S["zeroed"], 7)
            for d, s in ((xh2, xh2_d), (x1, x1_d)):
                sp.dma_start(d[:, 0:NT - 1, :], s[0:(NT - 1) * P, :].rearrange("(t p) f -> p t f", p=P)).then_inc(S["x1_ld"], 16)
                sp.dma_start(d[0:LAST, NT - 1, :], s[(NT - 1) * P:N, :]).then_inc(S["x1_ld"], 16)
            sp.dma_start(wg[:, :, :], w_gating.rearrange("(k p) e -> p k e", p=P)).then_inc(S["x1_ld"], 16)
            for e in range(2):
                sp.dma_start(w1r[e], f0_w1[e].rearrange("(k p) h -> p k h", p=P)).then_inc(S[f"w0_ld{e}"], 16)
                sp.dma_start(w2r[e], f0_w2[e].rearrange("(k p) f -> p k f", p=P)).then_inc(S[f"w0_ld{e}"], 16)
            sp.wait_ge(S["slot_set"], 16 * 2 * NT)
            sp.dma_start(slots_in[:], slot_d.rearrange("(p c) o -> p (c o)", p=P)).then_inc(S["slot_ld"], 16)
            for e in range(EX0):
                sp.wait_ge(S["y_ev"], 3 * e + 3)
                sp.dma_start(ye_d[e * CAP:(e + 1) * CAP, :].rearrange("(s p) f -> p s f", p=ST), ysb[0:ST, e % 2]).then_inc(S[f"y_st{e % 2}"], 16)
                if e + 2 < EX0:
                    sp.wait_ge(S["down"], 3 * e + 3)
                    sp.dma_start(w1r[e % 2], f0_w1[e + 2].rearrange("(k p) h -> p k h", p=P)).then_inc(S[f"w0_ld{e % 2}"], 16)
                    sp.dma_start(w2r[e % 2], f0_w2[e + 2].rearrange("(k p) f -> p k f", p=P)).then_inc(S[f"w0_ld{e % 2}"], 16)
            sp.wait_ge(S["down"], 3 * EX0)
            sp.dma_start(wcs[:, :, :], wc.rearrange("(k p) f -> p k f", p=P)).then_inc(S["wcn_ld"], 16)
            sp.dma_start(wns[:, :, :], wn.rearrange("(k p) f -> p k f", p=P)).then_inc(S["wcn_ld"], 16)
            sp.dma_start(gbias[:], g1_bias.to_broadcast([P, F])).then_inc(S["bias_ld"], 16)
            sp.dma_start(ei[:], x_indices.rearrange("(t p) k -> p t k", p=P)).then_inc(S["ld_moe"], 16)
            sp.dma_start(ew[:], x_weights.rearrange("(t p) k -> p t k", p=P)).then_inc(S["ld_moe"], 16)
            sp.wait_ge(S["g_ev"], NT)
            sp.dma_start(out[T1:(NT - 1) * P, :].rearrange("(t p) f -> p t f", p=P), x1[:, TT1:NT - 1, :]).then_inc(S["out_st"], 16)
            sp.dma_start(out[(NT - 1) * P:N, :], x1[0:LAST, NT - 1, :]).then_inc(S["out_st"], 16)
            for e in range(EX1):
                if e >= 2:
                    sp.wait_ge(S["down1"], e - 1)
                else:
                    sp.wait_ge(S["gm"], NT)
                sp.dma_start(w1r[e % 2], f1_w1[e].rearrange("(k p) h -> p k h", p=P)).then_inc(S[f"w1_ld{e % 2}"], 16)
                sp.dma_start(w2r[e % 2], f1_w2[e].rearrange("(k p) f -> p k f", p=P)).then_inc(S[f"w1_ld{e % 2}"], 16)
            sp.wait_ge(S["fin"], 1)
            sp.dma_start(out[0:T1, :].rearrange("(t p) f -> p t f", p=P), x1[:, 0:TT1, :]).then_inc(S["out_st"], 16)
            sp.wait_ge(S["out_st"], 48)

        @block.gpsimd
        def _(pool):
            nc.gpsimd.iota(iota_i[:], pattern=[[1, P]], base=0, channel_multiplier=0).then_inc(S["const_ready"], 1)
            nc.gpsimd.iota(part_i[:, 0:1], pattern=[[1, 1]], base=0, channel_multiplier=1).then_inc(S["const_ready"], 1)
            nc.gpsimd.iota(tok_i[:], pattern=[[P, NT]], base=0, channel_multiplier=1).then_inc(S["const_ready"], 1)
            nc.gpsimd.memset(zero_i[:], 0).then_inc(S["zero_ready"], 1)
            nc.gpsimd.memset(big[:, SETUP:32 * W], 0.0).then_inc(S["zeroed"], 1)
            pool.wait_ge(S["xh1_stored"], 32)
            pool.wait_ge(S["rounds_ready"], 1)
            rounds = pool.value_load(rounds_i[0:1, 0:1], min_val=1, max_val=W // WIN)
            with pool.Fori(0, rounds) as r:
                with pool.Fori(0, NB // 2) as i:
                    for h in range(2):
                        n = r * NB + i * 2 + h
                        pool.wait_ge(S["idx_ready"], n + 1)
                        for j in range(BCH):
                            pool.wait_ge(S["mm_done"], n * BCH + j + 1)
                            pool.nop(nofuse=True)
                            pool.indirect_dma_start(xg[:, j, :], None, xh1_d, bass.IndirectOffsetOnAxis(idx[:, h, j:j + 1], 0)).then_inc(g[j], 16)
            pool.wait_ge(S["slot_zero"], 16)
            pool.wait_ge(S["slots_ready"], 1)
            for t in range(NT):
                for k in range(2):
                    pool.indirect_dma_start(slot_d, bass.IndirectOffsetOnAxis(slot_i[:, k, t:t + 1], 0), tok_i[:, t:t + 1], None,
                                            bounds_check=SLOTS - 1, oob_is_err=False).then_inc(S["slot_set"], 16)
            pool.wait_ge(S["slot_ld"], 16)
            for c in range(SC):
                if c >= 6:
                    pool.wait_ge(S["xe_tp"], c - 5)
                pool.indirect_dma_start(xer[:, c % 6, :], None, xh2_d, bass.IndirectOffsetOnAxis(slots_in[:, c:c + 1], 0)).then_inc(gx[c % 6], 16)
            pool.wait_ge(S["y_st0"], 16 * EX0 // 2)
            pool.wait_ge(S["y_st1"], 16 * EX0 // 2)
            for n in range(2 * NT):
                if n >= 4:
                    pool.wait_ge(S["y2_used"], n - 3)
                else:
                    pool.wait_ge(S["xe_tp"], SC)
                pool.indirect_dma_start(y2[:, n % 4, :], None, ye_d, bass.IndirectOffsetOnAxis(slot_i[:, 2 + n % 2, n // 2:n // 2 + 1], 0)).then_inc(gy[n % 4], 16)

        @block.scalar
        def _(act):
            roots = [0]

            def root():
                a, b = ROOTS[roots[0]]
                roots[0] += 1
                act.wait_ge(S["sq"], roots[0])
                nc.scalar.activation(std[:, a:b], mv[:, a:b, 1], ACT.Sqrt, bias=eps[:]).then_inc(S["sqd"], 1)

            root()
            act.wait_ge(S["rounds_ready"], 1)
            rounds = act.value_load(rounds_i[0:1, 0:1], min_val=1, max_val=W // WIN)
            with act.Fori(0, rounds) as r:
                with act.Fori(0, NB // 2) as i:
                    for h in range(2):
                        n = r * NB + i * 2 + h
                        act.wait_ge(S["mm_done"], n * BCH + 1)
                        nc.scalar.copy(idx[:, h, :], src_i[:, ds((i * 2 + h) * BCH, BCH)]).then_inc(S["idx_ready"], 1)
            for t in range(NT):
                r = rows(t)
                if t:
                    act.wait_ge(S["xo_ready"], 2 * t - 1)
                    act.dma_start(xt[0:r, :], x[t * P:t * P + r, :]).then_inc(S["x_ld"], 16)
                root()
                act.wait_ge(S["xo_ready"], 2 * t + 2)
                act.dma_start(x1_d[t * P:t * P + r, :], xo[0:r, :]).then_inc(S["x1_stored"], 16)
                act.dma_start(xh2_d[t * P:t * P + r, :], xn[0:r, :]).then_inc(S["x1_stored"], 16)
            for t in range(NT):
                act.wait_ge(S["tp"], t + 1)
                nc.scalar.copy(xT[:, :, t * P:(t + 1) * P], ps[t % 2][:].rearrange("p (k n) -> p k n", k=NF)).then_inc(S["tp_done"], 1)
            act.wait_ge(S["cum"], 1)
            nc.scalar.activation(g_[:, 0], g_[:, 1], ACT.Exp).then_inc(S["act"], 1)
            for c in range(SC):
                act.wait_ge(S["xe_tp"], c + 1)
                nc.scalar.copy(xe[:, :, c:SLOTS:SC], ps[c % 2][:].rearrange("p (k n) -> p k n", k=NF)).then_inc(S["xe_ev"], 1)

            for e in range(EX0):
                act.wait_ge(S["up"], e + 1)
                if e >= 2:
                    act.wait_ge(S["down"], 3 * (e - 1))
                for k in range(2):
                    ins = nc.scalar.activation(hT[:, e % 2, k, :], ps[2 + (e % 2) * 2 + k][:, 0:CAP], ACT.Relu)
                ins.then_inc(S["relu"], 1)
            root()
            for t in range(NT):
                act.wait_ge(S["tp3"], t + 1)
                nc.scalar.copy(xT3[:, :, t * P:(t + 1) * P], ps[t % 2][:].rearrange("p (k n) -> p k n", k=NF)).then_inc(S["tp3_done"], 1)
            root()
            for t in range(TT1):
                act.wait_ge(S["tp4"], t + 1)
                nc.scalar.copy(xT4[:, :, t * P:(t + 1) * P], ps[t % 2][:].rearrange("p (k n) -> p k n", k=NF)).then_inc(S["tp4_done"], 1)
            for e in range(EX1):
                act.wait_ge(S["up1"], e + 1)
                if e >= 2:
                    act.wait_ge(S["down1"], e - 1)
                for k in range(2):
                    ins = nc.scalar.activation(hT1[:, e % 2, k, :], ps[(e % 2) * 2 + k][:], ACT.Gelu)
                ins.then_inc(S["gelu"], 1)

        @block.tensor
        def _(pe):
            pe.wait_ge(S["onet_ready"], 1)
            with pe.Fori(0, QCH // 9) as i:
                pe.wait_ge(S["coef_done"], i + 1)
                for j in range(9):
                    for part_ in range(3):
                        ins = nc.tensor.matmul(ps[7][:, j * 32:(j + 1) * 32], onet[:, ds((i * 9 + j) * P, P)],
                                               wbd[:, part_].rearrange("p q b -> p (q b)"), start=part_ == 0, stop=part_ == 2)
                ins.then_inc(S["coef_mm"], 1)
            pe.wait_ge(S["base_mm"], 1)
            for t in range(RT):
                nc.tensor.matmul(ps[5][:, t * ROWS:(t + 1) * ROWS], minb[:, t, :], ident[0:ROWS, 0:ROWS], start=True, stop=True)
            nc.tensor.matmul(ps[6][:, 0:ROWS], minb[:, RT, :], ident[0:ROWS, 0:ROWS], start=True, stop=True).then_inc(S["base_mm"], 1)
            pe.sem_inc(S["mm_done"], BCH)
            pe.wait_ge(S["rounds_ready"], 1)
            rounds = pe.value_load(rounds_i[0:1, 0:1], min_val=1, max_val=W // WIN)
            with pe.Fori(0, rounds) as r:
                with pe.Fori(0, NB // 2) as i:
                    for h in range(2):
                        n = r * NB + i * 2 + h
                        pe.wait_ge(S["c_ready"], n + r + 1)
                        for j in range(BCH):
                            pe.wait_ge(g[j], n * 16 + 16)
                            pe.wait_ge(S["acc_done"], n * BCH + j + 1)
                            for f in range(NF):
                                ins = nc.tensor.matmul(ps[j][:, f * 64:(f + 1) * 64], xg[:, j, f * P:(f + 1) * P],
                                                       cb[:, h, j].rearrange("p b w -> p (b w)"), start=True, stop=True)
                            ins.then_inc(S["mm_done"], 1)
            pe.wait_ge(S["table_ready"], 3)
            for half in range(2):
                for b in range(NBASE):
                    n = half * NBASE + b
                    pe.wait_ge(S[f"base_ld{n % 2}"], 16 * (n // 2 + 1))
                    for t in range(5 * half, 5 * half + 5):
                        m = min(P, W - t * P)
                        if b == 0 and t >= 8:
                            pe.wait_ge(S["xo_ready"], 2 * (t - 8) + 1)
                        for k in range(NF):
                            ins = nc.tensor.matmul(ps[t % 8][0:m, :], agg[:, k, b, t * P:t * P + m], bring[:, n % 2, k, :],
                                                   start=(b == 0 and k == 0), stop=(b == NBASE - 1 and k == NF - 1), skip_group_check=True)
                        if b == NBASE - 1:
                            ins.then_inc(S["cum_done"], 1)
                    pe.drain().then_inc(S["basis_mm"], 1)
            pe.wait_ge(S["x1_ld"], 16 * 5)
            for t in range(NT):
                if t >= 2:
                    pe.wait_ge(S["tp_done"], t - 1)
                else:
                    pe.wait_ge(S["xo_ready"], 2 * NT)
                for k in range(NF):
                    ins = nc.tensor.transpose(ps[t % 2][:, k * P:(k + 1) * P], xh2[:, t, k * P:(k + 1) * P], ident[:])
                ins.then_inc(S["tp"], 1)
            for t in range(NT):
                pe.wait_ge(S["tp_done"], t + 1)
                for k in range(NF):
                    ins = nc.tensor.matmul(ps[2][:, t * EX0:(t + 1) * EX0], xT[:, k, t * P:(t + 1) * P], wg[:, k, :], start=k == 0, stop=k == NF - 1)
            ins.then_inc(S["lg"], 1)
            for k in range(3):
                pe.wait_ge(S["cum"], k + 2)
                m = mb[:].rearrange("p t e -> p (t e)")
                if k != 1:
                    nc.tensor.matmul(ps[3][:, 0:NT * EX0], tri[:], m, start=True, stop=True)
                nc.tensor.matmul(ps[4][:, 0:NT * EX0], ones[:], m, start=True, stop=True).then_inc(S["lg"], 1)
            for c in range(SC):
                pe.wait_ge(gx[c % 6], 16 * (c // 6 + 1))
                if c >= 2:
                    pe.wait_ge(S["xe_ev"], c - 1)
                for k in range(NF):
                    ins = nc.tensor.transpose(ps[c % 2][:, k * P:(k + 1) * P], xer[:, c % 6, k * P:(k + 1) * P], ident[:])
                ins.then_inc(S["xe_tp"], 1)
            pe.wait_ge(S["xe_ev"], SC)
            pe.wait_ge(S["slots_ready"], 1)

            def up(e):
                pe.wait_ge(S[f"w0_ld{e % 2}"], 32 * (e // 2 + 1))
                if e >= 2:
                    pe.wait_ge(S["relu"], e - 1)
                for k in range(2):
                    for f in range(NF):
                        ins = nc.tensor.matmul(ps[2 + (e % 2) * 2 + k][:, 0:CAP], w1r[e % 2][:, f, k * P:(k + 1) * P],
                                               xe[:, f, e * CAP:(e + 1) * CAP], start=f == 0, stop=f == NF - 1)
                ins.then_inc(S["up"], 1)

            BANK = [6, 7, 0]

            def down(e):
                pe.wait_ge(S["relu"], e + 1)
                for s in range(3):
                    if e:
                        pe.wait_ge(S["y_ev"], 3 * (e - 1) + s + 1)
                    for k in range(2):
                        ins = nc.tensor.matmul(ps[BANK[s]][0:ST, :], hT[:, e % 2, k, s * ST:(s + 1) * ST], w2r[e % 2][:, k, :], start=k == 0, stop=k == 1)
                    ins.then_inc(S["down"], 1)

            up(0)
            for e in range(EX0):
                if e + 1 < EX0:
                    up(e + 1)
                down(e)
            pe.wait_ge(S["y_ev"], 3 * EX0)
            pe.sem_inc(S["n_mm"], BCH)
            with pe.Fori(0, rounds) as r:
                with pe.Fori(0, NB // 2) as i:
                    for h in range(2):
                        n = r * NB + i * 2 + h
                        pe.wait_ge(S["n_c"], n + r + 1)
                        for j in range(BCH):
                            pe.wait_ge(S["n_acc"], n * BCH + j + 1)
                            nc.tensor.matmul(ps[j][:, 0:UH * WIN], rside[:, h, j, :], lside[:, h, j].rearrange("p u w -> p (u w)"),
                                             start=True, stop=True).then_inc(S["n_mm"], 1)
            pe.wait_ge(S["n_ready"], 1)
            for t in range(NT):
                m = min(P, W - t * P)
                for q in range(3):
                    n = 3 * t + q
                    if n >= 2:
                        pe.wait_ge(S["tr_done"], n - 1)
                    for u in range(4 * q, min(4 * q + 4, UH)):
                        ins = nc.tensor.transpose(ps[6 + n % 2][0:m, (u % 4) * P:(u % 4 + 1) * P], nT[:, u, t * P:t * P + m], ident[:])
                    ins.then_inc(S["tr"], 1)
            pe.wait_ge(S["xh3_ready"], 1)
            pe.wait_ge(S["tr_done"], 3 * NT)
            BL = [(0, 512), (512, 512), (1024, 256)]
            for k in range(NF):
                for q, (a, w_) in enumerate(BL):
                    n = 3 * k + q
                    if n >= 3:
                        pe.wait_ge(S["sx_ev"], n - 2)
                    for t in range(NT):
                        r_ = min(P, N - t * P)
                        ins = nc.tensor.matmul(ps[2 + n % 3][:, 0:w_], xh3[0:r_, t, k * P:(k + 1) * P], adj[0:r_, t, a:a + w_], start=t == 0, stop=t == NT - 1)
                    ins.then_inc(S["sx"], 1)
            for t in range(NT):
                if t >= 2:
                    pe.wait_ge(S["tp3_done"], t - 1)
                r_ = rows(t)
                for k in range(NF):
                    ins = nc.tensor.transpose(ps[t % 2][:, k * P:k * P + r_], xh3[0:r_, t, k * P:(k + 1) * P], ident[0:r_, 0:r_])
                ins.then_inc(S["tp3"], 1)
            pe.wait_ge(S["tp3_done"], NT)
            pe.wait_ge(S["sx_ev"], 3 * NF)
            pe.wait_ge(S["wcn_ld"], 32)
            for t in range(NT):
                r_ = rows(t)
                pa, pb = ps[2 + 2 * (t % 2)], ps[3 + 2 * (t % 2)]
                if t >= 2:
                    pe.wait_ge(S["g_ev"], t - 1)
                for dst, left, right in ((pa, xT3, wcs), (pb, sT, wns)):
                    for k in range(NF):
                        ins = nc.tensor.matmul(dst[0:r_, :], left[:, k, t * P:t * P + r_], right[:, k, :], start=k == 0, stop=k == NF - 1)
                ins.then_inc(S["gm"], 1)
            pe.wait_ge(S["x4_ready"], 1)
            for t in range(TT1):
                if t >= 2:
                    pe.wait_ge(S["tp4_done"], t - 1)
                for k in range(NF):
                    ins = nc.tensor.transpose(ps[t % 2][:, k * P:(k + 1) * P], xh4[:, t, k * P:(k + 1) * P], ident[:])
                ins.then_inc(S["tp4"], 1)
            pe.wait_ge(S["tp4_done"], TT1)
            pe.wait_ge(S["g_ev"], NT)

            def up1(e):
                pe.wait_ge(S[f"w1_ld{e % 2}"], 32 * (e // 2 + 1))
                if e >= 2:
                    pe.wait_ge(S["gelu"], e - 1)
                for k in range(2):
                    for f in range(NF):
                        ins = nc.tensor.matmul(ps[(e % 2) * 2 + k][:], w1r[e % 2][:, f, k * P:(k + 1) * P], xT4[:, f, :], start=f == 0, stop=f == NF - 1)
                ins.then_inc(S["up1"], 1)

            up1(0)
            for e in range(EX1):
                if e + 1 < EX1:
                    up1(e + 1)
                pe.wait_ge(S["gelu"], e + 1)
                for t in range(TT1):
                    if e:
                        pe.wait_ge(S["ycopy"], TT1 * (e - 1) + t + 1)
                    for k in range(2):
                        ins = nc.tensor.matmul(ps[4 + t][:], hT1[:, e % 2, k, t * P:(t + 1) * P], w2r[e % 2][:, k, :], start=k == 0, stop=k == 1)
                    if t == TT1 - 1:
                        ins.then_inc(S["down1"], 1)
                    else:
                        ins.then_inc(S["n_round"], 1)

        @block.vector
        def _(dve):
            chain = [0]
            V = nc.vector

            def link(ins):
                chain[0] += 1
                ins.then_inc(S["dve"], 1)
                dve.wait_ge(S["dve"], chain[0])

            link(V.memset(eps[:], EPS))
            link(V.memset(ones[:], 1.0))
            link(V.memset(mv[:], 0.0))
            dve.wait_ge(S["const_ready"], 3)
            link(V.tensor_copy(iota[:], iota_i[:]))
            link(V.tensor_single_scalar(part_i[:, 1:2], part_i[:, 0:1], 31, ALU.bitwise_and))
            link(V.tensor_single_scalar(part_i[:, 2:3], part_i[:, 0:1], 5, ALU.logical_shift_right))
            link(V.tensor_copy(part[:], part_i[:]))
            link(V.tensor_scalar(ident[:], iota[:], part[:, 0:1], None, ALU.is_equal))
            link(V.tensor_scalar(tri[:], iota[:], part[:, 0:1], None, ALU.is_gt))
            link(V.tensor_scalar(qmask[:], iota[:, 0:4], part[:, 2:3], None, ALU.is_equal))
            dve.wait_ge(S["ld_rows"], 16)
            link(V.tensor_copy(dstr[0:ROWS], dstr_i[0:ROWS]))
            link(V.scalar_tensor_tensor(out=dstm[0:ROWS], in0=dstr[0:ROWS], scalar=float(N), in1=dstr[0:ROWS], op0=ALU.is_lt, op1=ALU.mult))
            link(V.tensor_reduce(mins[:, 0, :], dstr[0:ROWS], AX.X, ALU.min))
            link(V.tensor_reduce(mins[:, 1, :], dstm[0:ROWS], AX.X, ALU.max))
            link(V.tensor_tensor(mins[:, 2, :], mins[:, 1, :], mins[:, 0, :], ALU.subtract))
            link(V.tensor_reduce(mins[:, 1, 0:1], mins[:, 2, :], AX.X, ALU.max))
            link(V.tensor_copy(minb[:, 0:RT, :], mins[:, 0, :].unsqueeze(2).to_broadcast([ROWS, RT, P])))
            V.tensor_copy(minb[:, RT, :], mins[:, 1, 0:1].to_broadcast([ROWS, P])).then_inc(S["base_mm"], 1)
            dve.wait_ge(S["ld_small"], 80)
            dve.wait_ge(S["ld_small"], 80)
            res = wc4[:, :]
            link(V.tensor_copy(wpart[:, 0, :], res))
            link(V.tensor_tensor(res, res, wpart[:, 0, :], ALU.subtract))
            link(V.tensor_copy(wpart[:, 1, :], res))
            link(V.tensor_tensor(res, res, wpart[:, 1, :], ALU.subtract))
            link(V.tensor_copy(wpart[:, 2, :], res))
            for k in range(3):
                link(V.tensor_tensor(wbd[:, k], wpart[:, k, :].unsqueeze(1).to_broadcast([P, 4, NBASE]),
                                     qmask[:].unsqueeze(2).to_broadcast([P, 4, NBASE]), ALU.mult))
            dve.wait_ge(S["ld_x"], 32)
            layer_norm(dve, link, lambda t: xin[0:rows(t), t, :], lambda t: xh[0:rows(t), t, :], list(range(NT)), 1)
            V.engine_nop().then_inc(S["xh1_ready"], 1)
            dve.wait_ge(S["ld_etype"], 64)
            link(V.tensor_scalar(onet[:], etb[:], part[:, 1:2], None, ALU.is_equal))
            V.engine_nop().then_inc(S["onet_ready"], 1)
            dve.sem_inc(S["coef_done"], 1)
            dve.wait_ge(S["ld_edges"], 48)
            link(V.memset(coef[:, NCH:TCOL, :], 0.0))
            cq = coef[:, 0:NCH, :].rearrange("p (q c) b -> p q c b", q=4)
            wq4 = wgt[:, 0:NCH].rearrange("p (q c) -> p q c", q=4)
            pc = ps[7][:, 0:288].rearrange("p (c q b) -> p q c b", q=4, b=NBASE)
            with dve.Fori(0, QCH // 9) as i:
                dve.wait_ge(S["coef_mm"], i + 1)
                for q in range(4):
                    ins = V.tensor_tensor(cq[:, q, ds(i * 9, 9), :], pc[:, q],
                                          wq4[:, q, ds(i * 9, 9)].unsqueeze(2).to_broadcast([P, 9, NBASE]), ALU.mult)
                ins.then_inc(S["coef_done"], 1)
            link(V.tensor_copy(dstf[:], dst_i[:]))
            dve.wait_ge(S["base_mm"], 2)
            link(V.memset(base0[:, NCH:TCOL], 0.0))
            link(V.tensor_copy(base0[:, 0:NCH], ps[5][:, 0:NCH]))
            link(V.tensor_reduce(gap[:], ps[6][:, 0:ROWS], AX.X, ALU.max))
            link(V.tensor_copy(gap_i[:], gap[:]))
            link(V.tensor_single_scalar(gap_i[:], gap_i[:], 3, ALU.logical_shift_right))
            link(V.tensor_copy(gap[:], gap_i[:]))
            link(V.tensor_scalar(gap[:], gap[:], 1.0, None, ALU.add))
            V.tensor_copy(rounds_i[0:1, 0:1], gap[0:1, :]).then_inc(S["rounds_ready"], 1)
            dve.wait_ge(S["xh1_stored"], 32)
            dve.wait_ge(S["coef_done"], QCH // 9 + 1)
            link(V.memset(big[:, 0:SETUP], 0.0))
            link(V.tensor_copy(basef[:], base0[:]))
            dve.wait_ge(S["zeroed"], 1)
            dve.wait_ge(S["rounds_ready"], 1)
            rounds = dve.value_load(rounds_i[0:1, 0:1], min_val=1, max_val=W // WIN)
            dve.sem_inc(S["acc_done"], BCH)

            def round_tables(r, done):
                V.tensor_tensor(rel[:], dstf[:], basef[:], ALU.subtract).then_inc(done, 1)
                V.tensor_scalar(basec[:], basef[0:1, :], float(W - WIN), None, ALU.min).then_inc(done, 1)
                dve.wait_ge(done, r * 4 + 2)
                V.tensor_copy(basei[:], basec[:]).then_inc(done, 1)
                V.tensor_scalar(basef[:], basef[:], float(WIN), None, ALU.add).then_inc(done, 1)
                dve.wait_ge(done, r * 4 + 4)

            io8 = iota[:, 0:WIN].unsqueeze(1).to_broadcast([P, BCH, WIN])

            def build_c(r, b, h, n):
                V.tensor_tensor(oh[:, h], rel[:, ds(b * BCH, BCH)].unsqueeze(2).to_broadcast([P, BCH, WIN]), io8, ALU.is_equal).then_inc(S["tp_c"], 1)
                dve.wait_ge(S["tp_c"], n + 1)
                for j in range(BCH):
                    ins = V.tensor_tensor(cb[:, h, j], oh[:, h, j].unsqueeze(1).to_broadcast([P, NBASE, WIN]),
                                          coef[:, ds(b * BCH + j, 1), :].rearrange("p o b -> p (o b)").unsqueeze(2).to_broadcast([P, NBASE, WIN]), ALU.mult)
                ins.then_inc(S["c_ready"], 1)

            S["tp_c"] = sem("one_hot_done")
            with dve.Fori(0, rounds) as r:
                round_tables(r, S["round_ready"])
                build_c(r, 0, 0, r * (NB + 1))
                with dve.Fori(0, NB // 2) as i:
                    for h in range(2):
                        b = i * 2 + h
                        n = r * NB + b
                        build_c(r, b + 1, 1 - h, n + r + 1)
                        for j in range(BCH):
                            col = dve.value_load(basei[0:1, ds(b * BCH + j, 1)], min_val=0, max_val=W - WIN)
                            dve.wait_ge(S["mm_done"], n * BCH + j + 1 + BCH)
                            dve.wait_ge(S["acc_done"], n * BCH + j + BCH)
                            a = aggw[:, :, ds(col, WIN)]
                            V.tensor_tensor(a, ps[j][:, 0:256].rearrange("p (fb w) -> p fb w", w=WIN), a, ALU.add).then_inc(S["acc_done"], 1)
            dve.drain().then_inc(S["table_ready"], 3)
            for t in range(NT):
                r_ = rows(t)
                dve.wait_ge(S["cum_done"], t + 1)
                dve.wait_ge(S["x_ld"], 16 * (t + 1))
                if t:
                    dve.wait_ge(S["x1_stored"], 32 * t)
                link(V.tensor_tensor(xo[0:r_, :], ps[t % 8][0:r_, :], xt[0:r_, :], ALU.add))
                V.engine_nop().then_inc(S["xo_ready"], 1)
                link(V.tensor_tensor(xo[0:r_, :], xo[0:r_, :], hb[0:r_, :], ALU.add))
                layer_norm(dve, link, lambda t: xo[0:rows(t), :], lambda t: xn[0:rows(t), :], [t], 2 + t)
                V.engine_nop().then_inc(S["xo_ready"], 1)
            link(V.memset(x1[:, NT - 1, :], 0.0))
            link(V.memset(xh2[:, NT - 1, :], 0.0))
            V.engine_nop().then_inc(S["zeroed"], 6)
            dve.wait_ge(S["lg"], 1)
            G = lambda k: g_[:, k]
            sm = lambda k: s_[:, k, :]
            bc = lambda a: a.unsqueeze(2).to_broadcast([P, NT, EX0])
            lg = ps[2][:, 0:NT * EX0].rearrange("p (t e) -> p t e", e=EX0)
            link(V.tensor_reduce(sm(0), lg, AX.X, ALU.max))
            link(V.tensor_tensor(G(1), lg, bc(sm(0)), ALU.subtract))
            V.engine_nop().then_inc(S["cum"], 1)
            dve.wait_ge(S["act"], 1)
            link(V.tensor_reduce(sm(1), G(0), AX.X, ALU.add))
            link(V.reciprocal(sm(2), sm(1)))
            link(V.tensor_tensor(G(2), G(0), bc(sm(2)), ALU.mult))
            down_e = iota[:, 0:EX0].unsqueeze(1).to_broadcast([P, NT, EX0])
            link(V.tensor_scalar(G(3), G(2), 0.0, float(EX0), ALU.mult, ALU.add))
            link(V.tensor_tensor(G(3), G(3), down_e, ALU.subtract))
            valid = g_[:, 11]
            link(V.memset(valid, 1.0))
            link(V.tensor_scalar(sm(15), iota[:, 0:NT], float(P), part[:, 0:1], ALU.mult, ALU.add))
            link(V.tensor_scalar(sm(15), sm(15), float(N), None, ALU.is_lt))

            def first_max(gates, top, mask, tmp):
                link(V.tensor_reduce(top, gates, AX.X, ALU.max))
                link(V.tensor_tensor(tmp, gates, bc(top), ALU.is_equal))
                link(V.tensor_tensor(tmp, tmp, G(3), ALU.mult))
                link(V.tensor_reduce(sm(14), tmp, AX.X, ALU.max))
                link(V.tensor_tensor(mask, G(3), bc(sm(14)), ALU.is_equal))

            first_max(G(2), sm(3), G(4), G(5))
            link(V.tensor_scalar(sm(5), sm(14), -1.0, float(EX0), ALU.mult, ALU.add))
            link(V.tensor_scalar(G(5), G(4), -1.0, 1.0, ALU.mult, ALU.add))
            link(V.tensor_tensor(G(6), G(2), G(5), ALU.mult))
            first_max(G(6), sm(4), G(7), G(5))
            link(V.tensor_scalar(sm(6), sm(14), -1.0, float(EX0), ALU.mult, ALU.add))
            link(V.tensor_tensor(sm(7), sm(3), sm(4), ALU.add))
            link(V.tensor_scalar(sm(7), sm(7), 1e-9, None, ALU.add))
            link(V.reciprocal(sm(7), sm(7)))
            link(V.tensor_tensor(sm(3), sm(3), sm(7), ALU.mult))
            link(V.tensor_tensor(sm(4), sm(4), sm(7), ALU.mult))
            link(V.tensor_tensor(G(4), G(4), bc(sm(15)), ALU.mult))
            link(V.tensor_tensor(G(7), G(7), bc(sm(15)), ALU.mult))

            def places(mask, pos):
                link(V.tensor_copy(pos, ps[3][:, 0:NT * EX0].rearrange("p (t e) -> p t e", e=EX0)))
                link(V.memset(pref[:, 0, :], 0.0))
                for t in range(1, NT):
                    link(V.tensor_tensor(pref[:, t, :], pref[:, t - 1, :], ps[4][:, (t - 1) * EX0:t * EX0], ALU.add))
                link(V.tensor_tensor(pos, pos, pref[:], ALU.add))

            link(V.tensor_copy(mb[:], G(4)))
            V.engine_nop().then_inc(S["cum"], 1)
            dve.wait_ge(S["lg"], 2)
            places(G(4), G(8))
            link(V.tensor_tensor(G(8), G(8), G(4), ALU.mult))
            link(V.tensor_scalar(G(9), G(8), float(CAP), None, ALU.is_lt))
            link(V.tensor_tensor(G(4), G(4), G(9), ALU.mult))
            link(V.tensor_reduce(sm(8), G(8), AX.X, ALU.add))
            link(V.tensor_reduce(sm(9), G(4), AX.X, ALU.add))
            link(V.tensor_copy(mb[:], G(4)))
            V.engine_nop().then_inc(S["cum"], 1)
            dve.wait_ge(S["lg"], 3)
            link(V.tensor_reduce(g_[:, 10, 0, :], ps[4][:, 0:NT * EX0].rearrange("p (t e) -> p e t", e=EX0), AX.X, ALU.add))
            link(V.tensor_copy(mb[:], G(7)))
            V.engine_nop().then_inc(S["cum"], 1)
            dve.wait_ge(S["lg"], 4)
            places(G(7), G(8))
            link(V.tensor_tensor(G(8), G(8), g_[:, 10, 0:1, :].to_broadcast([P, NT, EX0]), ALU.add))
            link(V.tensor_tensor(G(8), G(8), G(7), ALU.mult))
            link(V.tensor_scalar(G(9), G(8), float(CAP), None, ALU.is_lt))
            link(V.tensor_tensor(G(7), G(7), G(9), ALU.mult))
            link(V.tensor_reduce(sm(10), G(8), AX.X, ALU.add))
            link(V.tensor_reduce(sm(11), G(7), AX.X, ALU.add))
            for k, (gate, ind, pos, kept) in enumerate(((3, 5, 8, 9), (4, 6, 10, 11))):
                link(V.tensor_tensor(sm(gate), sm(gate), sm(kept), ALU.mult))
                link(V.scalar_tensor_tensor(out=sm(12), in0=sm(ind), scalar=float(CAP), in1=sm(pos), op0=ALU.mult, op1=ALU.add))
                link(V.tensor_tensor(sm(12), sm(12), sm(kept), ALU.mult))
                link(V.tensor_copy(slot_i[:, 2 + k, :], sm(12)))
                link(V.tensor_scalar(sm(13), sm(kept), -NOSLOT, NOSLOT, ALU.mult, ALU.add))
                link(V.tensor_tensor(sm(13), sm(13), sm(12), ALU.add))
                link(V.tensor_copy(slot_i[:, k, :], sm(13)))
            V.engine_nop().then_inc(S["slots_ready"], 1)
            BANK = [6, 7, 0]
            for e in range(EX0):
                if e >= 2:
                    dve.wait_ge(S[f"y_st{e % 2}"], 16 * (e // 2))
                for s in range(3):
                    dve.wait_ge(S["down"], 3 * e + s + 1)
                    V.tensor_copy(ysb[0:ST, e % 2, s, :], ps[BANK[s]][0:ST, :]).then_inc(S["y_ev"], 1)
            for t in range(NT):
                for k in range(2):
                    n = 2 * t + k
                    r_ = rows(t)
                    dve.wait_ge(gy[n % 4], 16 * (n // 4 + 1))
                    link(V.scalar_tensor_tensor(out=x1[0:r_, t, :], in0=y2[0:r_, n % 4, :], scalar=s_[0:r_, 3 + k, t:t + 1], in1=x1[0:r_, t, :], op0=ALU.mult, op1=ALU.add))
                    V.engine_nop().then_inc(S["y2_used"], 1)
            layer_norm(dve, link, lambda t: x1[0:rows(t), t, :], lambda t: xh3[0:rows(t), t, :], list(range(NT)), 2 + NT)
            V.engine_nop().then_inc(S["xh3_ready"], 1)
            link(V.tensor_single_scalar(ulo_i[:], src_i[:], P - 1, ALU.bitwise_and))
            link(V.tensor_single_scalar(uhi_i[:], src_i[:], 7, ALU.logical_shift_right))
            link(V.tensor_copy(ulo[:], ulo_i[:]))
            link(V.tensor_copy(uhi[:], uhi_i[:]))
            dve.wait_ge(S["y_st0"], 8 * EX0)
            dve.wait_ge(S["y_st1"], 8 * EX0)
            link(V.memset(nT[:, :, :], 0.0))
            link(V.tensor_copy(basef[:], base0[:]))
            dve.sem_inc(S["n_acc"], BCH)
            S["n_oh"] = sem("one_hots_done")
            S["n_round2"] = sem("count_round_ready")
            ioP = iota[:].unsqueeze(1).to_broadcast([P, BCH, P])
            ioU = iota[:, 0:UH].unsqueeze(1).to_broadcast([P, BCH, UH])

            def build_n(b, h, n):
                at = ds(b * BCH, BCH)
                V.tensor_tensor(ohw[:, h], rel[:, at].unsqueeze(2).to_broadcast([P, BCH, WIN]), io8, ALU.is_equal)
                V.tensor_tensor(ohu[:, h], uhi[:, at].unsqueeze(2).to_broadcast([P, BCH, UH]), ioU, ALU.is_equal).then_inc(S["n_oh"], 1)
                V.tensor_tensor(rside[:, h], ulo[:, at].unsqueeze(2).to_broadcast([P, BCH, P]), ioP, ALU.is_equal)
                dve.wait_ge(S["n_oh"], n + 1)
                V.tensor_tensor(lside[:, h], ohw[:, h].unsqueeze(2).to_broadcast([P, BCH, UH, WIN]),
                                ohu[:, h].unsqueeze(3).to_broadcast([P, BCH, UH, WIN]), ALU.mult).then_inc(S["n_c"], 1)

            with dve.Fori(0, rounds) as r:
                round_tables(r, S["n_round2"])
                build_n(0, 0, r * (NB + 1))
                with dve.Fori(0, NB // 2) as i:
                    for h in range(2):
                        b = i * 2 + h
                        n = r * NB + b
                        build_n(b + 1, 1 - h, n + r + 1)
                        for j in range(BCH):
                            col = dve.value_load(basei[0:1, ds(b * BCH + j, 1)], min_val=0, max_val=W - WIN)
                            dve.wait_ge(S["n_mm"], n * BCH + j + 1 + BCH)
                            dve.wait_ge(S["n_acc"], n * BCH + j + BCH)
                            a = nT[:, :, ds(col, WIN)]
                            V.tensor_tensor(a, ps[j][:, 0:UH * WIN].rearrange("p (u w) -> p u w", w=WIN), a, ALU.add).then_inc(S["n_acc"], 1)
            dve.drain().then_inc(S["n_ready"], 1)
            link(V.tensor_reduce(cnt[:], nT[:, :, 0:N], AX.X, ALU.add))
            link(V.reciprocal(rcnt[:], cnt[:]))
            for t in range(NT):
                m = min(P, W - t * P)
                for q in range(3):
                    n = 3 * t + q
                    w_ = min(4 * P, NP - 4 * P * q)
                    dve.wait_ge(S["tr"], n + 1)
                    V.tensor_copy(adj[0:m, t, 4 * P * q:4 * P * q + w_], ps[6 + n % 2][0:m, 0:w_]).then_inc(S["tr_done"], 1)
            BL = [(0, 512), (512, 512), (1024, 256)]
            for k in range(NF):
                for q, (a, w_) in enumerate(BL):
                    n = 3 * k + q
                    dve.wait_ge(S["sx"], n + 1)
                    V.tensor_copy(sT[:, k, a:a + w_], ps[2 + n % 3][:, 0:w_]).then_inc(S["sx_ev"], 1)
            dve.wait_ge(S["bias_ld"], 16)
            for t in range(NT):
                r_ = rows(t)
                pa, pb = ps[2 + 2 * (t % 2)], ps[3 + 2 * (t % 2)]
                x_t = x1[0:r_, t, :]
                dve.wait_ge(S["gm"], t + 1)
                link(V.scalar_tensor_tensor(out=x_t, in0=pb[0:r_, :], scalar=rcnt[0:r_, t:t + 1], in1=x_t, op0=ALU.mult, op1=ALU.add))
                link(V.tensor_tensor(x_t, pa[0:r_, :], x_t, ALU.add))
                V.tensor_tensor(x_t, x_t, gbias[0:r_, :], ALU.add).then_inc(S["g_ev"], 1)
            dve.wait_ge(S["g_ev"], NT)
            layer_norm(dve, link, lambda t: x1[:, t, :], lambda t: xh4[:, t, :], list(range(TT1)), 3 + NT)
            V.engine_nop().then_inc(S["x4_ready"], 1)
            dve.wait_ge(S["ld_moe"], 32)
            link(V.tensor_copy(ef[:], ei[:]))
            for t in range(TT1):
                for k in range(TOPK):
                    link(V.tensor_scalar(combt[:, t, k, :], iota[:, 0:EX1], ef[:, t, k:k + 1], ew[:, t, k:k + 1], ALU.is_equal, ALU.mult))
            link(V.tensor_tensor(comb[:], combt[:, :, 0, :], combt[:, :, 1, :], ALU.add))
            for e in range(EX1):
                for t in range(TT1):
                    if t == TT1 - 1:
                        dve.wait_ge(S["down1"], e + 1)
                    else:
                        dve.wait_ge(S["n_round"], 3 * e + t + 1)
                    V.scalar_tensor_tensor(out=x1[:, t, :], in0=ps[4 + t][:], scalar=comb[:, t, e:e + 1], in1=x1[:, t, :], op0=ALU.mult, op1=ALU.add).then_inc(S["ycopy"], 1)
                    dve.wait_ge(S["ycopy"], TT1 * e + t + 1)
            V.engine_nop().then_inc(S["fin"], 1)


def kernel(**inputs):
    import numpy as np
    import concourse.bacc as bacc
    from concourse.bass_utils import run_bass_kernel_spmd as run

    def padded(a, n, fill):
        flat = np.full(n * P, fill, a.dtype)
        flat[:E] = a.reshape(-1)
        return flat.reshape(n, P)

    a = {k: np.asarray(v) for k, v in inputs.items()}
    arrays = {
        "x": a["x"],
        "src_cols": np.ascontiguousarray(padded(a["src"], TCOL, 0).T),
        "dst_cols": np.ascontiguousarray(padded(a["dst"], TCOL, N).T),
        "wgt_cols": np.ascontiguousarray(padded(a["edge_weight1"], TCOL, 0).T),
        "etype": padded(a["edge_type_32"], NCH, 0).reshape(4, QCH * P),
        "dst_rows": padded(a["dst"], NCH, N),
        "bases": a["L0_gnn_bases"], "w_comp": a["L0_gnn_w_comp"], "h_bias": a["L0_gnn_h_bias"].reshape(1, F),
        "w_gating": a["L0_ffn_w_gating"], "f0_w1": a["L0_ffn_w1"], "f0_w2": a["L0_ffn_w2"],
        "wc": a["L1_gnn_wc"], "wn": a["L1_gnn_wn"], "g1_bias": a["L1_gnn_bias"].reshape(1, F),
        "x_weights": a["L1_ffn_expert_weights"], "x_indices": a["L1_ffn_expert_indices"],
        "f1_w1": a["L1_ffn_w1"], "f1_w2": a["L1_ffn_w2"],
    }
    arrays = {k: np.ascontiguousarray(v) for k, v in arrays.items()}
    nc = bacc.Bacc("TRN2", target_bir_lowering=False, num_devices=1)
    t = {k: nc.dram_tensor("in_" + k, v.shape, mybir.dt.from_np(v.dtype), kind="ExternalInput").ap() for k, v in arrays.items()}
    out = nc.dram_tensor("out", (N, F), f32, kind="ExternalOutput").ap()
    build(nc, out=out, **t)
    r = run(nc, [{"in_" + k: v for k, v in arrays.items()}], core_ids=[0])
    return r.results[0]["out"]
```

```python
import concourse.bass as bass
from concourse import mybir
from contextlib import ExitStack

P = 128
N = 1250
F = 512
NF = F // P
NT = -(-N // P)
LAST = N - (NT - 1) * P
NP = NT * P
HALF = NT // 2
E = 41250
NREL, NBASE = 32, 8
EX0, CAP, H0 = 16, 312, 256
ST = CAP // 3
SLOTS = EX0 * CAP
T1, EX1, TOPK, H1 = 512, 8, 2, 256
TT1 = T1 // P
EPS = 1e-5

BCH = 6
NB = -(-E // (P * BCH))
NCH = NB * BCH
TCOL = NCH + BCH
WIN = 8
W = -(-N // WIN) * WIN + WIN
PITCH = 8
ROWS = 108
RT = NCH // ROWS
QCH = NCH // 4
CSTEP = 9
GRP = 3
WINN = 16
NGRP = BCH // GRP
PARTS = 3
NPITCH = 4
N_AHEAD = 12
N_PER = 3
NOSLOT = 8192.0
UH = NT

f32 = mybir.dt.float32
bf16 = mybir.dt.bfloat16
i32 = mybir.dt.int32
ALU = mybir.AluOpType
ACT = mybir.ActivationFunctionType
AX = mybir.AxisListType
ds = bass.ds
assert N_AHEAD + N_PER * (EX0 - 2) == NB


def rows(t):
    return P if t < NT - 1 else LAST


def cols(t):
    return min(P, W - t * P)


def build(nc, x, src_cols, dst_cols, wgt_cols, etype, dst_rows, bases, w_comp, h_bias, w_gating, f0_w1, f0_w2,
          wc, wn, g1_bias, x_weights, x_indices, f1_w1, f1_w2, out):
    xs_d = nc.dram_tensor("xs_d", (N, PARTS * F), bf16).ap()
    x1_d = nc.dram_tensor("x1_d", (N, F), f32).ap()
    xh2_d = nc.dram_tensor("xh2_d", (N, F), f32).ap()
    slot_d = nc.dram_tensor("slot_d", (SLOTS, 1), i32).ap()
    ye_d = nc.dram_tensor("ye_d", (SLOTS, F), f32).ap()

    with ExitStack() as ctx:
        def sb(name, shape, dt=f32):
            return ctx.enter_context(nc.sbuf_tensor(name, shape, dt))

        def sem(name):
            return ctx.enter_context(nc.semaphore(name))

        big = sb("big", [P, NF * NBASE * W])
        XG = BCH * PARTS * F // 2
        mid = sb("mid", [P, XG + TCOL * PARTS * NBASE // 2])

        agg = big[:, :].rearrange("p (f b w) -> p f b w", f=NF, b=NBASE)
        aggw = big[:, :].rearrange("p (fb w) -> p fb w", w=W)
        at = [0]

        def take(n):
            at[0] += n
            return big[:, at[0] - n:at[0]]

        xin = take(NT * F).rearrange("p (t f) -> p t f", f=F)
        xh = take(NT * F).rearrange("p (t f) -> p t f", f=F)
        xs = take(PARTS * NT * F // 2).bitcast(bf16).rearrange("p (t s f) -> p t s f", s=PARTS, f=F)
        etb = take(QCH * P).bitcast(i32)
        onet = take(QCH * P // 2).bitcast(bf16)
        dstr_i = take(RT * P).bitcast(i32).rearrange("p (t e) -> p t e", e=P)
        dstr = take(RT * P).rearrange("p (t e) -> p t e", e=P)
        dstm = take(RT * P).rearrange("p (t e) -> p t e", e=P)
        minb = take(RT * P)[0:ROWS, :].rearrange("p (t e) -> p t e", e=P)
        maxb = take(RT * P)[0:ROWS, :].rearrange("p (t e) -> p t e", e=P)
        wgt = take(TCOL)
        dst_i = take(TCOL).bitcast(i32)
        iota_i = take(P).bitcast(i32)
        gaps = take(NCH)
        top3 = take(NCH // GRP)
        coeff = take(NCH * NBASE).rearrange("p (c b) -> p c b", b=NBASE)
        SETUP = at[0]
        ZCUT = [0, SETUP * 2 // 5, SETUP * 3 // 5 + SETUP // 10, SETUP]

        xg = mid[:, 0:XG].bitcast(bf16).rearrange("p (j s f) -> p j s f", j=BCH, s=PARTS)
        coef = mid[:, XG:XG + TCOL * PARTS * NBASE // 2].bitcast(bf16).rearrange("p (s c b) -> p s c b", s=PARTS, b=NBASE)
        cb = sb("cb", [P, 2, PARTS, BCH, NBASE, WIN], bf16)
        oh = sb("oh", [P, 2, BCH, WIN], bf16)
        rel = sb("rel", [P, TCOL])
        basef = sb("basef", [P, TCOL])
        basei = sb("basei", [1, NB * PITCH], i32)
        src_i = sb("src_i", [P, TCOL], i32)
        dstf = sb("dstf", [P, TCOL])
        idx = sb("idx", [P, 2, BCH], i32)
        rounds_i = sb("rounds_i", [1, 2], i32)
        mins = sb("mins", [ROWS, 3, RT])
        gap = sb("gap", [P, 2])
        gap_i = sb("gap_i", [P, 2], i32)
        part_i = sb("part_i", [P, 3], i32)
        iota = sb("iota", [P, P])
        part = sb("part", [P, 3])
        ident = sb("ident", [P, P])
        tri = sb("tri", [P, P], bf16)
        ones = sb("ones", [P, P], bf16)
        wc4 = sb("wc4", [P, NBASE])
        wpart = sb("wpart", [P, PARTS, NBASE], bf16)
        qmask = sb("qmask", [P, 4])
        wbd = sb("wbd", [P, PARTS, 4, NBASE], bf16)
        eps = sb("eps", [P, 1])
        stats = sb("stats", [P, 6])
        mv = sb("mv", [P, NT, 2])
        std = sb("std", [P, NT])
        rstd = sb("rstd", [P, NT])

        def m(a, n):
            return mid[:, a:a + n]

        bring = m(0, 4096).rearrange("p (s k f) -> p s k f", s=2, k=NF)
        hb = m(4096, F)
        xt = m(4608, F)
        xo = m(5120, F)
        xn = m(5632, 2 * F).rearrange("p (s f) -> p s f", s=2)
        xT = m(6656, 2 * F).rearrange("p (s k n) -> p s k n", s=2, k=NF)
        wg = m(7680, NF * EX0).rearrange("p (k e) -> p k e", e=EX0)
        x1 = big[:, 0:5120].rearrange("p (t f) -> p t f", f=F)
        xer = big[0:ST, 5120:5120 + 6 * F].rearrange("p (j f) -> p j f", f=F)
        xe = big[:, 35680:35680 + 2 * NF * CAP].rearrange("p (s k c) -> p s k c", s=2, k=NF)
        gbias = big[:, 39936:39936 + F]
        w1r = [m(1024 * s, 1024).rearrange("p (k h) -> p k h", k=NF) for s in range(2)]
        w2r = [m(2048 + 1024 * s, 1024).rearrange("p (k f) -> p k f", k=2) for s in range(2)]
        hT = m(4096, 4 * CAP).rearrange("p (s k c) -> p s k c", s=2, k=2)
        ysb = m(5344, 6 * F)[0:ST, :].rearrange("p (s k f) -> p s k f", s=2, k=3)
        g_ = big[:, 35680:35680 + 12 * NT * EX0].rearrange("p (k t e) -> p k t e", k=12, t=NT)
        s_ = sb("small", [P, 16, NT])
        mb = big[:, 37760:37760 + NT * EX0 // 2].bitcast(bf16).rearrange("p (t e) -> p t e", e=EX0)
        pref = big[:, 37600:37600 + NT * EX0].rearrange("p (t e) -> p t e", t=NT)
        slot_i = sb("slot_i", [P, 4, NT], i32)
        tok_i = sb("tok_i", [P, NT], i32)
        slots_in = sb("slots_in", [ST, 3 * EX0], i32)
        zero_i = sb("zero_i", [ST, 3 * EX0], i32)
        lside = big[:, 8192:9152].bitcast(bf16).rearrange("p (h j u w) -> p h j u w", h=2, j=BCH, u=UH)
        rside = big[:, 9152:9920].bitcast(bf16).rearrange("p (h j u) -> p h j u", h=2, j=BCH)
        ohw = big[:, 9920:10016].bitcast(bf16).rearrange("p (h j w) -> p h j w", h=2, j=BCH)
        ohu = big[:, 10016:10076].bitcast(bf16).rearrange("p (h j u) -> p h j u", h=2, j=BCH)
        nT = big[:, 10240:10240 + UH * W].rearrange("p (u w) -> p u w", w=W)
        adj = big[:, 22880:22880 + NT * NP].rearrange("p (t u) -> p t u", u=NP)
        y2 = big[:, 35680:35680 + 6 * F].rearrange("p (j f) -> p j f", f=F)
        xh3 = big[:, 5120:10240].rearrange("p (t f) -> p t f", f=F)
        xT3 = big[:, 10240:15360].rearrange("p (k n) -> p k n", n=NP)
        sT = big[:, 15360:20480].rearrange("p (k n) -> p k n", n=NP)
        ulo, uhi, reln = basef, dstf, rel
        base3 = sb("base3", [P, NB * NGRP])
        base3i = basei[:, 0:NB * NPITCH]
        wcs = m(0, 2048).rearrange("p (k f) -> p k f", k=NF)
        wns = m(2048, 2048).rearrange("p (k f) -> p k f", k=NF)
        cnt = sb("cnt", [P, UH])
        rcnt = sb("rcnt", [P, UH])
        w1s = [m(4096 + 2048 * s, 1024).rearrange("p (k h) -> p k h", k=NF) for s in range(2)]
        w2s = [m(5120 + 2048 * s, 1024).rearrange("p (k f) -> p k f", k=2) for s in range(2)]
        xh4 = big[:, 5120:5120 + TT1 * F].rearrange("p (t f) -> p t f", f=F)
        xT4 = big[:, 22880:22880 + NF * T1].rearrange("p (k n) -> p k n", n=T1)
        hT1 = big[:, 25000:25000 + 4 * T1].rearrange("p (s k n) -> p s k n", s=2, k=2)
        ei = sb("ei", [P, TT1, TOPK], i32)
        ew = sb("ew", [P, TT1, TOPK])
        ef = big[:, 29100:29100 + TT1 * TOPK].rearrange("p (t k) -> p t k", k=TOPK)
        comb = big[:, 29200:29200 + TT1 * EX1].rearrange("p (t e) -> p t e", e=EX1)
        combt = big[:, 29300:29300 + TT1 * TOPK * EX1].rearrange("p (t k e) -> p t k e", k=TOPK, e=EX1)

        ps = [ctx.enter_context(nc.psum_tensor(f"ps{i}", [P, 512], f32)) for i in range(8)]

        names = """edges_in rows_in etype_in x_in w_in hb_in weight_in
        consts zeros norm_ready split_h split_r split_m xs_ready xs_out onet_ready coef_mm coef_out coef_h coef_m coef_r base_mm rounds_ready
        agg_zero oh_done round_ready c_ready mm_done acc_done idx_ready agg_done
        basis_mm tile_mm base_in0 base_in1 xt_in xt_used tile_ready tile_out0 tile_out1 std_req std_done gate_in
        tp tp_out logits exp_req exp_done mask_ready places slots_ready slot_zero slot_set slot_in x1_in
        xe_tp xe_out w1_in0 w1_in1 w2_in0 w2_in1 up relu down y_out y_st0 y_st1 y2_used
        n_zero n_oh n_c n_mm n_acc n_round n_ready tr tr_outa tr_outv xh3_ready sums sums_out wcn_in gbias_in tp3 tp3_out
        gm g_out x4_ready tp4 tp4_out up1 gelu down1 y1_used moe_in final out_st dve""".split()
        S = {n: sem(n) for n in names}
        g = [sem(f"gather{j}") for j in range(BCH)]
        gx = [sem(f"gather_slot{j}") for j in range(6)]
        gy = [sem(f"gather_out{j}") for j in range(6)]
        block = ctx.enter_context(nc.Block())

        def window_rounds(eng, k):
            eng.wait_ge(S["rounds_ready"], 1)
            return eng.value_load(rounds_i[0:1, k:k + 1], min_val=1, max_val=W // WIN)

        @block.sync
        def _(sp):
            sp.dma_start(xin[:, 0:NT - 1, :], x[0:(NT - 1) * P, :].rearrange("(t p) f -> p t f", p=P)).then_inc(S["x_in"], 16)
            sp.dma_start(xin[0:LAST, NT - 1, :], x[(NT - 1) * P:N, :]).then_inc(S["x_in"], 16)
            sp.dma_start(dstr_i[0:ROWS, :, :], dst_rows.rearrange("(t p) e -> p t e", p=ROWS)).then_inc(S["rows_in"], 16)
            for q in range(4):
                sp.dma_start(etb[32 * q:32 * q + 32, :], etype[q:q + 1, :].to_broadcast([32, QCH * P])).then_inc(S["etype_in"], 16)
            sp.wait_ge(S["xs_ready"], 1)
            sp.dma_start(xs_d[0:(NT - 1) * P, :].rearrange("(t p) f -> p t f", p=P), xs[:, 0:NT - 1].rearrange("p t s f -> p t (s f)")).then_inc(S["xs_out"], 16)
            sp.dma_start(xs_d[(NT - 1) * P:N, :], xs[0:LAST, NT - 1].rearrange("p s f -> p (s f)")).then_inc(S["xs_out"], 16)
            sp.wait_ge(S["zeros"], 1)
            sp.dma_start(slot_d.rearrange("(p c) o -> p (c o)", p=ST), zero_i[:]).then_inc(S["slot_zero"], 16)
            sp.wait_ge(S["agg_done"], 1)
            sp.dma_start(xt[:], x[0:P, :]).then_inc(S["xt_in"], 16)
            for n in range(2 * NBASE):
                if n >= 2:
                    sp.wait_ge(S["basis_mm"], n - 1)
                sp.dma_start(bring[:, n % 2], bases[n % NBASE].rearrange("(k p) f -> p k f", p=P)).then_inc(S[f"base_in{n % 2}"], 16)
                if n == 0:
                    sp.dma_start(hb[:], h_bias.to_broadcast([P, F])).then_inc(S["hb_in"], 16)
                    sp.dma_start(wg[:, :, :], w_gating.rearrange("(k p) e -> p k e", p=P)).then_inc(S["gate_in"], 16)
            sp.wait_ge(S["basis_mm"], 2 * NBASE)
            for e in range(2):
                sp.dma_start(w1r[e], f0_w1[e].rearrange("(k p) h -> p k h", p=P)).then_inc(S[f"w1_in{e}"], 16)
                sp.dma_start(w2r[e], f0_w2[e].rearrange("(k p) f -> p k f", p=P)).then_inc(S[f"w2_in{e}"], 16)
            sp.wait_ge(S["tile_out0"], 32 * HALF)
            sp.wait_ge(S["tile_out1"], 32 * HALF)
            sp.dma_start(x1[:, 0:NT - 1, :], x1_d[0:(NT - 1) * P, :].rearrange("(t p) f -> p t f", p=P)).then_inc(S["x1_in"], 16)
            sp.dma_start(x1[0:LAST, NT - 1, :], x1_d[(NT - 1) * P:N, :]).then_inc(S["x1_in"], 16)
            sp.dma_start(gbias[:], g1_bias.to_broadcast([P, F])).then_inc(S["gbias_in"], 16)
            sp.dma_start(ei[:], x_indices.rearrange("(t p) k -> p t k", p=P)).then_inc(S["moe_in"], 16)
            sp.dma_start(ew[:], x_weights.rearrange("(t p) k -> p t k", p=P)).then_inc(S["moe_in"], 16)
            sp.wait_ge(S["slot_set"], 16 * 2 * NT)
            sp.dma_start(slots_in[:], slot_d.rearrange("(p c) o -> p (c o)", p=ST)).then_inc(S["slot_in"], 16)

            def expert_io(e, h, more):
                if more:
                    sp.wait_ge(S["up"], e + 1)
                    sp.dma_start(w1r[h], f0_w1[ds(e + 2, 1)].rearrange("o (k p) h -> p (o k) h", p=P)).then_inc(S[f"w1_in{h}"], 16)
                    sp.wait_ge(S["down"], 3 * e + 3)
                    sp.dma_start(w2r[h], f0_w2[ds(e + 2, 1)].rearrange("o (k p) f -> p (o k) f", p=P)).then_inc(S[f"w2_in{h}"], 16)
                sp.wait_ge(S["y_out"], 3 * e + 3)
                sp.dma_start(ye_d[ds(e * CAP, CAP), :].rearrange("(s p) f -> p s f", p=ST), ysb[:, h]).then_inc(S[f"y_st{h}"], 16)

            with sp.Fori(0, EX0 // 2 - 1) as i:
                for h in range(2):
                    expert_io(i * 2 + h, h, True)
            for h in range(2):
                expert_io(EX0 - 2 + h, h, False)
            sp.dma_start(wcs[:, :, :], wc.rearrange("(k p) f -> p k f", p=P)).then_inc(S["wcn_in"], 16)
            sp.dma_start(wns[:, :, :], wn.rearrange("(k p) f -> p k f", p=P)).then_inc(S["wcn_in"], 16)
            sp.wait_ge(S["y_st0"], 16 * EX0 // 2)
            sp.wait_ge(S["y_st1"], 16 * EX0 // 2)
            for e in range(EX1):
                w = w1s[e % 2], w2s[e % 2]
                if e >= 2:
                    sp.wait_ge(S["up1"], e - 1)
                sp.dma_start(w[0], f1_w1[e].rearrange("(k p) h -> p k h", p=P)).then_inc(S[f"w1_in{e % 2}"], 16)
                if e >= 2:
                    sp.wait_ge(S["down1"], TT1 * (e - 1))
                sp.dma_start(w[1], f1_w2[e].rearrange("(k p) f -> p k f", p=P)).then_inc(S[f"w2_in{e % 2}"], 16)
                if e == 1:
                    sp.wait_ge(S["g_out"], NT)
                    sp.dma_start(out[T1:(NT - 1) * P, :].rearrange("(t p) f -> p t f", p=P), x1[:, TT1:NT - 1, :]).then_inc(S["out_st"], 16)
                    sp.dma_start(out[(NT - 1) * P:N, :], x1[0:LAST, NT - 1, :]).then_inc(S["out_st"], 16)
            for t in range(TT1):
                sp.wait_ge(S["y1_used"], TT1 * (EX1 - 1) + t + 1)
                sp.dma_start(out[t * P:(t + 1) * P, :], x1[:, t, :]).then_inc(S["out_st"], 16)
            sp.wait_ge(S["out_st"], 16 * (2 + TT1))


        @block.gpsimd
        def _(pool):
            nc.gpsimd.iota(iota_i[:], pattern=[[1, P]], base=0, channel_multiplier=0).then_inc(S["consts"], 1)
            nc.gpsimd.iota(part_i[:, 0:1], pattern=[[1, 1]], base=0, channel_multiplier=1).then_inc(S["consts"], 1)
            nc.gpsimd.iota(tok_i[:], pattern=[[P, NT]], base=0, channel_multiplier=1).then_inc(S["consts"], 1)
            nc.gpsimd.memset(zero_i[:], 0).then_inc(S["zeros"], 1)
            pool.dma_start(src_i[:], src_cols).then_inc(S["edges_in"], 16)
            pool.dma_start(dst_i[:], dst_cols).then_inc(S["edges_in"], 16)
            pool.dma_start(wgt[:], wgt_cols).then_inc(S["edges_in"], 16)
            nc.gpsimd.memset(big[:, SETUP:NF * NBASE * W], 0.0).then_inc(S["agg_zero"], 1)
            pool.wait_ge(S["coef_r"], 2)
            pool.wait_ge(S["xs_out"], 32)
            nc.gpsimd.memset(big[:, ZCUT[2]:ZCUT[3]], 0.0).then_inc(S["agg_zero"], 1)
            rounds = window_rounds(pool, 0)
            with pool.Fori(0, rounds) as r:
                with pool.Fori(0, NB // 2) as i:
                    for h in range(2):
                        n = r * NB + i * 2 + h
                        pool.wait_ge(S["idx_ready"], n + 1)
                        for j in range(BCH):
                            pool.wait_ge(S["mm_done"], n * BCH + j + 1)
                            pool.nop(nofuse=True)
                            pool.indirect_dma_start(xg[:, j].rearrange("p s f -> p (s f)"), None, xs_d,
                                                    bass.IndirectOffsetOnAxis(idx[:, h, j:j + 1], 0)).then_inc(g[j], 16)
            pool.wait_ge(S["basis_mm"], 2 * NBASE)
            nc.gpsimd.memset(nT[:, :, :], 0.0).then_inc(S["n_zero"], 1)
            pool.wait_ge(S["slot_zero"], 16)
            pool.wait_ge(S["slots_ready"], 1)
            for t in range(NT):
                for k in range(2):
                    pool.indirect_dma_start(slot_d, bass.IndirectOffsetOnAxis(slot_i[:, k, t:t + 1], 0), tok_i[:, t:t + 1], None,
                                            bounds_check=SLOTS - 1, oob_is_err=False).then_inc(S["slot_set"], 16)
            pool.wait_ge(S["slot_in"], 16)
            for c in range(3 * EX0):
                if c >= 6:
                    pool.wait_ge(S["xe_tp"], c - 5)
                pool.indirect_dma_start(xer[:, c % 6, :], None, xh2_d, bass.IndirectOffsetOnAxis(slots_in[:, c:c + 1], 0)).then_inc(gx[c % 6], 16)
            pool.wait_ge(S["y_st0"], 16 * EX0 // 2)
            pool.wait_ge(S["y_st1"], 16 * EX0 // 2)
            pool.wait_ge(S["up"], EX0)
            for n in range(2 * NT):
                if n >= 6:
                    pool.wait_ge(S["y2_used"], n - 5)
                pool.indirect_dma_start(y2[:, n % 6, :], None, ye_d, bass.IndirectOffsetOnAxis(slot_i[:, 2 + n % 2, n // 2:n // 2 + 1], 0)).then_inc(gy[n % 6], 16)

        @block.scalar
        def _(act):
            roots = [0]

            def root(a, b):
                roots[0] += 1
                act.wait_ge(S["std_req"], roots[0])
                nc.scalar.activation(std[:, a:b], mv[:, a:b, 1], ACT.Sqrt, bias=eps[:]).then_inc(S["std_done"], 1)

            for q in range(4):
                act.dma_start(wc4[32 * q:32 * q + 32, :], w_comp).then_inc(S["w_in"], 16)
            root(0, NT)
            for t in range(NT):
                act.wait_ge(S["norm_ready"], t + 1)
                nc.scalar.copy(xs[0:rows(t), t, 0], xh[0:rows(t), t]).then_inc(S["split_h"], 1)
            for t in range(NT):
                act.wait_ge(S["split_r"], t + 1)
                nc.scalar.copy(xs[0:rows(t), t, 1], xh[0:rows(t), t]).then_inc(S["split_m"], 1)
            act.wait_ge(S["coef_out"], QCH // CSTEP + 1)
            nc.scalar.copy(coef[:, 0, 0:NCH], coeff[:, :]).then_inc(S["coef_h"], 1)
            act.wait_ge(S["coef_r"], 1)
            nc.scalar.copy(coef[:, 1, 0:NCH], coeff[:, :]).then_inc(S["coef_m"], 1)
            act.wait_ge(S["coef_r"], 2)
            act.wait_ge(S["xs_out"], 32)
            nc.scalar.memzero(big[:, ZCUT[1]:ZCUT[2]]).then_inc(S["agg_zero"], 1)
            rounds = window_rounds(act, 0)
            with act.Fori(0, rounds) as r:
                with act.Fori(0, NB // 2) as i:
                    for h in range(2):
                        n = r * NB + i * 2 + h
                        act.wait_ge(S["mm_done"], n * BCH + 1)
                        nc.scalar.copy(idx[:, h, :], src_i[:, ds((i * 2 + h) * BCH, BCH)]).then_inc(S["idx_ready"], 1)

            def tile_columns(t):
                act.wait_ge(S["tp"], t + 1)
                if t >= 2:
                    act.wait_ge(S["logits"], t - 1)
                nc.scalar.copy(xT[:, t % 2, :, 0:rows(t)], ps[2 + t % 2][:].rearrange("p (k n) -> p k n", k=NF)[:, :, 0:rows(t)]).then_inc(S["tp_out"], 1)

            for t in range(NT):
                r_ = rows(t)
                if t == HALF:
                    tile_columns(t - 1)
                root(t, t + 1)
                act.wait_ge(S["tile_ready"], t + 1)
                act.dma_start(xh2_d[t * P:t * P + r_, :], xn[0:r_, t % 2, :]).then_inc(S[f"tile_out{t % 2}"], 16)
                act.dma_start(x1_d[t * P:t * P + r_, :], xo[0:r_, :]).then_inc(S[f"tile_out{t % 2}"], 16)
                if t + 1 < NT:
                    act.wait_ge(S["xt_used"], t + 1)
                    act.dma_start(xt[0:rows(t + 1), :], x[(t + 1) * P:(t + 1) * P + rows(t + 1), :]).then_inc(S["xt_in"], 16)
                if t and t != HALF:
                    tile_columns(t - 1)
            tile_columns(NT - 1)
            act.wait_ge(S["exp_req"], 1)
            nc.scalar.activation(g_[:, 0], g_[:, 1], ACT.Exp).then_inc(S["exp_done"], 1)

            def slot_tile(e, h, s):
                act.wait_ge(S["xe_tp"], e * 3 + s + 1)
                nc.scalar.copy(xe[:, h, :, s * ST:(s + 1) * ST], ps[0][:, 0:NF * ST].rearrange("p (k n) -> p k n", k=NF)).then_inc(S["xe_out"], 1)

            def relu(e, h):
                act.wait_ge(S["up"], e + 1)
                for k in range(2):
                    ins = nc.scalar.activation(hT[:, h, k, :], ps[2 + k][:, 0:CAP], ACT.Relu)
                ins.then_inc(S["relu"], 1)

            def expert_out(e, h, ahead, stored):
                if stored is not None:
                    act.wait_ge(S[f"y_st{h}"], stored)
                for s in range(3):
                    act.wait_ge(S["down"], e * 3 + s + 1)
                    nc.scalar.copy(ysb[:, h, s, :], ps[6 + (h + s) % 2][0:ST, :]).then_inc(S["y_out"], 1)
                    if ahead:
                        slot_tile(e + 2, h, s)

            act.wait_ge(S["tile_out0"], 32 * HALF)
            act.wait_ge(S["tile_out1"], 32 * HALF)
            for s in range(3):
                slot_tile(0, 0, s)
            relu(0, 0)
            for s in range(3):
                slot_tile(1, 1, s)
            relu(1, 1)
            expert_out(0, 0, True, None)
            act.wait_ge(S["down"], 3)
            relu(2, 0)
            expert_out(1, 1, True, None)
            with act.Fori(1, EX0 // 2 - 1) as i:
                for h in range(2):
                    e = i * 2 + h
                    act.wait_ge(S["down"], e * 3)
                    relu(e + 1, 1 - h)
                    expert_out(e, h, True, i * 16)
            relu(EX0 - 1, 1)
            for h in range(2):
                expert_out(EX0 - 2 + h, h, False, 16 * (EX0 // 2 - 1))
            for n in range(1, 3 * NT, 2):
                t, q = n // 3, n % 3
                w_ = min(4 * P, NP - 4 * P * q)
                act.wait_ge(S["tr"], n + 1)
                nc.scalar.copy(adj[0:cols(t), t, 4 * P * q:4 * P * q + w_], ps[2 + n % 4][0:cols(t), 0:w_]).then_inc(S["tr_outa"], 1)
            root(0, NT)
            for t in range(NT):
                act.wait_ge(S["tp3"], t + 1)
                nc.scalar.copy(xT3[:, :, t * P:t * P + rows(t)], ps[t % 2][:].rearrange("p (k n) -> p k n", k=NF)[:, :, 0:rows(t)]).then_inc(S["tp3_out"], 1)
            root(0, TT1)
            for t in range(TT1):
                act.wait_ge(S["tp4"], t + 1)
                nc.scalar.copy(xT4[:, :, t * P:(t + 1) * P], ps[6 + t % 2][:].rearrange("p (k n) -> p k n", k=NF)).then_inc(S["tp4_out"], 1)
            for e in range(EX1):
                act.wait_ge(S["up1"], e + 1)
                if e >= 2:
                    act.wait_ge(S["down1"], TT1 * (e - 1))
                for k in range(2):
                    ins = nc.scalar.activation(hT1[:, e % 2, k, :], ps[(e % 2) * 2 + k][:], ACT.Gelu)
                ins.then_inc(S["gelu"], 1)

        @block.tensor
        def _(pe):
            MM = nc.tensor.matmul
            pe.wait_ge(S["base_mm"], 1)
            for t in range(RT):
                MM(ps[5][:, t * ROWS:(t + 1) * ROWS], minb[:, t, :], ident[0:ROWS, 0:ROWS], start=True, stop=True)
            for t in range(RT):
                ins = MM(ps[4][:, t * ROWS:(t + 1) * ROWS], maxb[:, t, :], ident[0:ROWS, 0:ROWS], start=True, stop=True)
            ins.then_inc(S["base_mm"], 1)
            pe.wait_ge(S["onet_ready"], 2)
            with pe.Fori(0, QCH // CSTEP) as i:
                pe.wait_ge(S["coef_out"], i + 1)
                for j in range(CSTEP):
                    for s in range(PARTS):
                        ins = MM(ps[7][:, j * 32:(j + 1) * 32], onet[:, ds((i * CSTEP + j) * P, P)],
                                 wbd[:, s].rearrange("p q b -> p (q b)"), start=s == 0, stop=s == PARTS - 1)
                ins.then_inc(S["coef_mm"], 1)
            pe.sem_inc(S["mm_done"], BCH)
            rounds = window_rounds(pe, 0)
            with pe.Fori(0, rounds) as r:
                with pe.Fori(0, NB // 2) as i:
                    for h in range(2):
                        n = r * NB + i * 2 + h
                        pe.wait_ge(S["c_ready"], n + r + 1)
                        for j in range(BCH):
                            pe.wait_ge(g[j], n * 16 + 16)
                            pe.wait_ge(S["acc_done"], n * BCH + j + 1)
                            for f in range(NF):
                                for s in range(PARTS):
                                    for c in range(PARTS - s):
                                        ins = MM(ps[j][:, f * 64:(f + 1) * 64], xg[:, j, s, f * P:(f + 1) * P],
                                                 cb[:, h, c, j].rearrange("p b w -> p (b w)"),
                                                 start=s + c == 0, stop=s == PARTS - 1)
                            ins.then_inc(S["mm_done"], 1)

            def transpose_tile(t):
                r_ = rows(t)
                pe.wait_ge(S["tile_ready"], t + 1)
                if t < 2:
                    pe.wait_ge(S["xt_used"], 3 + t)
                else:
                    pe.wait_ge(S["tp_out"], t - 1)
                for k in range(NF):
                    ins = nc.tensor.transpose(ps[2 + t % 2][:, k * P:k * P + r_], xn[0:r_, t % 2, k * P:(k + 1) * P], ident[0:r_, 0:r_])
                ins.then_inc(S["tp"], 1)

            def logits(t):
                pe.wait_ge(S["tp_out"], t + 1)
                if t == 0:
                    pe.wait_ge(S["xt_used"], HALF)
                    pe.wait_ge(S["gate_in"], 16)
                for k in range(NF):
                    ins = MM(ps[4][:, t * EX0:(t + 1) * EX0], xT[:, t % 2, k, :], wg[:, k, :], start=k == 0, stop=k == NF - 1)
                ins.then_inc(S["logits"], 1)

            pe.wait_ge(S["agg_done"], 1)
            for half in range(2):
                for b in range(NBASE):
                    n = half * NBASE + b
                    pe.wait_ge(S[f"base_in{n % 2}"], 16 * (n // 2 + 1))
                    for t in range(HALF * half, HALF * half + HALF):
                        if b == 0 and t >= 8:
                            pe.wait_ge(S["xt_used"], t - 8 + 1)
                        for k in range(NF):
                            ins = MM(ps[t % 8][0:cols(t), :], agg[:, k, b, t * P:t * P + cols(t)], bring[:, n % 2, k, :],
                                     start=b == 0 and k == 0, stop=b == NBASE - 1 and k == NF - 1, skip_group_check=True)
                        if b == NBASE - 1:
                            ins.then_inc(S["tile_mm"], 1)
                        elif t == HALF * half + HALF - 1:
                            ins.then_inc(S["basis_mm"], 1)
                    if half and 1 <= b <= HALF:
                        transpose_tile(b - 1)
                    if half and 2 <= b <= HALF + 1:
                        logits(b - 2)
                    if b == NBASE - 1:
                        pe.drain().then_inc(S["basis_mm"], 1)
            for t in range(HALF, NT):
                transpose_tile(t)
                logits(t)
            for k in range(3):
                pe.wait_ge(S["mask_ready"], k + 1)
                mask = mb.rearrange("p t e -> p (t e)")
                if k != 1:
                    MM(ps[3][:, 0:NT * EX0], tri[:], mask, start=True, stop=True)
                MM(ps[4][:, 0:NT * EX0], ones[:], mask, start=True, stop=True).then_inc(S["places"], 1)

            def counts(b, h, r=0):
                pe.wait_ge(S["n_c"], b + r + 1)
                for q in range(NGRP):
                    pe.wait_ge(S["n_acc"], b * NGRP + q + 1)
                    for j in range(GRP):
                        ins = MM(ps[1 + 3 * q][:, 0:160], rside[:, h, q * GRP + j, :],
                                 lside[:, h, q * GRP + j].rearrange("p u w -> p (u w)"), start=j == 0, stop=j == GRP - 1)
                    ins.then_inc(S["n_mm"], 1)

            with pe.Fori(0, N_AHEAD // 2) as i:
                for h in range(2):
                    counts(i * 2 + h, h)

            def slot_tile(e, h, s, gathered):
                pe.wait_ge(gx[h * 3 + s], gathered)
                pe.wait_ge(S["xe_out"], e * 3 + s)
                for k in range(NF):
                    ins = nc.tensor.transpose(ps[0][:, k * ST:(k + 1) * ST], xer[:, h * 3 + s, k * P:(k + 1) * P], ident[0:ST, 0:ST])
                ins.then_inc(S["xe_tp"], 1)

            def up(e, h, loaded, relued):
                pe.wait_ge(S[f"w1_in{h}"], loaded)
                pe.wait_ge(S["xe_out"], e * 3 + 3)
                if relued is not None:
                    pe.wait_ge(S["relu"], relued)
                for k in range(2):
                    for f in range(NF):
                        ins = MM(ps[2 + k][:, 0:CAP], w1r[h][:, f, k * P:(k + 1) * P], xe[:, h, f, :], start=f == 0, stop=f == NF - 1)
                ins.then_inc(S["up"], 1)

            def down(e, h, loaded, ahead, first):
                pe.wait_ge(S[f"w2_in{h}"], loaded)
                pe.wait_ge(S["relu"], e + 1)
                for s in range(3):
                    if not (first and s < 2):
                        pe.wait_ge(S["y_out"], e * 3 + s - 1)
                    for k in range(2):
                        ins = MM(ps[6 + (h + s) % 2][0:ST, :], hT[:, h, k, s * ST:(s + 1) * ST], w2r[h][:, k, :], start=k == 0, stop=k == 1)
                    ins.then_inc(S["down"], 1)
                    if ahead:
                        slot_tile(e + 2, h, s, loaded + 16)

            pe.wait_ge(S["slots_ready"], 1)
            for h in range(2):
                for s in range(3):
                    pe.wait_ge(gx[h * 3 + s], 16)
                    if h or s:
                        pe.wait_ge(S["xe_out"], h * 3 + s)
                    for k in range(NF):
                        ins = nc.tensor.transpose(ps[0][:, k * ST:(k + 1) * ST], xer[:, h * 3 + s, k * P:(k + 1) * P], ident[0:ST, 0:ST])
                    ins.then_inc(S["xe_tp"], 1)
                if h == 0:
                    up(0, 0, 16, None)
            up(1, 1, 16, 1)
            down(0, 0, 16, True, True)
            for k in range(N_PER):
                counts(N_AHEAD + k, k % 2)
            up(2, 0, 32, 2)
            down(1, 1, 16, True, False)
            for k in range(N_PER):
                counts(N_AHEAD + N_PER + k, (N_PER + k) % 2)
            with pe.Fori(1, EX0 // 2 - 1) as i:
                for h in range(2):
                    e = i * 2 + h
                    up(e + 1, 1 - h, i * 16 + 16 + 16 * h, e + 1)
                    down(e, h, i * 16 + 16, True, False)
                    for k in range(N_PER):
                        counts(e * N_PER + N_AHEAD + k, (h * N_PER + k) % 2)
            up(EX0 - 1, 1, 16 * (EX0 // 2), EX0 - 1)
            for h in range(2):
                down(EX0 - 2 + h, h, 16 * (EX0 // 2), False, False)
            rounds = window_rounds(pe, 1)
            with pe.If(rounds > 1):
                with pe.Fori(1, rounds) as r:
                    with pe.Fori(0, NB // 2) as i:
                        for h in range(2):
                            counts(r * NB + i * 2 + h, h, r)
            pe.end_ifs()
            pe.wait_ge(S["n_ready"], 1)
            pe.wait_ge(S["y_out"], 3 * EX0)
            for n in range(3 * NT):
                t, q = n // 3, n % 3
                if n >= 4:
                    pe.wait_ge(S["tr_outa"] if n % 2 else S["tr_outv"], (n - 4) // 2 + 1)
                for u in range(4 * q, min(4 * q + 4, UH)):
                    ins = nc.tensor.transpose(ps[2 + n % 4][0:cols(t), (u % 4) * P:(u % 4 + 1) * P], nT[:, u, t * P:t * P + cols(t)], ident[:])
                ins.then_inc(S["tr"], 1)
            pe.wait_ge(S["xh3_ready"], 1)
            pe.wait_ge(S["tr_outa"], 3 * NT // 2)
            pe.wait_ge(S["tr_outv"], 3 * NT // 2)
            for t in range(NT):
                if t >= 2:
                    pe.wait_ge(S["tp3_out"], t - 1)
                for k in range(NF):
                    ins = nc.tensor.transpose(ps[t % 2][:, k * P:k * P + rows(t)], xh3[0:rows(t), t, k * P:(k + 1) * P], ident[0:rows(t), 0:rows(t)])
                ins.then_inc(S["tp3"], 1)
            for k in range(NF):
                for q in range(3):
                    n = 3 * k + q
                    w_ = min(512, NP - 512 * q)
                    if n >= 3:
                        pe.wait_ge(S["sums_out"], n - 2)
                    for t in range(NT):
                        ins = MM(ps[2 + n % 3][:, 0:w_], xh3[0:rows(t), t, k * P:(k + 1) * P], adj[0:rows(t), t, 512 * q:512 * q + w_], start=t == 0, stop=t == NT - 1)
                    ins.then_inc(S["sums"], 1)
            pe.wait_ge(S["tp3_out"], NT)
            pe.wait_ge(S["sums_out"], 3 * NF)
            pe.wait_ge(S["wcn_in"], 32)
            for t in range(NT):
                pa, pb = ps[2 * (t % 3)], ps[1 + 2 * (t % 3)]
                if t >= 3:
                    pe.wait_ge(S["g_out"], t - 2)
                for dst, left, right in ((pa, xT3, wcs), (pb, sT, wns)):
                    for k in range(NF):
                        ins = MM(dst[0:rows(t), :], left[:, k, t * P:t * P + rows(t)], right[:, k, :], start=k == 0, stop=k == NF - 1)
                ins.then_inc(S["gm"], 1)
            pe.wait_ge(S["x4_ready"], 1)
            for t in range(TT1):
                if t >= 2:
                    pe.wait_ge(S["tp4_out"], t - 1)
                for k in range(NF):
                    ins = nc.tensor.transpose(ps[6 + t % 2][:, k * P:(k + 1) * P], xh4[:, t, k * P:(k + 1) * P], ident[:])
                ins.then_inc(S["tp4"], 1)
            pe.wait_ge(S["tp4_out"], TT1)
            pe.wait_ge(S["g_out"], NT)

            def up1(e):
                pe.wait_ge(S[f"w1_in{e % 2}"], 16 * (EX0 // 2 + e // 2 + 1))
                if e >= 2:
                    pe.wait_ge(S["gelu"], e - 1)
                for k in range(2):
                    for f in range(NF):
                        ins = MM(ps[(e % 2) * 2 + k][:], w1s[e % 2][:, f, k * P:(k + 1) * P], xT4[:, f, :], start=f == 0, stop=f == NF - 1)
                ins.then_inc(S["up1"], 1)

            up1(0)
            for e in range(EX1):
                if e + 1 < EX1:
                    up1(e + 1)
                pe.wait_ge(S[f"w2_in{e % 2}"], 16 * (EX0 // 2 + e // 2 + 1))
                pe.wait_ge(S["gelu"], e + 1)
                for t in range(TT1):
                    if e:
                        pe.wait_ge(S["y1_used"], TT1 * (e - 1) + t + 1)
                    for k in range(2):
                        ins = MM(ps[4 + t][:], hT1[:, e % 2, k, t * P:(t + 1) * P], w2s[e % 2][:, k, :], start=k == 0, stop=k == 1)
                    ins.then_inc(S["down1"], 1)

        @block.vector
        def _(dve):
            V = nc.vector
            chain = [0]

            def link(ins):
                chain[0] += 1
                ins.then_inc(S["dve"], 1)
                dve.wait_ge(S["dve"], chain[0])

            roots = [0]

            def moments(t, src):
                link(V.bn_stats(stats[0:rows(t), :], src))
                link(V.bn_aggr(mv[0:rows(t), t, :], stats[0:rows(t), :]))

            def inverse_std(a, b):
                roots[0] += 1
                V.engine_nop().then_inc(S["std_req"], 1)
                dve.wait_ge(S["std_done"], roots[0])
                link(V.reciprocal(rstd[:, a:b], std[:, a:b]))

            def normalize(t, dst, src):
                return V.tensor_scalar(dst, src, mv[0:rows(t), t, 0:1], rstd[0:rows(t), t:t + 1], ALU.subtract, ALU.mult)

            link(V.memset(eps[:], EPS))
            link(V.memset(ones[:], 1.0))
            link(V.memset(mv[:], 0.0))
            dve.wait_ge(S["consts"], 3)
            link(V.tensor_copy(iota[:], iota_i[:]))
            link(V.tensor_single_scalar(part_i[:, 1:2], part_i[:, 0:1], NREL - 1, ALU.bitwise_and))
            link(V.tensor_single_scalar(part_i[:, 2:3], part_i[:, 0:1], 5, ALU.logical_shift_right))
            V.tensor_copy(part[:], part_i[:]).then_inc(S["onet_ready"], 1)
            dve.wait_ge(S["onet_ready"], 1)
            link(V.tensor_scalar(ident[:], iota[:], part[:, 0:1], None, ALU.is_equal))
            link(V.tensor_scalar(tri[:], iota[:], part[:, 0:1], None, ALU.is_gt))
            link(V.tensor_scalar(qmask[:], iota[:, 0:4], part[:, 2:3], None, ALU.is_equal))
            dve.wait_ge(S["w_in"], 64)
            link(V.tensor_copy(wpart[:, 0, :], wc4[:]))
            link(V.tensor_tensor(wc4[:], wc4[:], wpart[:, 0, :], ALU.subtract))
            link(V.tensor_copy(wpart[:, 1, :], wc4[:]))
            link(V.tensor_tensor(wc4[:], wc4[:], wpart[:, 1, :], ALU.subtract))
            link(V.tensor_copy(wpart[:, 2, :], wc4[:]))
            for k in range(PARTS):
                link(V.tensor_tensor(wbd[:, k], wpart[:, k, :].unsqueeze(1).to_broadcast([P, 4, NBASE]),
                                     qmask[:].unsqueeze(2).to_broadcast([P, 4, NBASE]), ALU.mult))
            dve.wait_ge(S["x_in"], 32)
            for t in range(NT):
                moments(t, xin[0:rows(t), t, :])
            inverse_std(0, NT)
            for t in range(NT):
                normalize(t, xh[0:rows(t), t], xin[0:rows(t), t]).then_inc(S["norm_ready"], 1)
            for t in range(NT):
                dve.wait_ge(S["split_h"], t + 1)
                V.tensor_tensor(xh[0:rows(t), t], xh[0:rows(t), t], xs[0:rows(t), t, 0], ALU.subtract).then_inc(S["split_r"], 1)
            for t in range(NT):
                dve.wait_ge(S["split_m"], t + 1)
                ins = V.tensor_tensor(xs[0:rows(t), t, 2], xh[0:rows(t), t], xs[0:rows(t), t, 1], ALU.subtract)
            ins.then_inc(S["xs_ready"], 1)
            dve.wait_ge(S["etype_in"], 64)
            V.tensor_scalar(onet[:], etb[:], part[:, 1:2], None, ALU.is_equal).then_inc(S["onet_ready"], 1)
            dve.wait_ge(S["rows_in"], 16)
            link(V.tensor_copy(dstr[0:ROWS], dstr_i[0:ROWS]))
            link(V.scalar_tensor_tensor(out=dstm[0:ROWS], in0=dstr[0:ROWS], scalar=float(N), in1=dstr[0:ROWS], op0=ALU.is_lt, op1=ALU.mult))
            link(V.tensor_reduce(mins[:, 0, :], dstr[0:ROWS], AX.X, ALU.min))
            link(V.tensor_reduce(mins[:, 1, :], dstm[0:ROWS], AX.X, ALU.max))
            link(V.tensor_copy(minb[:, :, :], mins[:, 0, :].unsqueeze(2).to_broadcast([ROWS, RT, P])))
            V.tensor_copy(maxb[:, :, :], mins[:, 1, :].unsqueeze(2).to_broadcast([ROWS, RT, P])).then_inc(S["base_mm"], 1)
            dve.sem_inc(S["coef_out"], 1)
            dve.wait_ge(S["edges_in"], 48)
            link(V.memset(coef[:, :, NCH:TCOL, :], 0.0))
            link(V.memset(basef[:, NCH:TCOL], 0.0))
            link(V.tensor_copy(dstf[:], dst_i[:]))
            cq = coeff[:, :, :].rearrange("p (q c) b -> p q c b", q=4)
            wq = wgt[:, 0:NCH].rearrange("p (q c) -> p q c", q=4)
            pc = ps[7][:, 0:CSTEP * 32].rearrange("p (c q b) -> p q c b", q=4, b=NBASE)
            with dve.Fori(0, QCH // CSTEP) as i:
                dve.wait_ge(S["coef_mm"], i + 1)
                V.tensor_tensor(cq[:, :, ds(i * CSTEP, CSTEP), :], pc,
                                wq[:, :, ds(i * CSTEP, CSTEP)].unsqueeze(3).to_broadcast([P, 4, CSTEP, NBASE]), ALU.mult).then_inc(S["coef_out"], 1)
            dve.wait_ge(S["base_mm"], 2)
            link(V.tensor_copy(basef[:, 0:NCH], ps[5][:, 0:NCH]))
            link(V.tensor_reduce(base3[:], basef[:, 0:NCH].rearrange("p (g c) -> p g c", c=GRP), AX.X, ALU.min))
            link(V.tensor_reduce(top3[:], ps[4][:, 0:NCH].rearrange("p (g c) -> p g c", c=GRP), AX.X, ALU.max))
            link(V.tensor_tensor(top3[:], top3[:], base3[:], ALU.subtract))
            link(V.tensor_reduce(gap[:, 1:2], top3[:], AX.X, ALU.max))
            link(V.tensor_tensor(gaps[:], ps[4][:, 0:NCH], basef[:, 0:NCH], ALU.subtract))
            link(V.tensor_reduce(gap[:, 0:1], gaps[:], AX.X, ALU.max))
            link(V.tensor_copy(gap_i[:], gap[:]))
            link(V.tensor_single_scalar(gap_i[:, 0:1], gap_i[:, 0:1], 3, ALU.logical_shift_right))
            link(V.tensor_single_scalar(gap_i[:, 1:2], gap_i[:, 1:2], 4, ALU.logical_shift_right))
            link(V.tensor_copy(gap[:], gap_i[:]))
            V.tensor_scalar(rounds_i[:], gap[0:1, :], 1.0, None, ALU.add).then_inc(S["rounds_ready"], 1)
            dve.wait_ge(S["coef_h"], 1)
            V.tensor_tensor(coeff[:, :], coeff[:, :], coef[:, 0, 0:NCH], ALU.subtract).then_inc(S["coef_r"], 1)
            dve.wait_ge(S["coef_m"], 1)
            V.tensor_tensor(coef[:, 2, 0:NCH], coeff[:, :], coef[:, 1, 0:NCH], ALU.subtract).then_inc(S["coef_r"], 1)
            dve.wait_ge(S["coef_r"], 2)
            dve.wait_ge(S["xs_out"], 32)
            V.memset(big[:, ZCUT[0]:ZCUT[1]], 0.0).then_inc(S["agg_zero"], 1)
            dve.sem_inc(S["acc_done"], BCH)
            rounds = window_rounds(dve, 0)
            io8 = iota[:, 0:WIN].unsqueeze(1).to_broadcast([P, BCH, WIN])

            def columns(table, at, n, top):
                return nc.values_load_multi_w_load_instructions(
                    table[0:1, ds(at, n)], engines=(mybir.EngineType.DVE,), min_val=0, max_val=top,
                    skip_runtime_bounds_check_because="the table is clamped to the accumulators")[1]

            def build_c(b, h, n):
                V.tensor_tensor(oh[:, h], rel[:, ds(b * BCH, BCH)].unsqueeze(2).to_broadcast([P, BCH, WIN]), io8, ALU.is_equal).then_inc(S["oh_done"], 1)
                dve.wait_ge(S["oh_done"], n + 1)
                for s in range(PARTS):
                    ins = V.tensor_tensor(cb[:, h, s], oh[:, h].unsqueeze(2).to_broadcast([P, BCH, NBASE, WIN]),
                                          coef[:, s, ds(b * BCH, BCH), :].unsqueeze(3).to_broadcast([P, BCH, NBASE, WIN]), ALU.mult)
                ins.then_inc(S["c_ready"], 1)

            with dve.Fori(0, rounds) as r:
                V.tensor_tensor(rel[:], dstf[:], basef[:], ALU.subtract).then_inc(S["round_ready"], 1)
                V.tensor_scalar(basei[:].rearrange("o (b j) -> o b j", j=PITCH)[:, :, 0:BCH], basef[0:1, 0:NCH].rearrange("o (b j) -> o b j", j=BCH),
                                float(W - WIN), None, ALU.min).then_inc(S["round_ready"], 1)
                dve.wait_ge(S["round_ready"], r * 3 + 2)
                V.tensor_scalar(basef[:], basef[:], float(WIN), None, ALU.add).then_inc(S["round_ready"], 1)
                dve.wait_ge(S["round_ready"], r * 3 + 3)
                build_c(0, 0, r * (NB + 1))
                dve.wait_ge(S["agg_zero"], 4)
                with dve.Fori(0, NB // 2) as i:
                    for h in range(2):
                        b = i * 2 + h
                        n = r * NB + b
                        build_c(b + 1, 1 - h, n + r + 1)
                        col = columns(basei, b * PITCH, BCH, W - WIN)
                        for j in range(BCH):
                            dve.wait_ge(S["mm_done"], n * BCH + j + 1 + BCH)
                            dve.wait_ge(S["acc_done"], n * BCH + j + BCH)
                            a = aggw[:, :, ds(col[j], WIN)]
                            V.tensor_tensor(a, ps[j][:, 0:256].rearrange("p (fb w) -> p fb w", w=WIN), a, ALU.add).then_inc(S["acc_done"], 1)
            dve.drain().then_inc(S["agg_done"], 1)
            dve.wait_ge(S["hb_in"], 16)
            for t in range(NT):
                r_ = rows(t)
                dve.wait_ge(S["xt_in"], 16 * (t + 1))
                link(V.tensor_tensor(xt[0:r_, :], xt[0:r_, :], hb[0:r_, :], ALU.add))
                dve.wait_ge(S["tile_mm"], t + 1)
                if t:
                    dve.wait_ge(S[f"tile_out{(t - 1) % 2}"], 32 * ((t - 1) // 2 + 1))
                V.tensor_tensor(xo[0:r_, :], ps[t % 8][0:r_, :], xt[0:r_, :], ALU.add).then_inc(S["xt_used"], 1)
                dve.wait_ge(S["xt_used"], t + 1)
                moments(t, xo[0:r_, :])
                inverse_std(t, t + 1)
                if t >= 2:
                    dve.wait_ge(S["tp"], t - 1)
                normalize(t, xn[0:r_, t % 2, :], xo[0:r_, :]).then_inc(S["tile_ready"], 1)
            usrc = ulo[:].bitcast(i32)
            hsrc = uhi[:].bitcast(i32)
            relf = reln[:, 0:NCH].rearrange("p (g c) -> p g c", c=GRP)
            link(V.memset(reln[:, NCH:TCOL], 0.0))
            link(V.tensor_tensor(relf, dstf[:, 0:NCH].rearrange("p (g c) -> p g c", c=GRP), base3[:].unsqueeze(2).to_broadcast([P, NCH // GRP, GRP]), ALU.subtract))
            link(V.tensor_single_scalar(usrc, src_i[:], P - 1, ALU.bitwise_and))
            link(V.tensor_single_scalar(hsrc, src_i[:], 7, ALU.logical_shift_right))
            link(V.tensor_copy(ulo[:], usrc))
            link(V.tensor_copy(uhi[:], hsrc))

            def G(k):
                return g_[:, k]

            def sm(k):
                return s_[:, k, :]

            def bc(a):
                return a.unsqueeze(2).to_broadcast([P, NT, EX0])

            dve.wait_ge(S["logits"], NT)
            lg = ps[4][:, 0:NT * EX0].rearrange("p (t e) -> p t e", e=EX0)
            link(V.tensor_reduce(sm(0), lg, AX.X, ALU.max))
            V.tensor_tensor(G(1), lg, bc(sm(0)), ALU.subtract).then_inc(S["exp_req"], 1)
            link(V.tensor_scalar(G(3), iota[:, 0:EX0].unsqueeze(1).to_broadcast([P, NT, EX0]), -1.0, float(EX0), ALU.mult, ALU.add))
            link(V.tensor_scalar(sm(15), iota[:, 0:NT], float(P), part[:, 0:1], ALU.mult, ALU.add))
            link(V.tensor_scalar(sm(15), sm(15), float(N), None, ALU.is_lt))
            dve.wait_ge(S["exp_done"], 1)
            link(V.tensor_reduce(sm(1), G(0), AX.X, ALU.add))
            link(V.reciprocal(sm(2), sm(1)))
            link(V.tensor_tensor(G(2), G(0), bc(sm(2)), ALU.mult))

            def first_max(gates, top, best, mask):
                link(V.tensor_reduce(top, gates, AX.X, ALU.max))
                link(V.tensor_tensor(G(5), gates, bc(top), ALU.is_equal))
                link(V.tensor_tensor(G(5), G(5), G(3), ALU.mult))
                link(V.tensor_reduce(best, G(5), AX.X, ALU.max))
                link(V.tensor_tensor(mask, G(3), bc(best), ALU.is_equal))

            def with_places(mask, pos, given):
                V.memset(pref[:, 0, :], 0.0)
                V.tensor_copy(pref[:, 1, :], ps[4][:, 0:EX0])
                link(V.tensor_copy(G(11), ps[4][:, 0:NT * EX0].rearrange("p (t e) -> p t e", e=EX0)))
                for t in range(2, NT):
                    link(V.tensor_tensor(pref[:, t, :], pref[:, t - 1, :], G(11)[:, t - 1, :], ALU.add))
                if given is not None:
                    link(V.tensor_tensor(pref[:], pref[:], given.unsqueeze(1).to_broadcast([P, NT, EX0]), ALU.add))
                link(V.tensor_tensor(pos, ps[3][:, 0:NT * EX0].rearrange("p (t e) -> p t e", e=EX0), pref[:], ALU.add))
                link(V.tensor_tensor(pos, pos, mask, ALU.mult))
                link(V.scalar_tensor_tensor(out=mask, in0=pos, scalar=float(CAP), in1=mask, op0=ALU.is_lt, op1=ALU.mult))

            first_max(G(2), sm(3), sm(5), G(4))
            link(V.tensor_tensor(G(10), G(4), bc(sm(15)), ALU.mult))
            V.tensor_copy(mb[:], G(10)).then_inc(S["mask_ready"], 1)
            link(V.tensor_scalar(G(5), G(4), -1.0, 1.0, ALU.mult, ALU.add))
            link(V.tensor_tensor(G(6), G(2), G(5), ALU.mult))
            first_max(G(6), sm(4), sm(6), G(7))
            link(V.tensor_tensor(sm(7), sm(3), sm(4), ALU.add))
            link(V.tensor_scalar(sm(7), sm(7), 1e-9, None, ALU.add))
            link(V.reciprocal(sm(7), sm(7)))
            link(V.tensor_tensor(sm(3), sm(3), sm(7), ALU.mult))
            link(V.tensor_tensor(sm(4), sm(4), sm(7), ALU.mult))
            link(V.tensor_tensor(G(7), G(7), bc(sm(15)), ALU.mult))
            dve.wait_ge(S["places"], 1)
            with_places(G(10), G(8), None)
            V.tensor_copy(mb[:], G(10)).then_inc(S["mask_ready"], 1)
            link(V.tensor_reduce(sm(8), G(8), AX.X, ALU.add))
            link(V.tensor_reduce(sm(9), G(10), AX.X, ALU.add))
            dve.wait_ge(S["places"], 2)
            link(V.tensor_reduce(G(9)[:, 0, :], ps[4][:, 0:NT * EX0].rearrange("p (t e) -> p e t", e=EX0), AX.X, ALU.add))
            V.tensor_copy(mb[:], G(7)).then_inc(S["mask_ready"], 1)
            dve.wait_ge(S["places"], 3)
            with_places(G(7), G(8), G(9)[:, 0, :])
            link(V.tensor_reduce(sm(10), G(8), AX.X, ALU.add))
            link(V.tensor_reduce(sm(11), G(7), AX.X, ALU.add))
            for k, (gate, best, pos, kept) in enumerate(((3, 5, 8, 9), (4, 6, 10, 11))):
                link(V.tensor_tensor(sm(gate), sm(gate), sm(kept), ALU.mult))
                link(V.tensor_scalar(sm(best), sm(best), -1.0, float(EX0), ALU.mult, ALU.add))
                link(V.tensor_scalar(sm(12), sm(pos), float(ST), None, ALU.is_ge))
                link(V.tensor_scalar(sm(13), sm(pos), float(2 * ST), None, ALU.is_ge))
                link(V.tensor_tensor(sm(12), sm(12), sm(13), ALU.add))
                link(V.tensor_scalar(sm(13), sm(pos), float(3 * EX0), None, ALU.mult))
                link(V.scalar_tensor_tensor(out=sm(13), in0=sm(12), scalar=1.0 - 3.0 * EX0 * ST, in1=sm(13), op0=ALU.mult, op1=ALU.add))
                link(V.scalar_tensor_tensor(out=sm(13), in0=sm(best), scalar=3.0, in1=sm(13), op0=ALU.mult, op1=ALU.add))
                link(V.tensor_tensor(sm(13), sm(13), sm(kept), ALU.mult))
                link(V.tensor_scalar(sm(14), sm(kept), -NOSLOT, NOSLOT, ALU.mult, ALU.add))
                link(V.tensor_tensor(slot_i[:, k, :], sm(13), sm(14), ALU.add))
                link(V.scalar_tensor_tensor(out=sm(12), in0=sm(best), scalar=float(CAP), in1=sm(pos), op0=ALU.mult, op1=ALU.add))
                link(V.tensor_tensor(slot_i[:, 2 + k, :], sm(12), sm(kept), ALU.mult))
            V.engine_nop().then_inc(S["slots_ready"], 1)

            ioP = iota[:].unsqueeze(1).to_broadcast([P, BCH, P])
            ioU = iota[:, 0:UH].unsqueeze(1).to_broadcast([P, BCH, UH])
            ioW = iota[:, 0:WINN].unsqueeze(1).to_broadcast([P, BCH, WINN])

            def build_n(b, h, n):
                at = ds(b * BCH, BCH)
                V.tensor_tensor(ohw[:, h], reln[:, at].unsqueeze(2).to_broadcast([P, BCH, WINN]), ioW, ALU.is_equal)
                V.tensor_tensor(ohu[:, h], uhi[:, at].unsqueeze(2).to_broadcast([P, BCH, UH]), ioU, ALU.is_equal).then_inc(S["n_oh"], 1)
                V.tensor_tensor(rside[:, h], ulo[:, at].unsqueeze(2).to_broadcast([P, BCH, P]), ioP, ALU.is_equal)
                dve.wait_ge(S["n_oh"], n + 1)
                V.tensor_tensor(lside[:, h], ohw[:, h].unsqueeze(2).to_broadcast([P, BCH, UH, WINN]),
                                ohu[:, h].unsqueeze(3).to_broadcast([P, BCH, UH, WINN]), ALU.mult).then_inc(S["n_c"], 1)

            def count_round(r):
                table = base3i.rearrange("o (b j) -> o b j", j=NPITCH)[:, :, 0:NGRP]
                V.tensor_scalar(table, base3[0:1, :].rearrange("o (b j) -> o b j", j=NGRP), float(W - WINN), None, ALU.min).then_inc(S["n_round"], 1)
                dve.wait_ge(S["n_round"], r + 1)
                build_n(0, 0, r * (NB + 1))
                with dve.Fori(0, NB // 2) as i:
                    for h in range(2):
                        b = i * 2 + h
                        n = r * NB + b
                        build_n(b + 1, 1 - h, n + r + 1)
                        col = columns(base3i, b * NPITCH, NGRP, W - WINN)
                        for q in range(NGRP):
                            dve.wait_ge(S["n_mm"], n * NGRP + q + 1)
                            dve.wait_ge(S["n_acc"], n * NGRP + q + NGRP)
                            a = nT[:, :, ds(col[q], WINN)]
                            V.tensor_tensor(a, ps[1 + 3 * q][:, 0:160].rearrange("p (u w) -> p u w", w=WINN), a, ALU.add).then_inc(S["n_acc"], 1)

            dve.sem_inc(S["n_acc"], NGRP)
            dve.wait_ge(S["n_zero"], 1)
            count_round(0)
            rounds = window_rounds(dve, 1)
            S["n_next"] = sem("count_distances_ready")
            with dve.If(rounds > 1):
                with dve.Fori(1, rounds) as r:
                    V.tensor_scalar(reln[:], reln[:], -float(WINN), None, ALU.add).then_inc(S["n_next"], 1)
                    V.tensor_scalar(base3[:], base3[:], float(WINN), None, ALU.add).then_inc(S["n_next"], 1)
                    dve.wait_ge(S["n_next"], r * 2)
                    count_round(r)
            dve.end_ifs()
            dve.drain().then_inc(S["n_ready"], 1)
            link(V.tensor_reduce(cnt[:], nT[:, :, 0:N], AX.X, ALU.add))
            link(V.reciprocal(rcnt[:], cnt[:]))
            for n in range(0, 3 * NT, 2):
                t, q = n // 3, n % 3
                w_ = min(4 * P, NP - 4 * P * q)
                dve.wait_ge(S["tr"], n + 1)
                V.tensor_copy(adj[0:cols(t), t, 4 * P * q:4 * P * q + w_], ps[2 + n % 4][0:cols(t), 0:w_]).then_inc(S["tr_outv"], 1)
            dve.wait_ge(S["x1_in"], 32)
            for t in range(NT):
                r_ = rows(t)
                for k in range(2):
                    n = 2 * t + k
                    dve.wait_ge(gy[n % 6], 16 * (n // 6 + 1))
                    V.scalar_tensor_tensor(out=x1[0:r_, t, :], in0=y2[0:r_, n % 6, :], scalar=s_[0:r_, 3 + k, t:t + 1], in1=x1[0:r_, t, :],
                                           op0=ALU.mult, op1=ALU.add).then_inc(S["y2_used"], 1)
                    dve.wait_ge(S["y2_used"], n + 1)
                moments(t, x1[0:r_, t, :])
            inverse_std(0, NT)
            for t in range(NT):
                ins = normalize(t, xh3[0:rows(t), t, :], x1[0:rows(t), t, :])
            ins.then_inc(S["xh3_ready"], 1)
            for k in range(NF):
                for q in range(3):
                    n = 3 * k + q
                    w_ = min(512, NP - 512 * q)
                    dve.wait_ge(S["sums"], n + 1)
                    V.tensor_copy(sT[:, k, 512 * q:512 * q + w_], ps[2 + n % 3][:, 0:w_]).then_inc(S["sums_out"], 1)
            dve.wait_ge(S["gbias_in"], 16)

            def graph_out(t):
                r_ = rows(t)
                x_t = x1[0:r_, t, :]
                pa, pb = ps[2 * (t % 3)], ps[1 + 2 * (t % 3)]
                link(V.tensor_tensor(x_t, x_t, gbias[0:r_, :], ALU.add))
                dve.wait_ge(S["gm"], t + 1)
                link(V.scalar_tensor_tensor(out=x_t, in0=pb[0:r_, :], scalar=rcnt[0:r_, t:t + 1], in1=x_t, op0=ALU.mult, op1=ALU.add))
                V.tensor_tensor(x_t, pa[0:r_, :], x_t, ALU.add).then_inc(S["g_out"], 1)
                dve.wait_ge(S["g_out"], t + 1)

            for t in range(TT1):
                graph_out(t)
                moments(t, x1[:, t, :])
            inverse_std(0, TT1)
            for t in range(TT1):
                ins = normalize(t, xh4[:, t, :], x1[:, t, :])
            ins.then_inc(S["x4_ready"], 1)
            for t in range(TT1, NT):
                graph_out(t)
            dve.wait_ge(S["moe_in"], 32)
            link(V.tensor_copy(ef[:], ei[:]))
            for t in range(TT1):
                for k in range(TOPK):
                    link(V.tensor_scalar(combt[:, t, k, :], iota[:, 0:EX1], ef[:, t, k:k + 1], ew[:, t, k:k + 1], ALU.is_equal, ALU.mult))
            link(V.tensor_tensor(comb[:], combt[:, :, 0, :], combt[:, :, 1, :], ALU.add))
            for e in range(EX1):
                for t in range(TT1):
                    n = TT1 * e + t
                    dve.wait_ge(S["down1"], n + 1)
                    if e:
                        dve.wait_ge(S["y1_used"], n - TT1 + 1)
                    V.scalar_tensor_tensor(out=x1[:, t, :], in0=ps[4 + t][:], scalar=comb[:, t, e:e + 1], in1=x1[:, t, :],
                                           op0=ALU.mult, op1=ALU.add).then_inc(S["y1_used"], 1)


def kernel(**inputs):
    import numpy as np
    import concourse.bacc as bacc
    from concourse.bass_utils import run_bass_kernel_spmd as run

    def padded(a, n, fill):
        flat = np.full(n * P, fill, a.dtype)
        flat[:E] = a.reshape(-1)
        return flat.reshape(n, P)

    a = {k: np.asarray(v) for k, v in inputs.items()}
    arrays = {
        "x": a["x"],
        "src_cols": np.ascontiguousarray(padded(a["src"], TCOL, 0).T),
        "dst_cols": np.ascontiguousarray(padded(a["dst"], TCOL, N).T),
        "wgt_cols": np.ascontiguousarray(padded(a["edge_weight1"], TCOL, 0).T),
        "etype": padded(a["edge_type_32"], NCH, 0).reshape(4, QCH * P),
        "dst_rows": padded(a["dst"], NCH, N),
        "bases": a["L0_gnn_bases"], "w_comp": a["L0_gnn_w_comp"], "h_bias": a["L0_gnn_h_bias"].reshape(1, F),
        "w_gating": a["L0_ffn_w_gating"], "f0_w1": a["L0_ffn_w1"], "f0_w2": a["L0_ffn_w2"],
        "wc": a["L1_gnn_wc"], "wn": a["L1_gnn_wn"], "g1_bias": a["L1_gnn_bias"].reshape(1, F),
        "x_weights": a["L1_ffn_expert_weights"], "x_indices": a["L1_ffn_expert_indices"],
        "f1_w1": a["L1_ffn_w1"], "f1_w2": a["L1_ffn_w2"],
    }
    arrays = {k: np.ascontiguousarray(v) for k, v in arrays.items()}
    nc = bacc.Bacc("TRN2", target_bir_lowering=False, num_devices=1)
    t = {k: nc.dram_tensor("in_" + k, v.shape, mybir.dt.from_np(v.dtype), kind="ExternalInput").ap() for k, v in arrays.items()}
    out = nc.dram_tensor("out", (N, F), f32, kind="ExternalOutput").ap()
    build(nc, out=out, **t)
    r = run(nc, [{"in_" + k: v for k, v in arrays.items()}], core_ids=[0])
    return r.results[0]["out"]
```

```python
import concourse.bass as bass
from concourse import mybir
from contextlib import ExitStack

P = 128
N = 1250
F = 512
NF = F // P
NT = -(-N // P)
LAST = N - (NT - 1) * P
NP = NT * P
HALF = NT // 2
E = 41250
NREL, NBASE = 32, 8
EX0, CAP, H0 = 16, 312, 256
ST = CAP // 3
SLOTS = EX0 * CAP
T1, EX1, TOPK, H1 = 512, 8, 2, 256
TT1 = T1 // P
EPS = 1e-5

BCH = 6
NB = -(-E // (P * BCH))
NCH = NB * BCH
TCOL = NCH + BCH
WIN = 8
W = -(-N // WIN) * WIN + WIN
PITCH = 8
ROWS = 108
RT = NCH // ROWS
QCH = NCH // 4
CSTEP = 9
GRP = 3
WINN = 16
NGRP = BCH // GRP
PARTS = 3
NPITCH = 4
N_AHEAD = 6
N_PER = 4
EXC = EX0 - 4
NOSLOT = 8192.0
PARTS_AT = 22880
UH = NT

f32 = mybir.dt.float32
f32r = mybir.dt.float32r
bf16 = mybir.dt.bfloat16
i32 = mybir.dt.int32
ALU = mybir.AluOpType
ACT = mybir.ActivationFunctionType
AX = mybir.AxisListType
ds = bass.ds
assert N_AHEAD + N_PER * EXC == NB and EXC % 2 == 0 and N_PER == 4 and N_AHEAD % 2 == 0
TURN = [0, 4, 8, 14, 3 * NT]
TBANK = [1, 4, 5]


def rows(t):
    return P if t < NT - 1 else LAST


def cols(t):
    return min(P, W - t * P)


def build(nc, x, src_cols, dst_cols, wgt_cols, etype, dst_rows, bases, w_comp, h_bias, w_gating, f0_w1, f0_w2,
          wc, wn, g1_bias, x_weights, x_indices, f1_w1, f1_w2, out):
    xs_d = nc.dram_tensor("xs_d", (N, PARTS * F), bf16).ap()
    x1_d = nc.dram_tensor("x1_d", (N, F), f32).ap()
    xh2_d = nc.dram_tensor("xh2_d", (N, F), f32).ap()
    xe_d = nc.dram_tensor("xe_d", (SLOTS, F), f32).ap()
    ye_d = nc.dram_tensor("ye_d", (SLOTS, F), f32).ap()

    with ExitStack() as ctx:
        def sb(name, shape, dt=f32):
            return ctx.enter_context(nc.sbuf_tensor(name, shape, dt))

        def sem(name):
            return ctx.enter_context(nc.semaphore(name))

        BIG = NF * NBASE * W
        with nc.sbuf_tensor("big", [P, BIG], f32) as big:
            pass
        sb("below_parts", [P, PARTS_AT])
        x4p = sb("x4_parts", [P, 2, NF, T1], f32r)
        h4p = sb("h4_parts", [P, 2, 2, 2, T1], f32r)
        w4p = sb("w4_parts", [P, 2, 2, 2, 1024], f32r)
        sb("behind_parts", [P, BIG - PARTS_AT - 2 * NF * T1 - 8 * T1 - 8192])
        XG = BCH * PARTS * F // 2
        mid = sb("mid", [P, XG + TCOL * PARTS * NBASE // 2])

        agg = big[:, :].rearrange("p (f b w) -> p f b w", f=NF, b=NBASE)
        aggw = big[:, :].rearrange("p (fb w) -> p fb w", w=W)
        at = [0]

        def take(n):
            at[0] += n
            return big[:, at[0] - n:at[0]]

        xin = take(NT * F).rearrange("p (t f) -> p t f", f=F)
        xh = take(NT * F).rearrange("p (t f) -> p t f", f=F)
        xs = take(PARTS * NT * F // 2).bitcast(bf16).rearrange("p (t s f) -> p t s f", s=PARTS, f=F)
        etb = take(QCH * P).bitcast(i32)
        onet = take(QCH * P // 2).bitcast(bf16)
        dstr_i = take(RT * P).bitcast(i32).rearrange("p (t e) -> p t e", e=P)
        dstr = take(RT * P).rearrange("p (t e) -> p t e", e=P)
        dstm = take(RT * P).rearrange("p (t e) -> p t e", e=P)
        minb = take(RT * P)[0:ROWS, :].rearrange("p (t e) -> p t e", e=P)
        maxb = take(RT * P)[0:ROWS, :].rearrange("p (t e) -> p t e", e=P)
        wgt = take(TCOL)
        dst_i = take(TCOL).bitcast(i32)
        iota_i = take(P).bitcast(i32)
        gaps = take(NCH)
        top3 = take(NCH // GRP)
        coeff = take(NCH * NBASE).rearrange("p (c b) -> p c b", b=NBASE)
        SETUP = at[0]
        cuts = [0, NT * F, 2 * NT * F, 2 * NT * F + PARTS * NT * F // 2]
        cuts += [cuts[-1] + QCH * P, cuts[-1] + QCH * P + QCH * P // 2, SETUP - NCH * NBASE, SETUP, NF * NBASE * W]
        zone = [big[:, cuts[k]:cuts[k + 1]] for k in range(8)]
        XH = PARTS * HALF * F // 2
        EP = QCH * P // 3
        CBANK = [7, 6, 3]

        xg = mid[:, 0:XG].bitcast(bf16).rearrange("p (j s f) -> p j s f", j=BCH, s=PARTS)
        coef = mid[:, XG:XG + TCOL * PARTS * NBASE // 2].bitcast(bf16).rearrange("p (s c b) -> p s c b", s=PARTS, b=NBASE)
        cb = sb("cb", [P, 2, PARTS, BCH, NBASE, WIN], bf16)
        oh = sb("oh", [P, 2, BCH, WIN], bf16)
        rel = sb("rel", [P, TCOL])
        basef = sb("basef", [P, TCOL])
        basei = sb("basei", [1, NB * PITCH], i32)
        src_i = sb("src_i", [P, NCH + 2 * BCH], i32)
        dstf = sb("dstf", [P, TCOL])
        idx = sb("idx", [P, 2, BCH], i32)
        rounds_i = sb("rounds_i", [1, 2], i32)
        mins = sb("mins", [ROWS, 3, RT])
        gap = sb("gap", [P, 2])
        gap_i = sb("gap_i", [P, 2], i32)
        part_i = sb("part_i", [P, 3], i32)
        iota = sb("iota", [P, P])
        part = sb("part", [P, 3])
        ident = sb("ident", [P, P])
        tri = sb("tri", [P, P], bf16)
        ones = sb("ones", [P, P], bf16)
        wc4 = sb("wc4", [P, NBASE])
        wpart = sb("wpart", [P, PARTS, NBASE], bf16)
        qmask = sb("qmask", [P, 4])
        wbd = sb("wbd", [P, PARTS, 4, NBASE], bf16)
        eps = sb("eps", [P, 1])
        one_row = sb("one_row", [1, P])
        stats = sb("stats", [P, 6])
        mv = sb("mv", [P, NT, 2])
        std = sb("std", [P, NT])
        rstd = sb("rstd", [P, NT])
        shift = sb("shift", [P, NT])

        def m(a, n):
            return mid[:, a:a + n]

        bring = m(0, 4096).rearrange("p (s k f) -> p s k f", s=2, k=NF)
        hb = m(4096, F)
        xt = m(4608, 2 * F).rearrange("p (s f) -> p s f", s=2)
        xo = m(5632, 2 * F).rearrange("p (s f) -> p s f", s=2)
        xn = m(6656, 2 * F).rearrange("p (s f) -> p s f", s=2)
        wg = m(7680, NF * EX0).rearrange("p (k e) -> p k e", e=EX0)
        zrow = m(7744, F)
        xT = cb[:].rearrange("p a s j b w -> p (a s j b w)")[:, 0:4 * F].bitcast(f32).rearrange("p (s k n) -> p s k n", s=2, k=NF)
        x1 = big[:, 0:5120].rearrange("p (t f) -> p t f", f=F)
        xer = big[0:ST, 5120:5120 + 6 * F].rearrange("p (j f) -> p j f", f=F)
        xe = big[:, 35680:35680 + 2 * NF * CAP].rearrange("p (s k c) -> p s k c", s=2, k=NF)
        gbias = big[0:1, 39936:39936 + F]
        xh2 = big[:, 22880:22880 + NT * F].rearrange("p (t f) -> p t f", f=F)
        w1r = [m(1024 * s, 1024).rearrange("p (k h) -> p k h", k=NF) for s in range(2)]
        w2r = [m(2048 + 1024 * s, 1024).rearrange("p (k f) -> p k f", k=2) for s in range(2)]
        hT = m(4096, 4 * CAP).rearrange("p (s k c) -> p s k c", s=2, k=2)
        ysb = m(5344, 6 * F)[0:ST, :].rearrange("p (s k f) -> p s k f", s=2, k=3)
        g_ = big[:, 35680:35680 + 12 * NT * EX0].rearrange("p (k t e) -> p k t e", k=12, t=NT)
        s_ = sb("small", [P, 16, NT])
        mb = big[:, 37760:37760 + NT * EX0 // 2].bitcast(bf16).rearrange("p (t e) -> p t e", e=EX0)
        pref = big[:, 37600:37600 + NT * EX0].rearrange("p (t e) -> p t e", t=NT)
        slot_i = sb("slot_i", [P, 4, NT], i32)
        lside = big[:, 8192:9152].bitcast(bf16).rearrange("p (h j u w) -> p h j u w", h=2, j=BCH, u=UH)
        rside = big[:, 9152:9920].bitcast(bf16).rearrange("p (h j u) -> p h j u", h=2, j=BCH)
        ohw = big[:, 9920:10016].bitcast(bf16).rearrange("p (h j w) -> p h j w", h=2, j=BCH)
        ohu = big[:, 10016:10076].bitcast(bf16).rearrange("p (h j u) -> p h j u", h=2, j=BCH)
        nT = big[:, 10240:10240 + UH * W].rearrange("p (u w) -> p u w", w=W)
        adj = big[:, 22880:22880 + NT * NP].rearrange("p (t u) -> p t u", u=NP)
        y2 = big[:, 35680:35680 + 6 * F].rearrange("p (j f) -> p j f", f=F)
        xh3 = big[:, 5120:10240].rearrange("p (t f) -> p t f", f=F)
        xT3 = big[:, 10240:11264].rearrange("p (s k n) -> p s k n", s=2, k=NF)
        sT = big[:, 15360:20480].rearrange("p (k n) -> p k n", n=NP)
        ulo, uhi, reln = basef, dstf, rel
        base3 = sb("base3", [P, NB * NGRP])
        base3i = basei[:, 0:NB * NPITCH]
        wcs = m(0, 2048).rearrange("p (k f) -> p k f", k=NF)
        wns = m(2048, 2048).rearrange("p (k f) -> p k f", k=NF)
        cnt = sb("cnt", [P, UH])
        rcnt = sb("rcnt", [P, UH])
        w1s = [m(4096 + 2048 * s, 1024) for s in range(2)]
        w2s = [m(5120 + 2048 * s, 1024) for s in range(2)]
        xh4 = big[:, 5120:5120 + TT1 * F].rearrange("p (t f) -> p t f", f=F)
        hT1 = big[:, 12288:12288 + 4 * T1].rearrange("p (s k n) -> p s k n", s=2, k=2)
        ei = sb("ei", [P, TT1, TOPK], i32)
        ew = sb("ew", [P, TT1, TOPK])
        ef = big[:, 11300:11300 + TT1 * TOPK].rearrange("p (t k) -> p t k", k=TOPK)
        comb = big[:, 11400:11400 + TT1 * EX1].rearrange("p (t e) -> p t e", e=EX1)
        combt = big[:, 11500:11500 + TT1 * TOPK * EX1].rearrange("p (t k e) -> p t k e", k=TOPK, e=EX1)

        ps = [ctx.enter_context(nc.psum_tensor(f"ps{i}", [P, 512], f32)) for i in range(8)]

        names = """src_in edges_in rows_in w_in hb_in
        consts norm_ready normed split_h split_r split_m xs_ready_v xs_ready_p xs_out0 xs_out part_ready wbd_ready onet_ready coef_mm coef_out coef_h coef_m coef_r base_mm rounds_ready
        agg_zero oh_done round_ready c_ready mm_done acc_done idx_ready agg_done
        basis_mm tile_mm base_in0 base_in1 xt_in0 xt_in1 xt_used tile_ready tile_out0 tile_out1 std_req std_done gate_in
        tp tp_out logits exp_req exp_done mask_ready places slots_ready zrow_ready xe_zero xh2_in0 xh2_in1 slot_set x1_in
        xe_in0 xe_in1 xe_tp xe_out w1_in0 w1_in1 w2_in0 w2_in1 up relu down y_out y_st0 y_st1 y2_used
        n_zero n_oh n_c n_mm n_acc n_round n_ready tr tr_outa tr_outv xh3_ready alpha alpha_out sums sums_out wc_in wn_in gbias_in tp3 tp3_out
        gm g_out x4_ready tp4 tp4_high tp4_out w_high0 w_high1 w_low0 w_low1 h_high h_low up1 gelu down1 y1_used moe_in out_st dve""".split()
        S = {n: sem(n) for n in names}
        x_in = [sem(f"x_in{k}") for k in range(4)]
        et_in = [sem(f"etype_in{k}") for k in range(3)]
        g = [sem(f"gather{j}") for j in range(BCH)]
        gy = [sem(f"gather_out{j}") for j in range(6)]
        block = ctx.enter_context(nc.Block())

        def window_rounds(eng, k):
            eng.wait_ge(S["rounds_ready"], 1)
            return eng.value_load(rounds_i[0:1, k:k + 1], min_val=1, max_val=W // WIN)

        @block.sync
        def _(sp):
            sp.dma_start(dstr_i[0:ROWS, :, :], dst_rows.rearrange("(t p) e -> p t e", p=ROWS)).then_inc(S["rows_in"], 16)
            for k in range(3):
                sp.dma_start(xin[:, 3 * k:3 * k + 3, :], x[3 * k * P:(3 * k + 3) * P, :].rearrange("(t p) f -> p t f", p=P)).then_inc(x_in[k], 16)
            sp.dma_start(xin[0:LAST, NT - 1, :], x[(NT - 1) * P:N, :]).then_inc(x_in[3], 16)
            for k in range(3):
                for q in range(4):
                    sp.dma_start(etb[32 * q:32 * q + 32, k * EP:(k + 1) * EP], etype[q:q + 1, k * EP:(k + 1) * EP].to_broadcast([32, EP])).then_inc(et_in[k], 16)
            sp.wait_ge(S["xs_ready_v"], 3)
            sp.wait_ge(S["xs_ready_p"], 2)
            sp.dma_start(xs_d[0:HALF * P, :].rearrange("(t p) f -> p t f", p=P), xs[:, 0:HALF].rearrange("p t s f -> p t (s f)")).then_inc(S["xs_out0"], 16)
            sp.wait_ge(S["xs_ready_v"], HALF)
            sp.wait_ge(S["xs_ready_p"], HALF)
            sp.dma_start(xs_d[HALF * P:(NT - 1) * P, :].rearrange("(t p) f -> p t f", p=P), xs[:, HALF:NT - 1].rearrange("p t s f -> p t (s f)")).then_inc(S["xs_out"], 16)
            sp.dma_start(xs_d[(NT - 1) * P:N, :], xs[0:LAST, NT - 1].rearrange("p s f -> p (s f)")).then_inc(S["xs_out"], 16)
            sp.wait_ge(S["agg_done"], 1)
            sp.wait_ge(S["zrow_ready"], 1)
            for n in range(2 * NBASE):
                if n >= 2:
                    sp.wait_ge(S["basis_mm"], n - 1)
                sp.dma_start(bring[:, n % 2], bases[n % NBASE].rearrange("(k p) f -> p k f", p=P)).then_inc(S[f"base_in{n % 2}"], 16)
                if n == 0:
                    sp.dma_start(hb[:], h_bias.to_broadcast([P, F])).then_inc(S["hb_in"], 16)
                    sp.dma_start(wg[:, :, :], w_gating.rearrange("(k p) e -> p k e", p=P)).then_inc(S["gate_in"], 16)
                if n % 2 and n < EX0:
                    sp.dma_start(xe_d[(n - 1) * CAP:(n + 1) * CAP, :].rearrange("(c p) f -> p c f", p=ST),
                                 zrow[0:ST, :].unsqueeze(1).to_broadcast([ST, 6, F])).then_inc(S["xe_zero"], 16)
            sp.wait_ge(S["basis_mm"], 2 * NBASE)
            for e in range(2):
                sp.dma_start(w1r[e], f0_w1[e].rearrange("(k p) h -> p k h", p=P)).then_inc(S[f"w1_in{e}"], 16)
                sp.dma_start(w2r[e], f0_w2[e].rearrange("(k p) f -> p k f", p=P)).then_inc(S[f"w2_in{e}"], 16)
            sp.wait_ge(S["tile_out0"], 32 * (HALF - 1))
            sp.wait_ge(S["tile_out1"], 32 * (HALF - 1))
            sp.dma_start(xh2[:, 0:NT - 2, :], xh2_d[0:(NT - 2) * P, :].rearrange("(t p) f -> p t f", p=P)).then_inc(S["xh2_in0"], 16)
            sp.wait_ge(S["tile_out0"], 32 * HALF)
            sp.wait_ge(S["tile_out1"], 32 * HALF)
            sp.dma_start(xh2[:, NT - 2, :], xh2_d[(NT - 2) * P:(NT - 1) * P, :]).then_inc(S["xh2_in1"], 16)
            sp.dma_start(xh2[0:LAST, NT - 1, :], xh2_d[(NT - 1) * P:N, :]).then_inc(S["xh2_in1"], 16)
            sp.dma_start(x1[:, 0:NT - 1, :], x1_d[0:(NT - 1) * P, :].rearrange("(t p) f -> p t f", p=P)).then_inc(S["x1_in"], 16)
            sp.dma_start(x1[0:LAST, NT - 1, :], x1_d[(NT - 1) * P:N, :]).then_inc(S["x1_in"], 16)
            sp.dma_start(gbias[:], g1_bias).then_inc(S["gbias_in"], 16)
            sp.dma_start(ei[:], x_indices.rearrange("(t p) k -> p t k", p=P)).then_inc(S["moe_in"], 16)
            sp.dma_start(ew[:], x_weights.rearrange("(t p) k -> p t k", p=P)).then_inc(S["moe_in"], 16)

            def expert_io(e, h, more):
                if more:
                    sp.wait_ge(S["up"], e + 1)
                    sp.dma_start(w1r[h], f0_w1[ds(e + 2, 1)].rearrange("o (k p) h -> p (o k) h", p=P)).then_inc(S[f"w1_in{h}"], 16)
                    sp.wait_ge(S["down"], 3 * e + 3)
                    sp.dma_start(w2r[h], f0_w2[ds(e + 2, 1)].rearrange("o (k p) f -> p (o k) f", p=P)).then_inc(S[f"w2_in{h}"], 16)
                sp.wait_ge(S["y_out"], 3 * e + 3)
                sp.dma_start(ye_d[ds(e * CAP, CAP), :].rearrange("(s p) f -> p s f", p=ST), ysb[:, h]).then_inc(S[f"y_st{h}"], 16)

            with sp.Fori(0, EX0 // 2 - 1) as i:
                for h in range(2):
                    expert_io(i * 2 + h, h, True)
            sp.wait_ge(S["up"], EX0)
            sp.dma_start(wcs[:, :, :], wc.rearrange("(k p) f -> p k f", p=P)).then_inc(S["wc_in"], 16)
            for h in range(2):
                expert_io(EX0 - 2 + h, h, False)
            sp.wait_ge(S["xh3_ready"], HALF)
            sp.dma_start(wns[:, :, :], wn.rearrange("(k p) f -> p k f", p=P)).then_inc(S["wn_in"], 16)
            sp.wait_ge(S["xh3_ready"], NT)
            for e in range(EX1):
                w = w1s[e % 2].rearrange("p (k h) -> p k h", k=NF), w2s[e % 2].rearrange("p (k f) -> p k f", k=2)
                if e >= 2:
                    sp.wait_ge(S["w_low0"], e - 1)
                sp.dma_start(w[0], f1_w1[e].rearrange("(k p) h -> p k h", p=P)).then_inc(S[f"w1_in{e % 2}"], 16)
                if e >= 2:
                    sp.wait_ge(S["w_low1"], e - 1)
                sp.dma_start(w[1], f1_w2[e].rearrange("(k p) f -> p k f", p=P)).then_inc(S[f"w2_in{e % 2}"], 16)
                if e == 1:
                    sp.wait_ge(S["g_out"], NT)
                    sp.dma_start(out[T1:(NT - 1) * P, :].rearrange("(t p) f -> p t f", p=P), x1[:, TT1:NT - 1, :]).then_inc(S["out_st"], 16)
                    sp.dma_start(out[(NT - 1) * P:N, :], x1[0:LAST, NT - 1, :]).then_inc(S["out_st"], 16)
            for t in range(TT1):
                sp.wait_ge(S["y1_used"], TT1 * (EX1 - 1) + t + 1)
                sp.dma_start(out[t * P:(t + 1) * P, :], x1[:, t, :]).then_inc(S["out_st"], 16)
            sp.wait_ge(S["out_st"], 16 * (2 + TT1))

        @block.gpsimd
        def _(pool):
            nc.gpsimd.iota(iota_i[:], pattern=[[1, P]], base=0, channel_multiplier=0).then_inc(S["consts"], 1)
            nc.gpsimd.iota(part_i[:, 0:1], pattern=[[1, 1]], base=0, channel_multiplier=1).then_inc(S["consts"], 1)
            pool.dma_start(src_i[:, 0:NCH], src_cols[:, 0:NCH]).then_inc(S["src_in"], 16)
            pool.dma_start(src_i[:, NCH:NCH + 2 * BCH], src_cols[:, 0:2 * BCH]).then_inc(S["src_in"], 16)
            pool.dma_start(dst_i[:], dst_cols).then_inc(S["edges_in"], 16)
            pool.dma_start(wgt[:], wgt_cols).then_inc(S["edges_in"], 16)
            nc.gpsimd.memset(zone[7], 0.0).then_inc(S["agg_zero"], 1)
            for k in range(2):
                pool.wait_ge(S["onet_ready"], k + 1)
                nc.gpsimd.memset(zone[3][:, k * EP:(k + 1) * EP], 0.0).then_inc(S["agg_zero"], 1)
                if k == 0:
                    for t in range(1, NT, 2):
                        pool.wait_ge(S["split_m"], t + 1)
                        nc.gpsimd.tensor_tensor(xs[0:rows(t), t, 2], xh[0:rows(t), t], xs[0:rows(t), t, 1], ALU.subtract).then_inc(S["xs_ready_p"], 1)
            pool.wait_ge(S["onet_ready"], 3)
            nc.gpsimd.memset(zone[3][:, 2 * EP:], 0.0).then_inc(S["agg_zero"], 1)
            pool.wait_ge(S["xs_out0"], 16)
            nc.gpsimd.memset(zone[2][:, 0:XH], 0.0).then_inc(S["agg_zero"], 1)
            pool.wait_ge(S["coef_mm"], QCH // CSTEP)
            nc.gpsimd.memset(zone[4], 0.0).then_inc(S["agg_zero"], 1)
            pool.wait_ge(S["xs_out"], 32)
            rounds = window_rounds(pool, 0)
            with pool.Fori(0, rounds) as r:
                with pool.Fori(0, NB // 2) as i:
                    for h in range(2):
                        n = r * NB + i * 2 + h
                        pool.wait_ge(S["idx_ready"], n + 1)
                        for j in range(BCH):
                            pool.wait_ge(S["mm_done"], n * BCH + j + 1)
                            pool.nop(nofuse=True)
                            pool.indirect_dma_start(xg[:, j].rearrange("p s f -> p (s f)"), None, xs_d,
                                                    bass.IndirectOffsetOnAxis(idx[:, h, j:j + 1], 0)).then_inc(g[j], 16)
            pool.wait_ge(S["agg_done"], 1)
            nc.gpsimd.memset(zrow[:], 0.0).then_inc(S["zrow_ready"], 1)
            for t in range(NT):
                if t >= 2:
                    pool.wait_ge(S["xt_used"], t - 1)
                pool.dma_start(xt[0:rows(t), t % 2, :], x[t * P:t * P + rows(t), :]).then_inc(S[f"xt_in{t % 2}"], 16)
            pool.wait_ge(S["basis_mm"], 2 * NBASE)
            nc.gpsimd.memset(nT[:, :, :], 0.0).then_inc(S["n_zero"], 1)
            pool.wait_ge(S["xe_zero"], 16 * NBASE)
            for k in range(2):
                pool.wait_ge(S["slots_ready"], k + 1)
                for t in range(NT):
                    if k == 0 and t == 0:
                        pool.wait_ge(S["xh2_in0"], 16)
                    if k == 0 and t == NT - 2:
                        pool.wait_ge(S["xh2_in1"], 32)
                    pool.indirect_dma_start(xe_d, bass.IndirectOffsetOnAxis(slot_i[0:rows(t), k, t:t + 1], 0), xh2[0:rows(t), t, :], None,
                                            bounds_check=SLOTS - 1, oob_is_err=False).then_inc(S["slot_set"], 16)

            def expert_rows(e, h):
                pool.dma_start(xer[:, ds(3 * h, 3), :], xe_d[ds(e * CAP, CAP), :].rearrange("(s p) f -> p s f", p=ST)).then_inc(S[f"xe_in{h}"], 16)

            pool.wait_ge(S["slot_set"], 16 * 2 * NT)
            for e in range(2):
                expert_rows(e, e)
            with pool.Fori(1, EX0 // 2) as i:
                for h in range(2):
                    pool.wait_ge(S["xe_tp"], 6 * i + 3 * h - 3)
                    expert_rows(i * 2 + h, h)
            pool.wait_ge(S["y_st0"], 16 * EX0 // 2)
            pool.wait_ge(S["y_st1"], 16 * EX0 // 2)
            pool.wait_ge(S["up"], EX0)
            for n in range(2 * NT):
                if n >= 6:
                    pool.wait_ge(S["y2_used"], n - 5)
                pool.indirect_dma_start(y2[:, n % 6, :], None, ye_d, bass.IndirectOffsetOnAxis(slot_i[:, 2 + n % 2, n // 2:n // 2 + 1], 0)).then_inc(gy[n % 6], 16)

        @block.scalar
        def _(act):
            roots = [0]

            def root(a, b):
                roots[0] += 1
                act.wait_ge(S["std_req"], roots[0])
                nc.scalar.activation(std[:, a:b], mv[:, a:b, 1], ACT.Sqrt, bias=eps[:]).then_inc(S["std_done"], 1)

            for q in range(4):
                act.dma_start(wc4[32 * q:32 * q + 32, :], w_comp).then_inc(S["w_in"], 16)
            root(0, NT)
            act.wait_ge(S["norm_ready"], 1)
            for t in range(NT):
                nc.scalar.activation(xh[0:rows(t), t], xin[0:rows(t), t], ACT.Identity, bias=shift[0:rows(t), t:t + 1], scale=rstd[0:rows(t), t:t + 1]).then_inc(S["normed"], 1)
                act.wait_ge(S["normed"], t + 1)
                nc.scalar.copy(xs[0:rows(t), t, 0], xh[0:rows(t), t]).then_inc(S["split_h"], 1)
            for t in range(NT):
                act.wait_ge(S["split_r"], t + 1)
                nc.scalar.copy(xs[0:rows(t), t, 1], xh[0:rows(t), t]).then_inc(S["split_m"], 1)
            act.wait_ge(S["src_in"], 32)
            for h in range(2):
                nc.scalar.copy(idx[:, h, :], src_i[:, h * BCH:(h + 1) * BCH]).then_inc(S["idx_ready"], 1)
            nc.scalar.memzero(zone[0]).then_inc(S["agg_zero"], 1)
            act.wait_ge(S["xs_ready_v"], HALF)
            act.wait_ge(S["xs_ready_p"], HALF)
            nc.scalar.memzero(zone[1]).then_inc(S["agg_zero"], 1)
            act.wait_ge(S["coef_out"], len(CBANK) + QCH // CSTEP)
            nc.scalar.copy(coef[:, 0, 0:NCH // 2], coeff[:, 0:NCH // 2]).then_inc(S["coef_h"], 1)
            nc.scalar.copy(coef[:, 0, NCH // 2:NCH], coeff[:, NCH // 2:NCH]).then_inc(S["coef_h"], 1)
            for k in range(2):
                act.wait_ge(S["coef_r"], k + 1)
                nc.scalar.copy(coef[:, 1, k * NCH // 2:(k + 1) * NCH // 2], coeff[:, k * NCH // 2:(k + 1) * NCH // 2]).then_inc(S["coef_m"], 1)
            act.wait_ge(S["xs_out"], 32)
            nc.scalar.memzero(zone[2][:, XH:]).then_inc(S["agg_zero"], 1)
            nc.scalar.memzero(zone[5]).then_inc(S["agg_zero"], 1)
            rounds = window_rounds(act, 0)
            with act.Fori(0, rounds) as r:
                with act.Fori(0, NB // 2) as i:
                    for h in range(2):
                        n = r * NB + i * 2 + h
                        act.wait_ge(S["mm_done"], n * BCH + 2 * BCH)
                        nc.scalar.copy(idx[:, h, :], src_i[:, ds((i * 2 + h) * BCH + 2 * BCH, BCH)]).then_inc(S["idx_ready"], 1)

            def tile_columns(t):
                act.wait_ge(S["tp"], t + 1)
                if t >= 2:
                    act.wait_ge(S["logits"], t - 1)
                nc.scalar.copy(xT[:, t % 2, :, 0:rows(t)], ps[2 + t % 2][:].rearrange("p (k n) -> p k n", k=NF)[:, :, 0:rows(t)]).then_inc(S["tp_out"], 1)

            for t in range(NT):
                r_ = rows(t)
                if t == HALF:
                    tile_columns(t - 1)
                root(t, t + 1)
                act.wait_ge(S["tile_ready"], t + 1)
                act.dma_start(xh2_d[t * P:t * P + r_, :], xn[0:r_, t % 2, :]).then_inc(S[f"tile_out{t % 2}"], 16)
                act.dma_start(x1_d[t * P:t * P + r_, :], xo[0:r_, t % 2, :]).then_inc(S[f"tile_out{t % 2}"], 16)
                if t and t != HALF:
                    tile_columns(t - 1)
            tile_columns(NT - 1)
            act.wait_ge(S["exp_req"], 1)
            nc.scalar.activation(g_[:, 0], g_[:, 1], ACT.Exp).then_inc(S["exp_done"], 1)

            def slot_tile(e, h, s):
                act.wait_ge(S["xe_tp"], e * 3 + s + 1)
                nc.scalar.copy(xe[:, h, :, s * ST:(s + 1) * ST], ps[0][:, 0:NF * ST].rearrange("p (k n) -> p k n", k=NF)).then_inc(S["xe_out"], 1)

            def relu(e, h):
                act.wait_ge(S["up"], e + 1)
                for k in range(2):
                    ins = nc.scalar.activation(hT[:, h, k, :], ps[2 + k][:, 0:CAP], ACT.Relu)
                ins.then_inc(S["relu"], 1)

            def expert_out(e, h, ahead, stored):
                if stored is not None:
                    act.wait_ge(S[f"y_st{h}"], stored)
                for s in range(3):
                    act.wait_ge(S["down"], e * 3 + s + 1)
                    nc.scalar.copy(ysb[:, h, s, :], ps[6 + (h + s) % 2][0:ST, :]).then_inc(S["y_out"], 1)
                    if ahead:
                        slot_tile(e + 2, h, s)

            act.wait_ge(S["tile_out0"], 32 * HALF)
            act.wait_ge(S["tile_out1"], 32 * HALF)
            for s in range(3):
                slot_tile(0, 0, s)
            relu(0, 0)
            for s in range(3):
                slot_tile(1, 1, s)
            relu(1, 1)
            expert_out(0, 0, True, None)
            act.wait_ge(S["down"], 3)
            relu(2, 0)
            expert_out(1, 1, True, None)
            with act.Fori(1, EXC // 2) as i:
                for h in range(2):
                    e = i * 2 + h
                    act.wait_ge(S["down"], e * 3)
                    relu(e + 1, 1 - h)
                    expert_out(e, h, True, i * 16)
            for e in range(EXC, EX0):
                if e + 1 < EX0:
                    act.wait_ge(S["down"], e * 3)
                    relu(e + 1, 1 - e % 2)
                expert_out(e, e % 2, e + 2 < EX0, 16 * (e // 2))
                for n in range(TURN[e - EXC], TURN[e - EXC + 1]):
                    if n % 2:
                        t, q = n // 3, n % 3
                        w_ = min(4 * P, NP - 4 * P * q)
                        act.wait_ge(S["tr"], n + 1)
                        nc.scalar.copy(adj[0:cols(t), t, 4 * P * q:4 * P * q + w_], ps[TBANK[n % 3]][0:cols(t), 0:w_]).then_inc(S["tr_outa"], 1)

            def own_columns(t):
                act.wait_ge(S["tp3"], t + 1)
                if t >= 2:
                    act.wait_ge(S["alpha"], t - 1)
                nc.scalar.copy(xT3[:, t % 2, :, 0:rows(t)], ps[t % 2][:].rearrange("p (k n) -> p k n", k=NF)[:, :, 0:rows(t)]).then_inc(S["tp3_out"], 1)

            for t in range(NT):
                root(t, t + 1)
                if t >= 2:
                    own_columns(t - 2)
            for t in range(NT - 2, NT):
                own_columns(t)

            def weights_high(e, k):
                act.wait_ge(S[f"w{k + 1}_in{e % 2}"], 16 * (EX0 // 2 + e // 2 + 1))
                if e >= 2:
                    act.wait_ge(*((S["up1"], e - 1) if k == 0 else (S["down1"], TT1 * (e - 1))))
                nc.scalar.copy(w4p[:, e % 2, 0, k], (w1s, w2s)[k][e % 2]).then_inc(S[f"w_high{k}"], 1)

            act.wait_ge(S["sums"], 3 * NF)
            for e, k in ((0, 0), (1, 0), (0, 1)):
                weights_high(e, k)
            root(0, TT1)
            for t in range(TT1):
                act.wait_ge(S["tp4"], t + 1)
                nc.scalar.copy(x4p[:, 0, :, t * P:(t + 1) * P], ps[6 + t % 2][:].rearrange("p (k n) -> p k n", k=NF)).then_inc(S["tp4_high"], 1)
            for e in range(EX1):
                act.wait_ge(S["up1"], e + 1)
                if e >= 2:
                    act.wait_ge(S["h_low"], e - 1)
                for k in range(2):
                    ins = nc.scalar.activation(hT1[:, e % 2, k, :], ps[(e % 2) * 2 + k][:], ACT.Gelu)
                ins.then_inc(S["gelu"], 1)
                act.wait_ge(S["gelu"], e + 1)
                if e >= 2:
                    act.wait_ge(S["down1"], TT1 * (e - 1))
                nc.scalar.copy(h4p[:, e % 2, 0], hT1[:, e % 2]).then_inc(S["h_high"], 1)
                if e + 2 < EX1:
                    weights_high(e + 2, 0)
                if e + 1 < EX1:
                    weights_high(e + 1, 1)

        @block.tensor
        def _(pe):
            MM = nc.tensor.matmul
            pe.wait_ge(S["base_mm"], 1)
            for t in range(RT):
                MM(ps[5][:, t * ROWS:(t + 1) * ROWS], minb[:, t, :], ident[0:ROWS, 0:ROWS], start=True, stop=True)
            for t in range(RT):
                ins = MM(ps[4][:, t * ROWS:(t + 1) * ROWS], maxb[:, t, :], ident[0:ROWS, 0:ROWS], start=True, stop=True)
            ins.then_inc(S["base_mm"], 1)
            pe.wait_ge(S["wbd_ready"], 1)
            with pe.Fori(0, 3) as i:
                pe.wait_ge(S["onet_ready"], i + 1)
                for u in range(3):
                    pe.wait_ge(S["coef_out"], i * 3 + u + 1)
                    for j in range(CSTEP):
                        for s in range(PARTS):
                            ins = MM(ps[CBANK[u]][:, j * 32:(j + 1) * 32], onet[:, ds((i * 3 + u) * CSTEP * P + j * P, P)],
                                     wbd[:, s].rearrange("p q b -> p (q b)"), start=s == 0, stop=s == PARTS - 1)
                    ins.then_inc(S["coef_mm"], 1)
            pe.sem_inc(S["mm_done"], BCH)
            rounds = window_rounds(pe, 0)
            with pe.Fori(0, rounds) as r:
                with pe.Fori(0, NB // 2) as i:
                    for h in range(2):
                        n = r * NB + i * 2 + h
                        pe.wait_ge(S["c_ready"], n + r + 1)
                        for j in range(BCH):
                            pe.wait_ge(g[j], n * 16 + 16)
                            pe.wait_ge(S["acc_done"], n * BCH + j + 1)
                            for f in range(NF):
                                for s in range(PARTS):
                                    for c in range(PARTS - s):
                                        ins = MM(ps[j][:, f * 64:(f + 1) * 64], xg[:, j, s, f * P:(f + 1) * P],
                                                 cb[:, h, c, j].rearrange("p b w -> p (b w)"),
                                                 start=s + c == 0, stop=s == PARTS - 1)
                            ins.then_inc(S["mm_done"], 1)

            def transpose_tile(t):
                r_ = rows(t)
                pe.wait_ge(S["tile_ready"], t + 1)
                if t < 2:
                    pe.wait_ge(S["xt_used"], 3 + t)
                else:
                    pe.wait_ge(S["tp_out"], t - 1)
                for k in range(NF):
                    ins = nc.tensor.transpose(ps[2 + t % 2][:, k * P:k * P + r_], xn[0:r_, t % 2, k * P:(k + 1) * P], ident[0:r_, 0:r_])
                ins.then_inc(S["tp"], 1)

            def logits(t):
                pe.wait_ge(S["tp_out"], t + 1)
                if t == 0:
                    pe.wait_ge(S["xt_used"], HALF)
                    pe.wait_ge(S["gate_in"], 16)
                for k in range(NF):
                    ins = MM(ps[4][:, t * EX0:(t + 1) * EX0], xT[:, t % 2, k, :], wg[:, k, :], start=k == 0, stop=k == NF - 1)
                ins.then_inc(S["logits"], 1)

            pe.wait_ge(S["agg_done"], 1)
            for half in range(2):
                for b in range(NBASE):
                    n = half * NBASE + b
                    pe.wait_ge(S[f"base_in{n % 2}"], 16 * (n // 2 + 1))
                    for t in range(HALF * half, HALF * half + HALF):
                        if b == 0 and t >= 8:
                            pe.wait_ge(S["xt_used"], t - 8 + 1)
                        for k in range(NF):
                            ins = MM(ps[t % 8][0:cols(t), :], agg[:, k, b, t * P:t * P + cols(t)], bring[:, n % 2, k, :],
                                     start=b == 0 and k == 0, stop=b == NBASE - 1 and k == NF - 1, skip_group_check=True)
                        if b == NBASE - 1:
                            ins.then_inc(S["tile_mm"], 1)
                            if t >= HALF + 2:
                                transpose_tile(t - 2)
                            if t >= HALF + 3:
                                logits(t - 3)
                        elif t == HALF * half + HALF - 1:
                            ins.then_inc(S["basis_mm"], 1)
                    if half and 1 <= b <= HALF:
                        transpose_tile(b - 1)
                    if half and 2 <= b <= HALF + 1:
                        logits(b - 2)
                    if b == NBASE - 1:
                        pe.drain().then_inc(S["basis_mm"], 1)
            logits(NT - 3)
            for t in range(NT - 2, NT):
                transpose_tile(t)
                logits(t)
            for k in range(3):
                pe.wait_ge(S["mask_ready"], k + 1)
                mask = mb.rearrange("p t e -> p (t e)")
                if k != 1:
                    MM(ps[3][:, 0:NT * EX0], tri[:], mask, start=True, stop=True)
                MM(ps[4][:, 0:NT * EX0], ones[:], mask, start=True, stop=True).then_inc(S["places"], 1)

            def counts(b, h, r=0):
                pe.wait_ge(S["n_c"], b + r + 1)
                for q in range(NGRP):
                    pe.wait_ge(S["n_acc"], b * NGRP + q + 1)
                    for j in range(GRP):
                        ins = MM(ps[1 + 3 * q][:, 0:160], rside[:, h, q * GRP + j, :],
                                 lside[:, h, q * GRP + j].rearrange("p u w -> p (u w)"), start=j == 0, stop=j == GRP - 1)
                    ins.then_inc(S["n_mm"], 1)

            with pe.Fori(0, N_AHEAD // 2) as i:
                for h in range(2):
                    counts(i * 2 + h, h)

            def slot_tile(e, h, s, loaded):
                pe.wait_ge(S[f"xe_in{h}"], loaded)
                if loaded > 16 or h or s:
                    pe.wait_ge(S["xe_out"], e * 3 + s)
                for k in range(NF):
                    ins = nc.tensor.transpose(ps[0][:, k * ST:(k + 1) * ST], xer[:, h * 3 + s, k * P:(k + 1) * P], ident[0:ST, 0:ST])
                ins.then_inc(S["xe_tp"], 1)

            def up(e, h, loaded, relued, beside=None):
                pe.wait_ge(S[f"w1_in{h}"], loaded)
                pe.wait_ge(S["xe_out"], e * 3 + 3)
                if relued is not None:
                    pe.wait_ge(S["relu"], relued)
                for k in range(2):
                    for f in range(NF):
                        ins = MM(ps[2 + k][:, 0:CAP], w1r[h][:, f, k * P:(k + 1) * P], xe[:, h, f, :], start=f == 0, stop=f == NF - 1)
                    if k == 1:
                        ins.then_inc(S["up"], 1)
                    elif beside is not None:
                        counts(beside, 0)

            def down(e, h, loaded, ahead, first, beside=None):
                pe.wait_ge(S[f"w2_in{h}"], loaded)
                pe.wait_ge(S["relu"], e + 1)
                for s in range(3):
                    if not (first and s < 2):
                        pe.wait_ge(S["y_out"], e * 3 + s - 1)
                    for k in range(2):
                        ins = MM(ps[6 + (h + s) % 2][0:ST, :], hT[:, h, k, s * ST:(s + 1) * ST], w2r[h][:, k, :], start=k == 0, stop=k == 1)
                    ins.then_inc(S["down"], 1)
                    if ahead:
                        slot_tile(e + 2, h, s, loaded + 16)
                    if beside is not None:
                        counts(beside + s, (s + 1) % 2)

            pe.wait_ge(S["slots_ready"], 2)
            for h in range(2):
                for s in range(3):
                    slot_tile(h, h, s, 16)
                if h == 0:
                    up(0, 0, 16, None)
            up(1, 1, 16, 1)
            counts(N_AHEAD, 0)
            down(0, 0, 16, True, True, N_AHEAD + 1)
            up(2, 0, 32, 2, N_AHEAD + N_PER)
            down(1, 1, 16, True, False, N_AHEAD + N_PER + 1)
            with pe.Fori(1, EXC // 2) as i:
                for h in range(2):
                    e = i * 2 + h
                    beside = e * N_PER + N_AHEAD
                    up(e + 1, 1 - h, i * 16 + 16 + 16 * h, e + 1, beside)
                    down(e, h, i * 16 + 16, True, False, beside + 1)
            rounds = window_rounds(pe, 1)
            with pe.If(rounds > 1):
                with pe.Fori(1, rounds) as r:
                    with pe.Fori(0, NB // 2) as i:
                        for h in range(2):
                            counts(r * NB + i * 2 + h, h, r)
            pe.end_ifs()

            def turn(n):
                t, q = n // 3, n % 3
                if n >= 3:
                    pe.wait_ge(S["tr_outv" if n % 2 else "tr_outa"], (n - 3) // 2 + 1)
                for u in range(4 * q, min(4 * q + 4, UH)):
                    ins = nc.tensor.transpose(ps[TBANK[n % 3]][0:cols(t), (u % 4) * P:(u % 4 + 1) * P], nT[:, u, t * P:t * P + cols(t)], ident[:])
                ins.then_inc(S["tr"], 1)

            for e in range(EXC, EX0):
                h = e % 2
                if e + 1 < EX0:
                    up(e + 1, 1 - h, 16 * ((e + 1) // 2 + 1), e + 1)
                down(e, h, 16 * (e // 2 + 1), e + 2 < EX0, False)
                if e == EXC:
                    pe.wait_ge(S["n_ready"], 1)
                for n in range(TURN[e - EXC], TURN[e - EXC + 1]):
                    turn(n)
            pe.wait_ge(S["wc_in"], 16)
            pe.wait_ge(S["gbias_in"], 16)
            pe.wait_ge(S["y_out"], 3 * EX0)

            def own_product(t):
                pe.wait_ge(S["tp3_out"], t + 1)
                if t >= 2:
                    pe.wait_ge(S["alpha_out"], t - 1)
                for k in range(NF):
                    MM(ps[6 + t % 2][0:rows(t), :], xT3[:, t % 2, k, 0:rows(t)], wcs[:, k, :], start=k == 0, stop=False)
                MM(ps[6 + t % 2][0:rows(t), :], one_row[:, 0:rows(t)], gbias[:], start=False, stop=True).then_inc(S["alpha"], 1)

            for t in range(NT):
                pe.wait_ge(S["xh3_ready"], t + 1)
                if t >= 2:
                    pe.wait_ge(S["tp3_out"], t - 1)
                for k in range(NF):
                    ins = nc.tensor.transpose(ps[t % 2][:, k * P:k * P + rows(t)], xh3[0:rows(t), t, k * P:(k + 1) * P], ident[0:rows(t), 0:rows(t)])
                ins.then_inc(S["tp3"], 1)
                if t:
                    own_product(t - 1)
            own_product(NT - 1)
            pe.wait_ge(S["tr_outa"], 3 * NT // 2)
            pe.wait_ge(S["tr_outv"], 3 * NT // 2)
            for k in range(NF):
                for q in range(3):
                    n = 3 * k + q
                    w_ = min(512, NP - 512 * q)
                    if n >= 3:
                        pe.wait_ge(S["sums_out"], n - 2)
                    for t in range(NT):
                        ins = MM(ps[2 + n % 3][:, 0:w_], xh3[0:rows(t), t, k * P:(k + 1) * P], adj[0:rows(t), t, 512 * q:512 * q + w_], start=t == 0, stop=t == NT - 1)
                    ins.then_inc(S["sums"], 1)
            pe.wait_ge(S["sums_out"], 3 * NF)
            pe.wait_ge(S["tp3_out"], NT)
            pe.wait_ge(S["wn_in"], 16)
            for t in range(NT):
                if t >= 6:
                    pe.wait_ge(S["g_out"], t - 5)
                for k in range(NF):
                    ins = MM(ps[t % 6][0:rows(t), :], sT[:, k, t * P:t * P + rows(t)], wns[:, k, :], start=k == 0, stop=k == NF - 1)
                ins.then_inc(S["gm"], 1)
                if t >= NT - TT1:
                    u = t - (NT - TT1)
                    pe.wait_ge(S["x4_ready"], 1)
                    if u >= 2:
                        pe.wait_ge(S["tp4_out"], u - 1)
                    for k in range(NF):
                        ins = nc.tensor.transpose(ps[6 + u % 2][:, k * P:(k + 1) * P], xh4[:, u, k * P:(k + 1) * P], ident[:])
                    ins.then_inc(S["tp4"], 1)
            pe.wait_ge(S["tp4_out"], TT1)
            pe.wait_ge(S["g_out"], NT)

            pairs = ((0, 0), (0, 1), (1, 0))

            def up1(e):
                pe.wait_ge(S["w_low0"], e + 1)
                if e >= 2:
                    pe.wait_ge(S["gelu"], e - 1)
                for k in range(2):
                    for f in range(NF):
                        w = f * H1 + k * P
                        for a, b in pairs:
                            ins = MM(ps[(e % 2) * 2 + k][:], w4p[:, e % 2, a, 0, w:w + P], x4p[:, b, f, :],
                                     start=f == 0 and a + b == 0, stop=f == NF - 1 and a == 1)
                ins.then_inc(S["up1"], 1)

            up1(0)
            for e in range(EX1):
                if e + 1 < EX1:
                    up1(e + 1)
                pe.wait_ge(S["w_low1"], e + 1)
                pe.wait_ge(S["h_low"], e + 1)
                for t in range(TT1):
                    if e:
                        pe.wait_ge(S["y1_used"], TT1 * (e - 1) + t + 1)
                    for k in range(2):
                        for a, b in pairs:
                            ins = MM(ps[4 + t][:], h4p[:, e % 2, a, k, t * P:(t + 1) * P], w4p[:, e % 2, b, 1, k * F:(k + 1) * F],
                                     start=k == 0 and a + b == 0, stop=k == 1 and a == 1)
                    ins.then_inc(S["down1"], 1)

        @block.vector
        def _(dve):
            V = nc.vector
            chain = [0]

            def link(ins):
                chain[0] += 1
                ins.then_inc(S["dve"], 1)
                dve.wait_ge(S["dve"], chain[0])

            roots = [0]

            def moments(t, src):
                link(V.bn_stats(stats[0:rows(t), :], src))
                link(V.bn_aggr(mv[0:rows(t), t, :], stats[0:rows(t), :]))

            def inverse_std(a, b):
                roots[0] += 1
                V.engine_nop().then_inc(S["std_req"], 1)
                dve.wait_ge(S["std_done"], roots[0])
                link(V.reciprocal(rstd[:, a:b], std[:, a:b]))

            def normalize(t, dst, src):
                return V.tensor_scalar(dst, src, mv[0:rows(t), t, 0:1], rstd[0:rows(t), t:t + 1], ALU.subtract, ALU.mult)

            link(V.memset(eps[:], EPS))
            dve.sem_inc(S["coef_out"], len(CBANK))
            link(V.memset(ones[:], 1.0))
            link(V.memset(one_row[:], 1.0))
            link(V.memset(mv[:], 0.0))
            dve.wait_ge(S["consts"], 2)
            link(V.tensor_copy(iota[:], iota_i[:]))
            link(V.tensor_single_scalar(part_i[:, 1:2], part_i[:, 0:1], NREL - 1, ALU.bitwise_and))
            link(V.tensor_single_scalar(part_i[:, 2:3], part_i[:, 0:1], 5, ALU.logical_shift_right))
            V.tensor_copy(part[:], part_i[:]).then_inc(S["part_ready"], 1)
            dve.wait_ge(S["part_ready"], 1)
            link(V.tensor_scalar(ident[:], iota[:], part[:, 0:1], None, ALU.is_equal))
            link(V.tensor_scalar(tri[:], iota[:], part[:, 0:1], None, ALU.is_gt))
            link(V.tensor_scalar(qmask[:], iota[:, 0:4], part[:, 2:3], None, ALU.is_equal))
            dve.wait_ge(S["rows_in"], 16)
            link(V.tensor_copy(dstr[0:ROWS], dstr_i[0:ROWS]))
            link(V.scalar_tensor_tensor(out=dstm[0:ROWS], in0=dstr[0:ROWS], scalar=float(N), in1=dstr[0:ROWS], op0=ALU.is_lt, op1=ALU.mult))
            link(V.tensor_reduce(mins[:, 0, :], dstr[0:ROWS], AX.X, ALU.min))
            link(V.tensor_reduce(mins[:, 1, :], dstm[0:ROWS], AX.X, ALU.max))
            link(V.tensor_copy(minb[:, :, :], mins[:, 0, :].unsqueeze(2).to_broadcast([ROWS, RT, P])))
            V.tensor_copy(maxb[:, :, :], mins[:, 1, :].unsqueeze(2).to_broadcast([ROWS, RT, P])).then_inc(S["base_mm"], 1)
            cq = coeff[:, :, :].rearrange("p (q c) b -> p q c b", q=4)
            wq = wgt[:, 0:NCH].rearrange("p (q c) -> p q c", q=4)

            def coefficients(i):
                for u in range(3):
                    n = i * 3 + u
                    dve.wait_ge(S["coef_mm"], n + 1)
                    pc = ps[CBANK[u]][:, 0:CSTEP * 32].rearrange("p (c q b) -> p q c b", q=4, b=NBASE)
                    at_ = slice(n * CSTEP, (n + 1) * CSTEP)
                    V.tensor_tensor(cq[:, :, at_, :], pc, wq[:, :, at_].unsqueeze(3).to_broadcast([P, 4, CSTEP, NBASE]), ALU.mult).then_inc(S["coef_out"], 1)

            for t in range(NT):
                if t % 3 == 0:
                    dve.wait_ge(x_in[t // 3], 16)
                moments(t, xin[0:rows(t), t, :])
            V.engine_nop().then_inc(S["std_req"], 1)
            dve.wait_ge(S["w_in"], 64)
            link(V.tensor_copy(wpart[:, 0, :], wc4[:]))
            link(V.tensor_tensor(wc4[:], wc4[:], wpart[:, 0, :], ALU.subtract))
            link(V.tensor_copy(wpart[:, 1, :], wc4[:]))
            link(V.tensor_tensor(wc4[:], wc4[:], wpart[:, 1, :], ALU.subtract))
            link(V.tensor_copy(wpart[:, 2, :], wc4[:]))
            for k in range(PARTS):
                ins = V.tensor_tensor(wbd[:, k], wpart[:, k, :].unsqueeze(1).to_broadcast([P, 4, NBASE]),
                                      qmask[:].unsqueeze(2).to_broadcast([P, 4, NBASE]), ALU.mult)
            ins.then_inc(S["wbd_ready"], 1)
            roots[0] += 1
            dve.wait_ge(S["std_done"], 1)
            link(V.reciprocal(rstd[:], std[:]))
            V.scalar_tensor_tensor(out=shift[:], in0=mv[:, :, 0], scalar=-1.0, in1=rstd[:], op0=ALU.mult, op1=ALU.mult).then_inc(S["norm_ready"], 1)

            def relations(k):
                dve.wait_ge(et_in[k], 64)
                V.tensor_scalar(onet[:, k * EP:(k + 1) * EP], etb[:, k * EP:(k + 1) * EP], part[:, 1:2], None, ALU.is_equal).then_inc(S["onet_ready"], 1)

            relations(0)
            for t in range(NT):
                dve.wait_ge(S["split_h"], t + 1)
                V.tensor_tensor(xh[0:rows(t), t], xh[0:rows(t), t], xs[0:rows(t), t, 0], ALU.subtract).then_inc(S["split_r"], 1)
            relations(1)
            dve.wait_ge(S["src_in"], 32)
            dve.wait_ge(S["edges_in"], 32)
            link(V.memset(coef[:, :, NCH:TCOL, :], 0.0))
            link(V.memset(basef[:, NCH:TCOL], 0.0))
            link(V.tensor_copy(dstf[:], dst_i[:]))
            coefficients(0)
            for t in range(0, NT, 2):
                dve.wait_ge(S["split_m"], t + 1)
                V.tensor_tensor(xs[0:rows(t), t, 2], xh[0:rows(t), t], xs[0:rows(t), t, 1], ALU.subtract).then_inc(S["xs_ready_v"], 1)
            relations(2)
            coefficients(1)
            dve.wait_ge(S["base_mm"], 2)
            link(V.tensor_copy(basef[:, 0:NCH], ps[5][:, 0:NCH]))
            link(V.tensor_reduce(base3[:], basef[:, 0:NCH].rearrange("p (g c) -> p g c", c=GRP), AX.X, ALU.min))
            link(V.tensor_reduce(top3[:], ps[4][:, 0:NCH].rearrange("p (g c) -> p g c", c=GRP), AX.X, ALU.max))
            link(V.tensor_tensor(top3[:], top3[:], base3[:], ALU.subtract))
            link(V.tensor_reduce(gap[:, 1:2], top3[:], AX.X, ALU.max))
            link(V.tensor_tensor(gaps[:], ps[4][:, 0:NCH], basef[:, 0:NCH], ALU.subtract))
            link(V.tensor_reduce(gap[:, 0:1], gaps[:], AX.X, ALU.max))
            link(V.tensor_copy(gap_i[:], gap[:]))
            link(V.tensor_single_scalar(gap_i[:, 0:1], gap_i[:, 0:1], 3, ALU.logical_shift_right))
            link(V.tensor_single_scalar(gap_i[:, 1:2], gap_i[:, 1:2], 4, ALU.logical_shift_right))
            link(V.tensor_copy(gap[:], gap_i[:]))
            V.tensor_scalar(rounds_i[:], gap[0:1, :], 1.0, None, ALU.add).then_inc(S["rounds_ready"], 1)
            coefficients(2)
            half = [slice(k * NCH // 2, (k + 1) * NCH // 2) for k in range(2)]
            for k in range(2):
                dve.wait_ge(S["coef_h"], k + 1)
                V.tensor_tensor(coeff[:, half[k]], coeff[:, half[k]], coef[:, 0, half[k]], ALU.subtract).then_inc(S["coef_r"], 1)
            for k in range(2):
                dve.wait_ge(S["coef_m"], k + 1)
                V.tensor_tensor(coef[:, 2, half[k]], coeff[:, half[k]], coef[:, 1, half[k]], ALU.subtract).then_inc(S["coef_r"], 1)
            dve.wait_ge(S["coef_r"], 4)
            V.memset(zone[6], 0.0).then_inc(S["agg_zero"], 1)
            dve.sem_inc(S["acc_done"], BCH)
            rounds = window_rounds(dve, 0)
            io8 = iota[:, 0:WIN].unsqueeze(1).to_broadcast([P, BCH, WIN])

            def columns(table, at, n, top):
                return nc.values_load_multi_w_load_instructions(
                    table[0:1, ds(at, n)], engines=(mybir.EngineType.DVE,), min_val=0, max_val=top,
                    skip_runtime_bounds_check_because="the table is clamped to the accumulators")[1]

            def build_c(b, h, n):
                V.tensor_tensor(oh[:, h], rel[:, ds(b * BCH, BCH)].unsqueeze(2).to_broadcast([P, BCH, WIN]), io8, ALU.is_equal).then_inc(S["oh_done"], 1)
                dve.wait_ge(S["oh_done"], n + 1)
                for s in range(PARTS):
                    ins = V.tensor_tensor(cb[:, h, s], oh[:, h].unsqueeze(2).to_broadcast([P, BCH, NBASE, WIN]),
                                          coef[:, s, ds(b * BCH, BCH), :].unsqueeze(3).to_broadcast([P, BCH, NBASE, WIN]), ALU.mult)
                ins.then_inc(S["c_ready"], 1)

            with dve.Fori(0, rounds) as r:
                V.tensor_tensor(rel[:], dstf[:], basef[:], ALU.subtract).then_inc(S["round_ready"], 1)
                V.tensor_scalar(basei[:].rearrange("o (b j) -> o b j", j=PITCH)[:, :, 0:BCH], basef[0:1, 0:NCH].rearrange("o (b j) -> o b j", j=BCH),
                                float(W - WIN), None, ALU.min).then_inc(S["round_ready"], 1)
                dve.wait_ge(S["round_ready"], r * 3 + 2)
                V.tensor_scalar(basef[:], basef[:], float(WIN), None, ALU.add).then_inc(S["round_ready"], 1)
                dve.wait_ge(S["round_ready"], r * 3 + 3)
                build_c(0, 0, r * (NB + 1))
                dve.wait_ge(S["agg_zero"], 11)
                with dve.Fori(0, NB // 2) as i:
                    for h in range(2):
                        b = i * 2 + h
                        n = r * NB + b
                        build_c(b + 1, 1 - h, n + r + 1)
                        col = columns(basei, b * PITCH, BCH, W - WIN)
                        for j in range(BCH):
                            dve.wait_ge(S["mm_done"], n * BCH + j + 1 + BCH)
                            dve.wait_ge(S["acc_done"], n * BCH + j + BCH)
                            a = aggw[:, :, ds(col[j], WIN)]
                            V.tensor_tensor(a, ps[j][:, 0:256].rearrange("p (fb w) -> p fb w", w=WIN), a, ALU.add).then_inc(S["acc_done"], 1)
            dve.drain().then_inc(S["agg_done"], 1)
            dve.wait_ge(S["hb_in"], 16)
            for t in range(NT):
                r_ = rows(t)
                xt_, xo_ = xt[0:r_, t % 2, :], xo[0:r_, t % 2, :]
                dve.wait_ge(S[f"xt_in{t % 2}"], 16 * (t // 2 + 1))
                link(V.tensor_tensor(xt_, xt_, hb[0:r_, :], ALU.add))
                dve.wait_ge(S["tile_mm"], t + 1)
                if t >= 2:
                    dve.wait_ge(S[f"tile_out{t % 2}"], 32 * (t // 2))
                V.tensor_tensor(xo_, ps[t % 8][0:r_, :], xt_, ALU.add).then_inc(S["xt_used"], 1)
                dve.wait_ge(S["xt_used"], t + 1)
                moments(t, xo_)
                inverse_std(t, t + 1)
                if t >= 2:
                    dve.wait_ge(S["tp"], t - 1)
                normalize(t, xn[0:r_, t % 2, :], xo_).then_inc(S["tile_ready"], 1)
            usrc = ulo[:].bitcast(i32)
            hsrc = uhi[:].bitcast(i32)
            relf = reln[:, 0:NCH].rearrange("p (g c) -> p g c", c=GRP)
            link(V.memset(reln[:, NCH:TCOL], 0.0))
            link(V.tensor_tensor(relf, dstf[:, 0:NCH].rearrange("p (g c) -> p g c", c=GRP), base3[:].unsqueeze(2).to_broadcast([P, NCH // GRP, GRP]), ALU.subtract))
            link(V.tensor_single_scalar(usrc, src_i[:, 0:TCOL], P - 1, ALU.bitwise_and))
            link(V.tensor_single_scalar(hsrc, src_i[:, 0:TCOL], 7, ALU.logical_shift_right))
            link(V.tensor_copy(ulo[:], usrc))
            link(V.tensor_copy(uhi[:], hsrc))

            def G(k):
                return g_[:, k]

            def sm(k):
                return s_[:, k, :]

            def bc(a):
                return a.unsqueeze(2).to_broadcast([P, NT, EX0])

            dve.wait_ge(S["logits"], NT)
            lg = ps[4][:, 0:NT * EX0].rearrange("p (t e) -> p t e", e=EX0)
            link(V.tensor_reduce(sm(0), lg, AX.X, ALU.max))
            V.tensor_tensor(G(1), lg, bc(sm(0)), ALU.subtract).then_inc(S["exp_req"], 1)
            link(V.tensor_scalar(G(3), iota[:, 0:EX0].unsqueeze(1).to_broadcast([P, NT, EX0]), -1.0, float(EX0), ALU.mult, ALU.add))
            link(V.tensor_scalar(sm(15), iota[:, 0:NT], float(P), part[:, 0:1], ALU.mult, ALU.add))
            link(V.tensor_scalar(sm(15), sm(15), float(N), None, ALU.is_lt))
            dve.wait_ge(S["exp_done"], 1)
            link(V.tensor_reduce(sm(1), G(0), AX.X, ALU.add))
            link(V.reciprocal(sm(2), sm(1)))
            link(V.tensor_tensor(G(2), G(0), bc(sm(2)), ALU.mult))

            def first_max(gates, top, best, mask):
                link(V.tensor_reduce(top, gates, AX.X, ALU.max))
                link(V.tensor_tensor(G(5), gates, bc(top), ALU.is_equal))
                link(V.tensor_tensor(G(5), G(5), G(3), ALU.mult))
                link(V.tensor_reduce(best, G(5), AX.X, ALU.max))
                link(V.tensor_tensor(mask, G(3), bc(best), ALU.is_equal))

            def with_places(mask, pos, given):
                V.memset(pref[:, 0, :], 0.0)
                V.tensor_copy(pref[:, 1, :], ps[4][:, 0:EX0])
                link(V.tensor_copy(G(11), ps[4][:, 0:NT * EX0].rearrange("p (t e) -> p t e", e=EX0)))
                for t in range(2, NT):
                    link(V.tensor_tensor(pref[:, t, :], pref[:, t - 1, :], G(11)[:, t - 1, :], ALU.add))
                if given is not None:
                    link(V.tensor_tensor(pref[:], pref[:], given.unsqueeze(1).to_broadcast([P, NT, EX0]), ALU.add))
                link(V.tensor_tensor(pos, ps[3][:, 0:NT * EX0].rearrange("p (t e) -> p t e", e=EX0), pref[:], ALU.add))
                link(V.tensor_tensor(pos, pos, mask, ALU.mult))
                link(V.scalar_tensor_tensor(out=mask, in0=pos, scalar=float(CAP), in1=mask, op0=ALU.is_lt, op1=ALU.mult))

            def to_slots(k, best, pos, kept):
                link(V.tensor_scalar(sm(best), sm(best), -1.0, float(EX0), ALU.mult, ALU.add))
                link(V.scalar_tensor_tensor(out=sm(12), in0=sm(best), scalar=float(CAP), in1=sm(pos), op0=ALU.mult, op1=ALU.add))
                link(V.tensor_tensor(sm(12), sm(12), sm(kept), ALU.mult))
                link(V.tensor_scalar(sm(14), sm(kept), -NOSLOT, NOSLOT, ALU.mult, ALU.add))
                V.tensor_tensor(slot_i[:, k, :], sm(12), sm(14), ALU.add).then_inc(S["slots_ready"], 1)
                link(V.tensor_copy(slot_i[:, 2 + k, :], sm(12)))

            first_max(G(2), sm(3), sm(5), G(4))
            link(V.tensor_tensor(G(10), G(4), bc(sm(15)), ALU.mult))
            V.tensor_copy(mb[:], G(10)).then_inc(S["mask_ready"], 1)
            link(V.tensor_scalar(G(5), G(4), -1.0, 1.0, ALU.mult, ALU.add))
            link(V.tensor_tensor(G(6), G(2), G(5), ALU.mult))
            dve.wait_ge(S["places"], 1)
            with_places(G(10), G(8), None)
            V.tensor_copy(mb[:], G(10)).then_inc(S["mask_ready"], 1)
            link(V.tensor_reduce(sm(8), G(8), AX.X, ALU.add))
            link(V.tensor_reduce(sm(9), G(10), AX.X, ALU.add))
            to_slots(0, 5, 8, 9)
            first_max(G(6), sm(4), sm(6), G(7))
            link(V.tensor_tensor(G(7), G(7), bc(sm(15)), ALU.mult))
            dve.wait_ge(S["places"], 2)
            link(V.tensor_reduce(G(9)[:, 0, :], ps[4][:, 0:NT * EX0].rearrange("p (t e) -> p e t", e=EX0), AX.X, ALU.add))
            V.tensor_copy(mb[:], G(7)).then_inc(S["mask_ready"], 1)
            link(V.tensor_tensor(sm(7), sm(3), sm(4), ALU.add))
            link(V.tensor_scalar(sm(7), sm(7), 1e-9, None, ALU.add))
            link(V.reciprocal(sm(7), sm(7)))
            link(V.tensor_tensor(sm(3), sm(3), sm(7), ALU.mult))
            link(V.tensor_tensor(sm(4), sm(4), sm(7), ALU.mult))
            dve.wait_ge(S["places"], 3)
            with_places(G(7), G(8), G(9)[:, 0, :])
            link(V.tensor_reduce(sm(10), G(8), AX.X, ALU.add))
            link(V.tensor_reduce(sm(11), G(7), AX.X, ALU.add))
            to_slots(1, 6, 10, 11)
            link(V.tensor_tensor(sm(3), sm(3), sm(9), ALU.mult))
            link(V.tensor_tensor(sm(4), sm(4), sm(11), ALU.mult))

            ioP = iota[:].unsqueeze(1).to_broadcast([P, BCH, P])
            ioU = iota[:, 0:UH].unsqueeze(1).to_broadcast([P, BCH, UH])
            ioW = iota[:, 0:WINN].unsqueeze(1).to_broadcast([P, BCH, WINN])

            def build_n(b, h, n):
                at = ds(b * BCH, BCH)
                V.tensor_tensor(ohw[:, h], reln[:, at].unsqueeze(2).to_broadcast([P, BCH, WINN]), ioW, ALU.is_equal)
                V.tensor_tensor(ohu[:, h], uhi[:, at].unsqueeze(2).to_broadcast([P, BCH, UH]), ioU, ALU.is_equal).then_inc(S["n_oh"], 1)
                V.tensor_tensor(rside[:, h], ulo[:, at].unsqueeze(2).to_broadcast([P, BCH, P]), ioP, ALU.is_equal)
                dve.wait_ge(S["n_oh"], n + 1)
                V.tensor_tensor(lside[:, h], ohw[:, h].unsqueeze(2).to_broadcast([P, BCH, UH, WINN]),
                                ohu[:, h].unsqueeze(3).to_broadcast([P, BCH, UH, WINN]), ALU.mult).then_inc(S["n_c"], 1)

            def count_round(r):
                table = base3i.rearrange("o (b j) -> o b j", j=NPITCH)[:, :, 0:NGRP]
                V.tensor_scalar(table, base3[0:1, :].rearrange("o (b j) -> o b j", j=NGRP), float(W - WINN), None, ALU.min).then_inc(S["n_round"], 1)
                dve.wait_ge(S["n_round"], r + 1)
                build_n(0, 0, r * (NB + 1))
                with dve.Fori(0, NB // 2) as i:
                    for h in range(2):
                        b = i * 2 + h
                        n = r * NB + b
                        build_n(b + 1, 1 - h, n + r + 1)
                        col = columns(base3i, b * NPITCH, NGRP, W - WINN)
                        for q in range(NGRP):
                            dve.wait_ge(S["n_mm"], n * NGRP + q + 1)
                            dve.wait_ge(S["n_acc"], n * NGRP + q + NGRP)
                            a = nT[:, :, ds(col[q], WINN)]
                            V.tensor_tensor(a, ps[1 + 3 * q][:, 0:160].rearrange("p (u w) -> p u w", w=WINN), a, ALU.add).then_inc(S["n_acc"], 1)

            dve.sem_inc(S["n_acc"], NGRP)
            dve.wait_ge(S["n_zero"], 1)
            count_round(0)
            rounds = window_rounds(dve, 1)
            S["n_next"] = sem("count_distances_ready")
            with dve.If(rounds > 1):
                with dve.Fori(1, rounds) as r:
                    V.tensor_scalar(reln[:], reln[:], -float(WINN), None, ALU.add).then_inc(S["n_next"], 1)
                    V.tensor_scalar(base3[:], base3[:], float(WINN), None, ALU.add).then_inc(S["n_next"], 1)
                    dve.wait_ge(S["n_next"], r * 2)
                    count_round(r)
            dve.end_ifs()
            dve.drain().then_inc(S["n_ready"], 1)
            link(V.tensor_reduce(cnt[:], nT[:, :, 0:N], AX.X, ALU.add))
            link(V.reciprocal(rcnt[:], cnt[:]))

            def adjacency(n):
                t, q = n // 3, n % 3
                w_ = min(4 * P, NP - 4 * P * q)
                dve.wait_ge(S["tr"], n + 1)
                V.tensor_copy(adj[0:cols(t), t, 4 * P * q:4 * P * q + w_], ps[TBANK[n % 3]][0:cols(t), 0:w_]).then_inc(S["tr_outv"], 1)

            def combine(t):
                r_ = rows(t)
                for k in range(2):
                    n = 2 * t + k
                    dve.wait_ge(gy[n % 6], 16 * (n // 6 + 1))
                    V.scalar_tensor_tensor(out=x1[0:r_, t, :], in0=y2[0:r_, n % 6, :], scalar=s_[0:r_, 3 + k, t:t + 1], in1=x1[0:r_, t, :],
                                           op0=ALU.mult, op1=ALU.add).then_inc(S["y2_used"], 1)
                    dve.wait_ge(S["y2_used"], n + 1)
                moments(t, x1[0:r_, t, :])
                V.engine_nop().then_inc(S["std_req"], 1)

            def norm3(t):
                roots[0] += 1
                dve.wait_ge(S["std_done"], roots[0])
                link(V.reciprocal(rstd[:, t:t + 1], std[:, t:t + 1]))
                normalize(t, xh3[0:rows(t), t, :], x1[0:rows(t), t, :]).then_inc(S["xh3_ready"], 1)

            def add_alpha(t):
                dve.wait_ge(S["alpha"], t + 1)
                V.tensor_tensor(x1[0:rows(t), t, :], ps[6 + t % 2][0:rows(t), :], x1[0:rows(t), t, :], ALU.add).then_inc(S["alpha_out"], 1)

            for n in range(0, 3 * NT, 2):
                adjacency(n)
            dve.wait_ge(S["x1_in"], 32)
            for t in range(NT):
                combine(t)
                if t:
                    norm3(t - 1)
                if t >= 3:
                    add_alpha(t - 3)
            norm3(NT - 1)
            for t in range(NT - 3, NT):
                add_alpha(t)
            for k in range(NF):
                for q in range(3):
                    n = 3 * k + q
                    w_ = min(512, NP - 512 * q)
                    dve.wait_ge(S["sums"], n + 1)
                    V.tensor_copy(sT[:, k, 512 * q:512 * q + w_], ps[2 + n % 3][:, 0:w_]).then_inc(S["sums_out"], 1)

            def low(dst, src, high, done):
                V.tensor_tensor(dst, src, high.bitcast(f32), ALU.subtract).then_inc(done, 1)

            def weights_low(e, k):
                dve.wait_ge(S[f"w_high{k}"], e + 1)
                low(w4p[:, e % 2, 1, k], (w1s, w2s)[k][e % 2], w4p[:, e % 2, 0, k], S[f"w_low{k}"])

            for e, k in ((0, 0), (1, 0), (0, 1)):
                weights_low(e, k)

            def graph_out(t):
                r_ = rows(t)
                x_t = x1[0:r_, t, :]
                dve.wait_ge(S["gm"], t + 1)
                V.scalar_tensor_tensor(out=x_t, in0=ps[t % 6][0:r_, :], scalar=rcnt[0:r_, t:t + 1], in1=x_t, op0=ALU.mult, op1=ALU.add).then_inc(S["g_out"], 1)
                dve.wait_ge(S["g_out"], t + 1)

            for t in range(TT1):
                graph_out(t)
                moments(t, x1[:, t, :])
            inverse_std(0, TT1)
            for t in range(TT1):
                ins = normalize(t, xh4[:, t, :], x1[:, t, :])
            ins.then_inc(S["x4_ready"], 1)
            for t in range(TT1):
                dve.wait_ge(S["tp4_high"], t + 1)
                cols_t = slice(t * P, (t + 1) * P)
                low(x4p[:, 1, :, cols_t], ps[6 + t % 2][:].rearrange("p (k n) -> p k n", k=NF), x4p[:, 0, :, cols_t], S["tp4_out"])
            for t in range(TT1, NT):
                graph_out(t)
            dve.wait_ge(S["moe_in"], 32)
            link(V.tensor_copy(ef[:], ei[:]))
            for t in range(TT1):
                for k in range(TOPK):
                    link(V.tensor_scalar(combt[:, t, k, :], iota[:, 0:EX1], ef[:, t, k:k + 1], ew[:, t, k:k + 1], ALU.is_equal, ALU.mult))
            link(V.tensor_tensor(comb[:], combt[:, :, 0, :], combt[:, :, 1, :], ALU.add))
            for e in range(EX1 + 1):
                if e < EX1:
                    dve.wait_ge(S["h_high"], e + 1)
                    low(h4p[:, e % 2, 1], hT1[:, e % 2], h4p[:, e % 2, 0], S["h_low"])
                for t in range(TT1):
                    if e:
                        n = TT1 * (e - 1) + t
                        dve.wait_ge(S["down1"], n + 1)
                        if e > 1:
                            dve.wait_ge(S["y1_used"], n - TT1 + 1)
                        V.scalar_tensor_tensor(out=x1[:, t, :], in0=ps[4 + t][:], scalar=comb[:, t, e - 1:e], in1=x1[:, t, :],
                                               op0=ALU.mult, op1=ALU.add).then_inc(S["y1_used"], 1)
                if e + 2 < EX1:
                    weights_low(e + 2, 0)
                if e + 1 < EX1:
                    weights_low(e + 1, 1)


def kernel(**inputs):
    import numpy as np
    import concourse.bacc as bacc
    from concourse.bass_utils import run_bass_kernel_spmd as run

    def padded(a, n, fill):
        flat = np.full(n * P, fill, a.dtype)
        flat[:E] = a.reshape(-1)
        return flat.reshape(n, P)

    a = {k: np.asarray(v) for k, v in inputs.items()}
    arrays = {
        "x": a["x"],
        "src_cols": np.ascontiguousarray(padded(a["src"], TCOL, 0).T),
        "dst_cols": np.ascontiguousarray(padded(a["dst"], TCOL, N).T),
        "wgt_cols": np.ascontiguousarray(padded(a["edge_weight1"], TCOL, 0).T),
        "etype": padded(a["edge_type_32"], NCH, 0).reshape(4, QCH * P),
        "dst_rows": padded(a["dst"], NCH, N),
        "bases": a["L0_gnn_bases"], "w_comp": a["L0_gnn_w_comp"], "h_bias": a["L0_gnn_h_bias"].reshape(1, F),
        "w_gating": a["L0_ffn_w_gating"], "f0_w1": a["L0_ffn_w1"], "f0_w2": a["L0_ffn_w2"],
        "wc": a["L1_gnn_wc"], "wn": a["L1_gnn_wn"], "g1_bias": a["L1_gnn_bias"].reshape(1, F),
        "x_weights": a["L1_ffn_expert_weights"], "x_indices": a["L1_ffn_expert_indices"],
        "f1_w1": a["L1_ffn_w1"], "f1_w2": a["L1_ffn_w2"],
    }
    arrays = {k: np.ascontiguousarray(v) for k, v in arrays.items()}
    nc = bacc.Bacc("TRN2", target_bir_lowering=False, num_devices=1)
    t = {k: nc.dram_tensor("in_" + k, v.shape, mybir.dt.from_np(v.dtype), kind="ExternalInput").ap() for k, v in arrays.items()}
    out = nc.dram_tensor("out", (N, F), f32, kind="ExternalOutput").ap()
    build(nc, out=out, **t)
    r = run(nc, [{"in_" + k: v for k, v in arrays.items()}], core_ids=[0])
    return r.results[0]["out"]
```
